# Optimizing a Trainium2 kernel written in Bass

```python
import numpy as np
import jax
import jax.numpy as jnp

def _softmax(x, axis=-1):
    return jax.nn.softmax(x, axis=axis)

def _gelu(x):
    return jax.nn.gelu(x, approximate=True)

def _silu(x):
    return jax.nn.silu(x)

def _sigmoid(x):
    return jax.nn.sigmoid(x)

def _layernorm(x, axis=-1, eps=1e-05):
    m = jnp.mean(x, axis=axis, keepdims=True)
    v = jnp.var(x, axis=axis, keepdims=True)
    return (x - m) / jnp.sqrt(v + eps)

def _scatter_add(tgt, idx, src, axis=0):
    return tgt.at[idx].add(src)

def _segment_sum(src, seg, n):
    return jax.ops.segment_sum(src, seg, n)
kernel_name = 'mk_lm_tower_d2_tok_ids768_r4_03e024'

def setup_inputs(seed: int=0):
    np.random.seed(seed)
    _w = jnp.asarray

    def _rec_inputs():
        import jax
        import jax.numpy as jnp
        _rk = jax.random.key(seed)
        x = jax.random.randint(jax.random.fold_in(_rk, 1), (64, 128), 0, 30521, jnp.int32)
        itok_BS_2_399970 = jax.random.randint(jax.random.fold_in(_rk, 21), (64, 128), 2, 399971, jnp.int32)
        return (x, itok_BS_2_399970)
    x, itok_BS_2_399970 = _rec_inputs()

    def _L0_tok_setup():
        import jax, jax.numpy as jnp
        import numpy as np
        LN_EPS = 1e-12
        key = jax.random.key(seed)
        ks = jax.random.split(key, 8)
        B, S, H, D = (32, 128, 192, 75)
        V_BERT, V_W, P = (30522, 400001, 128)
        inp = {'sents': jax.random.randint(ks[0], (B, S), 0, V_BERT), 'wids': jax.random.randint(ks[1], (B, S), 0, V_W), 'word_emb': jax.random.normal(ks[2], (V_BERT, H), jnp.float32) * 0.02, 'pos_emb': jax.random.normal(ks[3], (P, H), jnp.float32) * 0.02, 'type_emb': jax.random.normal(ks[4], (2, H), jnp.float32) * 0.02, 'ln_gamma': jnp.ones((H,), jnp.float32), 'ln_beta': jnp.zeros((H,), jnp.float32), 'wvec': jax.random.normal(ks[5], (V_W, D), jnp.float32) * 0.1, 'g2b_w': jax.random.normal(ks[6], (H, D), jnp.float32) * 0.02, 'g2b_b': jnp.zeros((H,), jnp.float32), 'gate_w': jax.random.normal(ks[7], (1, H), jnp.float32) * 0.02, 'gate_b': jnp.zeros((1,), jnp.float32)}
        return inp
    _L0_tok_all = _L0_tok_setup()
    _L0_tok_in = {k: v for k, v in _L0_tok_all.items() if k in ('word_emb', 'pos_emb', 'type_emb', 'ln_gamma', 'ln_beta', 'wvec', 'g2b_w', 'g2b_b', 'gate_w', 'gate_b')}
    del _L0_tok_all

    def _L0_attn_setup():
        import jax, jax.numpy as jnp
        import numpy as np
        L = 14
        H = 12
        HD = 64

        def rel_pos_embed(N, table_v, table_h):
            n = N - 1
            s = int(n ** 0.5)
            r = jnp.arange(n)
            dv = r[None, :] // s - r[:, None] // s
            dh = r[None, :] % s - r[:, None] % s
            iv = jnp.clip(dv, -L, L) + L + 1
            ih = jnp.clip(dh, -L, L) + L + 1
            iv = jnp.pad(iv, ((1, 0), (1, 0)))
            ih = jnp.pad(ih, ((1, 0), (1, 0)))
            return table_v[iv] + table_h[ih]
        key = jax.random.key(seed)
        ks = jax.random.split(key, 11)
        B, N, E = (64, 197, 192)
        T = 2 * L + 2
        std = 0.02
        return {'x': jax.random.normal(ks[0], (B, N, E), jnp.float32), 'wq': jax.random.normal(ks[1], (E, H * HD), jnp.float32) * std, 'wk': jax.random.normal(ks[2], (E, H * HD), jnp.float32) * std, 'wv': jax.random.normal(ks[3], (E, H * HD), jnp.float32) * std, 'wproj': jax.random.normal(ks[4], (H * HD, E), jnp.float32) * std, 'bproj': jnp.zeros((E,), jnp.float32), 'rk_v': jax.random.normal(ks[5], (T, HD), jnp.float32) * std, 'rk_h': jax.random.normal(ks[6], (T, HD), jnp.float32) * std, 'rv_v': jax.random.normal(ks[7], (T, HD), jnp.float32) * std, 'rv_h': jax.random.normal(ks[8], (T, HD), jnp.float32) * std}
    _L0_attn_all = _L0_attn_setup()
    _L0_attn_in = {k: v for k, v in _L0_attn_all.items() if k in ('wq', 'wk', 'wv', 'wproj', 'bproj', 'rk_v', 'rk_h', 'rv_v', 'rv_h')}
    del _L0_attn_all

    def _L0_ffn_setup():
        import jax, jax.numpy as jnp
        import numpy as np
        B, N, D, E, F, K = (2, 512, 192, 8, 768, 2)
        V_MAX = 3.0
        FEAT_CLAMP = 10.0

        def bk_green_diag(a):
            aT = jnp.swapaxes(a, 0, 1)

            def step(c, ai):
                d = ai - 1.0 / c
                return (d, d)
            d0 = aT[0]
            _, d_rest = jax.lax.scan(step, d0, aT[1:])
            d = jnp.concatenate([d0[None], d_rest], axis=0)
            eN = aT[-1]
            _, e_rest = jax.lax.scan(step, eN, aT[:-1], reverse=True)
            e = jnp.concatenate([e_rest, eN[None]], axis=0)
            G = 1.0 / (d + e - aT)
            return jnp.swapaxes(G, 0, 1)
        key = jax.random.key(seed)
        ks = jax.random.split(key, 8)
        s = lambda k, shape, sc: jax.random.normal(k, shape, jnp.float32) * sc
        return {'x': s(ks[0], (B, N, D), 1.0), 'v_w': s(ks[1], (D,), 0.02), 'v_b': jnp.zeros((), jnp.float32), 'gate_w': s(ks[2], (D, E), 0.02), 'gate_b': jnp.zeros((E,), jnp.float32), 'w1': s(ks[3], (E, D, F), 0.02), 'b1': jnp.zeros((E, F), jnp.float32), 'w2': s(ks[4], (E, F, D), 0.02), 'b2': jnp.zeros((E, D), jnp.float32), 'out_w': s(ks[5], (2, D), 0.02), 'out_b': jnp.zeros((D,), jnp.float32), 'bk_scale': jnp.ones((D,), jnp.float32)}
    _L0_ffn_all = _L0_ffn_setup()
    _L0_ffn_in = {k: v for k, v in _L0_ffn_all.items() if k in ('v_w', 'v_b', 'gate_w', 'gate_b', 'w1', 'b1', 'w2', 'b2', 'out_w', 'out_b', 'bk_scale')}
    del _L0_ffn_all

    def _L1_attn_setup():
        import jax, jax.numpy as jnp
        import numpy as np
        import math
        B, S, H = (2, 512, 192)
        NH = 12
        HD = H // NH // 2
        LAMBDA_INIT = 0.8 - 0.6 * math.exp(-0.3 * 0)
        EPS = 1e-05
        key = jax.random.key(seed)
        ks = jax.random.split(key, 16)
        std = 0.02
        return {'hidden_states': jax.random.normal(ks[0], (B, S, H), dtype=jnp.float32), 'Wq': jax.random.normal(ks[1], (H, H), dtype=jnp.float32) * std, 'bq': jnp.zeros((H,), dtype=jnp.float32), 'Wk': jax.random.normal(ks[2], (H, H), dtype=jnp.float32) * std, 'bk': jnp.zeros((H,), dtype=jnp.float32), 'Wv': jax.random.normal(ks[3], (H, H), dtype=jnp.float32) * std, 'bv': jnp.zeros((H,), dtype=jnp.float32), 'Wo': jax.random.normal(ks[4], (H, H), dtype=jnp.float32) * std, 'bo': jnp.zeros((H,), dtype=jnp.float32), 'lambda_q1': jax.random.normal(ks[5], (HD,), dtype=jnp.float32) * 0.1, 'lambda_k1': jax.random.normal(ks[6], (HD,), dtype=jnp.float32) * 0.1, 'lambda_q2': jax.random.normal(ks[7], (HD,), dtype=jnp.float32) * 0.1, 'lambda_k2': jax.random.normal(ks[8], (HD,), dtype=jnp.float32) * 0.1, 'subln_w': jnp.ones((2 * HD,), dtype=jnp.float32)}
    _L1_attn_all = _L1_attn_setup()
    _L1_attn_in = {k: v for k, v in _L1_attn_all.items() if k in ('Wq', 'bq', 'Wk', 'bk', 'Wv', 'bv', 'Wo', 'bo', 'lambda_q1', 'lambda_k1', 'lambda_q2', 'lambda_k2', 'subln_w')}
    del _L1_attn_all

    def _L1_ffn_setup():
        import jax, jax.numpy as jnp
        import numpy as np
        GT0 = [[0, 1, 0, 0, 1, 0], [0, 1, 0, 0, 0, 1], [0, 0, 1, 0, 1, 0], [0, 0, 1, 0, 0, 1], [0, 0, 0, 1, 1, 0], [0, 0, 0, 1, 0, 1]]
        NCLS = 6
        K = 1

        def _expert_pairs():
            pairs = []
            for i in range(NCLS):
                p = [(j - 1, k - 1) for j in range(1, 6) for k in range(1, 6) if j != k and GT0[i][j] == 1 and (GT0[i][k] == 1)]
                pairs.append(p)
            return pairs
        PAIRS = _expert_pairs()
        B, P, D, H = (64, 64, 192, 768)

        def _gelu(t):
            return jax.nn.gelu(t, approximate=False)
        key = jax.random.key(seed)
        ks = jax.random.split(key, 8)
        s = 0.02
        x = jax.random.normal(ks[0], (B, NCLS + P, D), dtype=jnp.float32)
        mids = jax.random.randint(ks[1], (B,), 0, 6)
        moe0_W1 = jax.random.normal(ks[2], (D, H), dtype=jnp.float32) * s
        moe0_b1 = jnp.zeros((H,), jnp.float32)
        moe0_W2 = jax.random.normal(ks[3], (H, D), dtype=jnp.float32) * s
        moe0_b2 = jnp.zeros((D,), jnp.float32)
        A1_W = jax.random.normal(ks[4], (5, D, H), dtype=jnp.float32) * s
        A1_b = jnp.zeros((5, H), jnp.float32)
        A2_W = jax.random.normal(ks[5], (5, H, D), dtype=jnp.float32) * s
        A2_b = jnp.zeros((5, D), jnp.float32)
        G_W = jax.random.normal(ks[6], (NCLS, D, 2), dtype=jnp.float32) * s
        return {'x': x, 'moe0_W1': moe0_W1, 'moe0_b1': moe0_b1, 'moe0_W2': moe0_W2, 'moe0_b2': moe0_b2, 'A1_W': A1_W, 'A1_b': A1_b, 'A2_W': A2_W, 'A2_b': A2_b, 'G_W': G_W, 'mids': mids}
    _L1_ffn_all = _L1_ffn_setup()
    _L1_ffn_in = {k: v for k, v in _L1_ffn_all.items() if k in ('moe0_W1', 'moe0_b1', 'moe0_W2', 'moe0_b2', 'A1_W', 'A1_b', 'A2_W', 'A2_b', 'G_W', 'mids')}
    del _L1_ffn_all
    return {'x': x, 'itok_BS_2_399970': itok_BS_2_399970, 'L0_tok_word_emb': _L0_tok_in['word_emb'], 'L0_tok_pos_emb': _L0_tok_in['pos_emb'], 'L0_tok_type_emb': _L0_tok_in['type_emb'], 'L0_tok_ln_gamma': _L0_tok_in['ln_gamma'], 'L0_tok_ln_beta': _L0_tok_in['ln_beta'], 'L0_tok_wvec': _L0_tok_in['wvec'], 'L0_tok_g2b_w': _L0_tok_in['g2b_w'], 'L0_tok_g2b_b': _L0_tok_in['g2b_b'], 'L0_tok_gate_w': _L0_tok_in['gate_w'], 'L0_tok_gate_b': _L0_tok_in['gate_b'], 'L0_attn_wq': _L0_attn_in['wq'], 'L0_attn_wk': _L0_attn_in['wk'], 'L0_attn_wv': _L0_attn_in['wv'], 'L0_attn_wproj': _L0_attn_in['wproj'], 'L0_attn_bproj': _L0_attn_in['bproj'], 'L0_attn_rk_v': _L0_attn_in['rk_v'], 'L0_attn_rk_h': _L0_attn_in['rk_h'], 'L0_attn_rv_v': _L0_attn_in['rv_v'], 'L0_attn_rv_h': _L0_attn_in['rv_h'], 'L0_ffn_v_w': _L0_ffn_in['v_w'], 'L0_ffn_v_b': _L0_ffn_in['v_b'], 'L0_ffn_gate_w': _L0_ffn_in['gate_w'], 'L0_ffn_gate_b': _L0_ffn_in['gate_b'], 'L0_ffn_w1': _L0_ffn_in['w1'], 'L0_ffn_b1': _L0_ffn_in['b1'], 'L0_ffn_w2': _L0_ffn_in['w2'], 'L0_ffn_b2': _L0_ffn_in['b2'], 'L0_ffn_out_w': _L0_ffn_in['out_w'], 'L0_ffn_out_b': _L0_ffn_in['out_b'], 'L0_ffn_bk_scale': _L0_ffn_in['bk_scale'], 'L1_attn_Wq': _L1_attn_in['Wq'], 'L1_attn_bq': _L1_attn_in['bq'], 'L1_attn_Wk': _L1_attn_in['Wk'], 'L1_attn_bk': _L1_attn_in['bk'], 'L1_attn_Wv': _L1_attn_in['Wv'], 'L1_attn_bv': _L1_attn_in['bv'], 'L1_attn_Wo': _L1_attn_in['Wo'], 'L1_attn_bo': _L1_attn_in['bo'], 'L1_attn_lambda_q1': _L1_attn_in['lambda_q1'], 'L1_attn_lambda_k1': _L1_attn_in['lambda_k1'], 'L1_attn_lambda_q2': _L1_attn_in['lambda_q2'], 'L1_attn_lambda_k2': _L1_attn_in['lambda_k2'], 'L1_attn_subln_w': _L1_attn_in['subln_w'], 'L1_ffn_moe0_W1': _L1_ffn_in['moe0_W1'], 'L1_ffn_moe0_b1': _L1_ffn_in['moe0_b1'], 'L1_ffn_moe0_W2': _L1_ffn_in['moe0_W2'], 'L1_ffn_moe0_b2': _L1_ffn_in['moe0_b2'], 'L1_ffn_A1_W': _L1_ffn_in['A1_W'], 'L1_ffn_A1_b': _L1_ffn_in['A1_b'], 'L1_ffn_A2_W': _L1_ffn_in['A2_W'], 'L1_ffn_A2_b': _L1_ffn_in['A2_b'], 'L1_ffn_G_W': _L1_ffn_in['G_W'], 'L1_ffn_mids': _L1_ffn_in['mids']}

def reference(x, itok_BS_2_399970, L0_tok_word_emb, L0_tok_pos_emb, L0_tok_type_emb, L0_tok_ln_gamma, L0_tok_ln_beta, L0_tok_wvec, L0_tok_g2b_w, L0_tok_g2b_b, L0_tok_gate_w, L0_tok_gate_b, L0_attn_wq, L0_attn_wk, L0_attn_wv, L0_attn_wproj, L0_attn_bproj, L0_attn_rk_v, L0_attn_rk_h, L0_attn_rv_v, L0_attn_rv_h, L0_ffn_v_w, L0_ffn_v_b, L0_ffn_gate_w, L0_ffn_gate_b, L0_ffn_w1, L0_ffn_b1, L0_ffn_w2, L0_ffn_b2, L0_ffn_out_w, L0_ffn_out_b, L0_ffn_bk_scale, L1_attn_Wq, L1_attn_bq, L1_attn_Wk, L1_attn_bk, L1_attn_Wv, L1_attn_bv, L1_attn_Wo, L1_attn_bo, L1_attn_lambda_q1, L1_attn_lambda_k1, L1_attn_lambda_q2, L1_attn_lambda_k2, L1_attn_subln_w, L1_ffn_moe0_W1, L1_ffn_moe0_b1, L1_ffn_moe0_W2, L1_ffn_moe0_b2, L1_ffn_A1_W, L1_ffn_A1_b, L1_ffn_A2_W, L1_ffn_A2_b, L1_ffn_G_W, L1_ffn_mids):
    import jax
    import jax.numpy as jnp

    def _L0_tok_ref(sents, wids, word_emb, pos_emb, type_emb, ln_gamma, ln_beta, wvec, g2b_w, g2b_b, gate_w, gate_b):
        import jax, jax.numpy as jnp
        import numpy as np
        LN_EPS = 1e-12
        S = sents.shape[1]
        e = word_emb[sents] + pos_emb[:S][None, :, :] + type_emb[0][None, None, :]
        mu = jnp.mean(e, axis=-1, keepdims=True)
        var = jnp.mean(jnp.square(e - mu), axis=-1, keepdims=True)
        b = (e - mu) * jax.lax.rsqrt(var + LN_EPS) * ln_gamma + ln_beta
        a = jax.nn.sigmoid(jnp.einsum('bsh,oh->bso', b, gate_w) + gate_b)
        g = jnp.einsum('bsd,hd->bsh', wvec[wids], g2b_w) + g2b_b
        return (1.0 - a) * b + a * g

    def _L0_attn_ref(x, wq, wk, wv, wproj, bproj, rk_v, rk_h, rv_v, rv_h):
        import jax, jax.numpy as jnp
        import numpy as np
        L = 14
        H = 12
        HD = 64

        def rel_pos_embed(N, table_v, table_h):
            n = N - 1
            s = int(n ** 0.5)
            r = jnp.arange(n)
            dv = r[None, :] // s - r[:, None] // s
            dh = r[None, :] % s - r[:, None] % s
            iv = jnp.clip(dv, -L, L) + L + 1
            ih = jnp.clip(dh, -L, L) + L + 1
            iv = jnp.pad(iv, ((1, 0), (1, 0)))
            ih = jnp.pad(ih, ((1, 0), (1, 0)))
            return table_v[iv] + table_h[ih]
        B, N, E = x.shape
        scale = HD ** (-0.5)
        q = (x @ wq).reshape(B, N, H, HD).transpose(0, 2, 1, 3)
        k = (x @ wk).reshape(B, N, H, HD).transpose(0, 2, 1, 3)
        v = (x @ wv).reshape(B, N, H, HD).transpose(0, 2, 1, 3)
        attn = jnp.einsum('bhid,bhjd->bhij', q, k) * scale
        rpk = rel_pos_embed(N, rk_v, rk_h)
        attn = attn + jnp.einsum('bhid,ijd->bhij', q, rpk) * scale
        attn = jax.nn.softmax(attn, axis=-1)
        out = jnp.einsum('bhij,bhjd->bhid', attn, v)
        rpv = rel_pos_embed(N, rv_v, rv_h)
        out = out + jnp.einsum('bhij,ijd->bhid', attn, rpv)
        out = out.transpose(0, 2, 1, 3).reshape(B, N, H * HD)
        return out @ wproj + bproj

    def _L0_ffn_ref(x, v_w, v_b, gate_w, gate_b, w1, b1, w2, b2, out_w, out_b, bk_scale):
        import jax, jax.numpy as jnp
        import numpy as np
        B, N, D, E, F, K = (2, 512, 192, 8, 768, 2)
        V_MAX = 3.0
        FEAT_CLAMP = 10.0

        def bk_green_diag(a):
            aT = jnp.swapaxes(a, 0, 1)

            def step(c, ai):
                d = ai - 1.0 / c
                return (d, d)
            d0 = aT[0]
            _, d_rest = jax.lax.scan(step, d0, aT[1:])
            d = jnp.concatenate([d0[None], d_rest], axis=0)
            eN = aT[-1]
            _, e_rest = jax.lax.scan(step, eN, aT[:-1], reverse=True)
            e = jnp.concatenate([e_rest, eN[None]], axis=0)
            G = 1.0 / (d + e - aT)
            return jnp.swapaxes(G, 0, 1)
        v = jnp.clip(x @ v_w + v_b, -V_MAX, V_MAX)
        a = (-2.0 + v).astype(jnp.complex64) - 1j
        G = bk_green_diag(a)
        feats = jnp.stack([G.real, G.imag], axis=-1)
        logits = x @ gate_w + gate_b
        probs = jax.nn.softmax(logits, axis=-1)
        topv, topi = jax.lax.top_k(probs, K)
        topv = topv / jnp.sum(topv, axis=-1, keepdims=True)
        comb = jnp.sum(topv[..., None] * jax.nn.one_hot(topi, E, dtype=x.dtype), axis=2)
        h = jax.nn.gelu(jnp.einsum('bnd,edf->bnef', x, w1) + b1)
        y = jnp.einsum('bnef,efd->bned', h, w2) + b2
        ffn_out = jnp.einsum('bne,bned->bnd', comb, y)
        feats_c = jnp.clip(feats, -FEAT_CLAMP, FEAT_CLAMP)
        spec_out = feats_c @ out_w + out_b
        return ffn_out + bk_scale * spec_out

    def _L1_attn_ref(hidden_states, Wq, bq, Wk, bk, Wv, bv, Wo, bo, lambda_q1, lambda_k1, lambda_q2, lambda_k2, subln_w):
        import jax, jax.numpy as jnp
        import numpy as np
        import math
        B, S, H = (2, 512, 192)
        NH = 12
        HD = H // NH // 2
        LAMBDA_INIT = 0.8 - 0.6 * math.exp(-0.3 * 0)
        EPS = 1e-05
        bsz, seq_len, _ = hidden_states.shape
        scaling = HD ** (-0.5)
        q = hidden_states @ Wq + bq
        k = hidden_states @ Wk + bk
        v = hidden_states @ Wv + bv
        q = q.reshape(bsz, seq_len, 2 * NH, HD).transpose(0, 2, 1, 3) * scaling
        k = k.reshape(bsz, seq_len, 2 * NH, HD).transpose(0, 2, 1, 3)
        v = v.reshape(bsz, seq_len, NH, 2 * HD).transpose(0, 2, 1, 3)
        attn = jnp.einsum('bhqd,bhkd->bhqk', q, k)
        attn = jnp.nan_to_num(attn)
        attn = jax.nn.softmax(attn, axis=-1)
        lambda_1 = jnp.exp(jnp.sum(lambda_q1 * lambda_k1))
        lambda_2 = jnp.exp(jnp.sum(lambda_q2 * lambda_k2))
        lambda_full = lambda_1 - lambda_2 + LAMBDA_INIT
        attn = attn.reshape(bsz, NH, 2, seq_len, seq_len)
        attn = attn[:, :, 0] - lambda_full * attn[:, :, 1]
        ctx = jnp.einsum('bhqk,bhkd->bhqd', attn, v)
        rms = jax.lax.rsqrt(jnp.mean(ctx * ctx, axis=-1, keepdims=True) + EPS)
        ctx = ctx * rms * subln_w
        ctx = ctx * (1.0 - LAMBDA_INIT)
        ctx = ctx.transpose(0, 2, 1, 3).reshape(bsz, seq_len, NH * 2 * HD)
        out = ctx @ Wo + bo
        return out

    def _L1_ffn_ref(x, moe0_W1, moe0_b1, moe0_W2, moe0_b2, A1_W, A1_b, A2_W, A2_b, G_W, mids):
        import jax, jax.numpy as jnp
        import numpy as np
        GT0 = [[0, 1, 0, 0, 1, 0], [0, 1, 0, 0, 0, 1], [0, 0, 1, 0, 1, 0], [0, 0, 1, 0, 0, 1], [0, 0, 0, 1, 1, 0], [0, 0, 0, 1, 0, 1]]
        NCLS = 6
        K = 1

        def _expert_pairs():
            pairs = []
            for i in range(NCLS):
                p = [(j - 1, k - 1) for j in range(1, 6) for k in range(1, 6) if j != k and GT0[i][j] == 1 and (GT0[i][k] == 1)]
                pairs.append(p)
            return pairs
        PAIRS = _expert_pairs()
        B, P, D, H = (64, 64, 192, 768)

        def _gelu(t):
            return jax.nn.gelu(t, approximate=False)
        cls_tokens = x[:, :NCLS]
        patch_tokens = x[:, NCLS:]
        patch_out = _gelu(patch_tokens @ moe0_W1 + moe0_b1) @ moe0_W2 + moe0_b2
        cls_outs = []
        for i in range(NCLS):
            tok = cls_tokens[:, i]
            eouts = [_gelu(tok @ A1_W[a] + A1_b[a]) @ A2_W[c] + A2_b[c] for a, c in PAIRS[i]]
            out = jnp.stack(eouts, axis=-1)
            gate = jax.nn.softmax(tok @ G_W[i], axis=-1)
            thr = jnp.sort(gate, axis=-1)[..., -(K + 1)]
            mask = (gate > thr[..., None]).astype(gate.dtype)
            g = gate * mask
            g = g / jnp.clip(jnp.sum(g, axis=-1, keepdims=True), 1e-06)
            cls_outs.append(jnp.sum(out * g[:, None, :], axis=-1))
        cls_out = jnp.stack(cls_outs, axis=1)
        return jnp.concatenate([cls_out, patch_out], axis=1)
    h = _L0_tok_ref(x, itok_BS_2_399970, L0_tok_word_emb, L0_tok_pos_emb, L0_tok_type_emb, L0_tok_ln_gamma, L0_tok_ln_beta, L0_tok_wvec, L0_tok_g2b_w, L0_tok_g2b_b, L0_tok_gate_w, L0_tok_gate_b)
    h = h + _L0_attn_ref(_layernorm(h, axis=-1), L0_attn_wq, L0_attn_wk, L0_attn_wv, L0_attn_wproj, L0_attn_bproj, L0_attn_rk_v, L0_attn_rk_h, L0_attn_rv_v, L0_attn_rv_h)
    h = h + _L0_ffn_ref(_layernorm(h, axis=-1), L0_ffn_v_w, L0_ffn_v_b, L0_ffn_gate_w, L0_ffn_gate_b, L0_ffn_w1, L0_ffn_b1, L0_ffn_w2, L0_ffn_b2, L0_ffn_out_w, L0_ffn_out_b, L0_ffn_bk_scale)
    h = h + _L1_attn_ref(_layernorm(h, axis=-1), L1_attn_Wq, L1_attn_bq, L1_attn_Wk, L1_attn_bk, L1_attn_Wv, L1_attn_bv, L1_attn_Wo, L1_attn_bo, L1_attn_lambda_q1, L1_attn_lambda_k1, L1_attn_lambda_q2, L1_attn_lambda_k2, L1_attn_subln_w)
    h = h + _L1_ffn_ref(_layernorm(h, axis=-1), L1_ffn_moe0_W1, L1_ffn_moe0_b1, L1_ffn_moe0_W2, L1_ffn_moe0_b2, L1_ffn_A1_W, L1_ffn_A1_b, L1_ffn_A2_W, L1_ffn_A2_b, L1_ffn_G_W, L1_ffn_mids)
    return h

_drawn_inputs = setup_inputs


def setup_inputs(seed=0):
    import zlib

    import numpy as np

    out = dict(_drawn_inputs(seed))
    spreads = {'L0_tok_ln_gamma': (1.0, 0.2),
     'L0_tok_ln_beta': (0.0, 0.1),
     'L0_tok_g2b_b': (0.0, 0.1),
     'L0_attn_bproj': (0.0, 0.1),
     'L0_ffn_gate_b': (0.0, 0.1),
     'L0_ffn_b1': (0.0, 0.1),
     'L0_ffn_b2': (0.0, 0.1),
     'L0_ffn_out_b': (0.0, 0.1),
     'L0_ffn_bk_scale': (1.0, 0.2),
     'L1_attn_bq': (0.0, 0.8),
     'L1_attn_bk': (0.0, 0.8),
     'L1_attn_bv': (0.0, 0.1),
     'L1_attn_bo': (0.0, 0.1),
     'L1_attn_subln_w': (1.0, 0.2),
     'L1_ffn_moe0_b1': (0.0, 0.1),
     'L1_ffn_moe0_b2': (0.0, 0.1),
     'L1_ffn_A1_b': (0.0, 0.8),
     'L1_ffn_A2_b': (0.0, 0.1)}
    factors = {'L0_tok_wvec': 2.994,
     'L0_tok_g2b_w': 3.107,
     'L0_attn_wq': 8.0,
     'L0_attn_wk': 8.0,
     'L0_attn_rk_v': 8.0,
     'L0_attn_rk_h': 8.0,
     'L0_attn_rv_v': 7.244,
     'L0_attn_rv_h': 5.297,
     'L0_ffn_v_w': 8.0,
     'L0_ffn_out_w': 2.678,
     'L1_attn_Wq': 8.0,
     'L1_attn_Wk': 8.0,
     'L1_attn_lambda_q1': 8.0,
     'L1_attn_lambda_k1': 8.0,
     'L1_attn_lambda_q2': 8.0,
     'L1_attn_lambda_k2': 8.0}
    for name, (base, spread) in spreads.items():
        noise = np.random.default_rng([zlib.crc32(name.encode()), seed]).standard_normal(out[name].shape)
        drawn = base * np.exp(spread * noise) if base else spread * noise
        out[name] = jnp.asarray(drawn.astype(out[name].dtype))
    for name, factor in factors.items():
        out[name] = (out[name] * factor).astype(out[name].dtype)
    return out
```

```python
from contextlib import ExitStack

import concourse.bass as bass
from concourse import mybir

F32 = mybir.dt.float32
I32 = mybir.dt.int32
U32 = mybir.dt.uint32
ALU = mybir.AluOpType
ACT = mybir.ActivationFunctionType
AX = mybir.AxisListType.X

P = 128
B = 64
D = 192
DH = D // 2
F = 768
HF = F // 2
MT = F // P
WD = 75
H0, HD0 = 12, 64
PAIRS = H0 // 2
SIDE = 11
NV = (P - 2) // SIDE + 1
NGV, NGH = NV + 1, SIDE + 1
CUT = 1 + 6 * SIDE
E = 8
CAP = B * P + P
TILES = 2 * B * P // P + E
DUMP = E * CAP
NSUB, HS = 24, 8
H1, HV = 12, 16
NCLS = 6
GRP = 4
LAMBDA_INIT = 0.8 - 0.6
BIG = 3.4028234663852886e38
FEAT_CLAMP = 10.0
V_MAX = 3.0
CLS_PAIRS = [[(0, 3), (3, 0)], [(0, 4), (4, 0)], [(1, 3), (3, 1)], [(1, 4), (4, 1)], [(2, 3), (3, 2)], [(2, 4), (4, 2)]]

CONSTS = {}
_at = 0
for _n, _w in (("ident", P), ("anti", P), ("tri", P), ("ones", P), ("ohk", P), ("ohv", 32), ("iota8", 8), ("step128", TILES),
               ("ebase", 8), ("neg_half", 1), ("eps12", 1), ("eps5", 1)):
    CONSTS[_n] = (_at, _w)
    _at += _w
NCONST = _at
ROWS = {}
_at = 0
for _n, _w in (("type", D), ("gamma", D), ("beta", D), ("gatew", D), ("gateb", 1), ("bproj", D), ("subln", D),
               ("moe0_b2", D), ("a2_b", 5 * D), ("lam", 4 * HS)):
    ROWS[_n] = (_at, _w)
    _at += _w
NROW = _at


def norm_statistics(v, w, sem, src):
    v.bn_stats(w["st"][:], src).then_inc(sem["dve"], 1)
    v.wait_ge(sem["dve"], 1)
    v.sem_inc(sem["dve"], -1)
    v.bn_aggr(w["mv"][:], w["st"][:]).then_inc(sem["var"], 1)


def norm_apply(v, w, sem, src, dst, done):
    v.wait_ge(sem["rstd"], 1)
    v.sem_inc(sem["rstd"], -1)
    return v.tensor_scalar(dst, src, w["mv"][:, 0:1], w["rstd"][:], ALU.subtract, ALU.mult).then_inc(done, 1)


def layer_norm(v, w, sem, src, dst, done):
    norm_statistics(v, w, sem, src)
    return norm_apply(v, w, sem, src, dst, done)


def inverse_root(g, w, sem, eps, half):
    g.wait_ge(sem["var"], 1)
    g.sem_inc(sem["var"], -1)
    g.tensor_tensor(w["ve"][:], w["mv"][:, 1:2], eps, ALU.add).then_inc(sem["pool"], 1)
    g.wait_ge(sem["pool"], 1)
    g.sem_inc(sem["pool"], -1)
    g.tensor_tensor(w["rstd"][:], w["ve"][:], half, ALU.pow).then_inc(sem["rstd"], 1)


class Tower:
    def __init__(self, nc, ins, out):
        self.nc, self.ins, self.out = nc, ins, out

    def sems(self, ctx, *names):
        return {n: ctx.enter_context(self.nc.semaphore(n)) for n in names}

    def build(self):
        nc, ins = self.nc, self.ins
        with ExitStack() as ctx:
            def sb(name, shape, dt=F32):
                return ctx.enter_context(nc.sbuf_tensor(name, shape, dt))
            self.ps = [ctx.enter_context(nc.psum_tensor(f"bank{i}", [P, 512], F32)) for i in range(8)]
            self.h = sb("h", [P, B * D])
            self.consts = sb("consts", [P, NCONST])
            self.rows = sb("rows", [P, NROW])
            self.w1 = sb("moe_w1", [DH + 1, E * 2 * F])
            self.slots = sb("slots", [P, 2 * B])
            self.yrows = sb("yrows", [P, 2 * B], I32)
            self.mixw = sb("mixw", [P, 2 * B])
            self.feats = sb("feats", [P, B * 11])
            self.vall = sb("vall", [P, B])
            self.slotbase = sb("slotbase", [P, E])
            self.mixrows = sb("mixrows", [11, D])
            self.mixscale = sb("mixscale", [11, D])
            self.ln = {"st": sb("ln_st", [P, 6]), "mv": sb("ln_mv", [P, 2]), "ve": sb("ln_ve", [P, 1]),
                       "rstd": sb("ln_rstd", [P, 1])}
            self.zslots = nc.dram_tensor("zslots", ((E + 1) * CAP, D), F32, kind="Internal").ap()
            self.yslots = nc.dram_tensor("yslots", (TILES * P, D), F32, kind="Internal").ap()
            self.S = self.sems(ctx, "dve", "act", "pool", "var", "rstd", "loaded", "w1_loaded", "l1_loaded")
            self.embed_and_attend()
            self.w_qk = sb("w_qk", [DH + 1, 2 * 2 * F])
            self.w_vo = sb("w_vo", [DH + 1, 2 * 2 * D])
            self.w_up = sb("w_up", [DH + 1, 2 * F])
            self.w_down = sb("w_down", [P, MT * D])
            self.experts()
            self.differential_attention()
            self.feed_forward()

    def c(self, name, rows=slice(0, P)):
        a, w = CONSTS[name]
        return self.consts[rows, a:a + w]

    def r(self, name):
        a, w = ROWS[name]
        return self.rows[:, a:a + w]

    def embed_and_attend(self):
        nc, ins, ps, h, T = self.nc, self.ins, self.ps, self.h, self.S
        with ExitStack() as ctx:
            def sb(name, shape, dt=F32):
                return ctx.enter_context(nc.sbuf_tensor(name, shape, dt))
            wqkv = sb("wqkv", [DH, 3 * 2 * F])
            wproj = sb("wproj", [P, MT * D])
            relk = sb("relk", [P, (NGV + NGH) * 64])
            relv = sb("relv", [64, (NGV + NGH) * P])
            wroute = sb("wroute", [DH + 1, 2 * 9])
            g2b = sb("g2b", [WD + 1, D])
            postype = sb("postype", [P, D])
            negb = sb("negb", [P, 1])
            ids_in = sb("ids_in", [B, 2 * P], I32)
            ids_f = sb("ids_f", [B, 2 * P])
            ids = sb("ids", [P, 2 * B], I32)
            idw, idv = sb("idw", [P, 1], I32), sb("idv", [P, 1], I32)
            wrow, vrow = sb("wrow", [P, D]), sb("vrow", [P, WD + 1])
            emb, nrm, tok, h0, y, z, junk = (sb(n, [P, D]) for n in ("emb", "nrm", "tok", "h0", "y", "z", "junk"))
            vrowT = sb("vrowT", [WD + 1, P])
            zs = sb("zs", [P, 4])
            yT = sb("yT", [DH, 2 * P])
            zT = sb("zT", [DH + 1, 2 * P])
            qT = sb("qT", [P, PAIRS * P])
            qa, ka = sb("qa", [88, H0 * P]), sb("ka", [88, H0 * P])
            vv = sb("vv", [P, F])
            probs = sb("probs", [P, H0 * P])
            probsT = sb("probsT", [P, H0 * P])
            avT = sb("avT", [64, PAIRS * P])
            oT = sb("oT", [P, PAIRS * P])
            nmax, psum_, rinv = sb("nmax", [P, H0]), sb("psum_", [P, H0]), sb("rinv", [P, H0])
            lg = sb("lg", [P, 9])
            rt = sb("rt", [P, 4])
            prob8, top8, oh1, oh2, cmb, rank = (sb(n, [P, E]) for n in ("prob8", "top8", "oh1", "oh2", "cmb", "rank"))
            both = sb("both", [P, E])
            top8i = sb("top8i", [P, E], U32)
            top2f = sb("top2f", [P, 2])
            w2s = sb("w2s", [P, 2])
            s2f = sb("s2f", [P, 2])
            ids1, ids2 = sb("ids1", [P, 1], I32), sb("ids2", [P, 1], I32)

            S = self.sems(
                ctx, "ids_loaded", "ids_float", "ids_ps", "ids_ready", "word_in", "wvec_in", "word_free", "wvec_free",
                "vrowT_ps", "vrowT_in", "gate_z", "gate_e", "g_ps", "g_free", "y_ready", "y_free", "yT_ps", "yT_in",
                "qk_ps", "q_in", "k_ps", "k_in", "qr_ps", "qr_in", "s_ps", "nmax_ready", "exp_done", "probs_ready",
                "pT_ps", "pT_in", "v_ps", "v_in", "av_ps", "av_in", "o_ps", "o_in", "proj_ps", "proj_free",
                "z_ready", "z_free", "zT_ps", "zT_in", "lg_ps", "rank_free", "rt_max", "values_done", "rt_exp", "chosen", "rank_ps",
                "slot_ready", "z_scattered", "idx_free")
            block = ctx.enter_context(nc.Block())
            NW = 11

            def heads(t):
                return t[:].rearrange("p (h t) -> p h t", t=P)

            def by_parity(t, e):
                return t[:].rearrange("p (h e t) -> p e h t", e=2, t=P)[:, e]

            ranges = ((0, CUT), (CUT, P))

            def group_cols(g, bank):
                lo, hi = ranges[bank]
                if g < NGV:
                    a, b_, st = (1 + SIDE * g, min(1 + SIDE * (g + 1), P), 1) if g < NV else (0, 1, 1)
                else:
                    g -= NGV
                    a, b_, st = (1 + g, P, SIDE) if g < SIDE else (0, 1, 1)
                cols = [i for i in range(a, b_, st) if lo <= i < hi]
                return slice(cols[0], cols[-1] + 1, st) if cols else None

            def bank_slice(s, bank):
                lo = ranges[bank][0]
                return slice(s.start - lo, s.stop - lo, s.step)

            def banked(tile, bank, rows):
                n = ranges[bank][1] - ranges[bank][0]
                return tile[rows, 0:PAIRS * n].rearrange("p (h t) -> p h t", t=n)

            @block.sync
            def _(sp):
                sp.dma_start(ids_in[:, 0:P], ins["x"]).then_inc(S["ids_loaded"], 16)
                sp.dma_start(ids_in[:, P:2 * P], ins["itok"]).then_inc(S["ids_loaded"], 16)
                sp.dma_start(self.consts[:], ins["consts"]).then_inc(T["loaded"], 16)
                sp.dma_start(self.rows[:], ins["rows"].partition_broadcast(P)).then_inc(T["loaded"], 16)
                sp.dma_start(postype[:], ins["pos"]).then_inc(T["loaded"], 16)
                sp.dma_start(g2b[:], ins["g2b"]).then_inc(T["loaded"], 16)
                sp.dma_start(wqkv[:], ins["wqkv"]).then_inc(T["loaded"], 16)
                sp.dma_start(relk[:], ins["relk"]).then_inc(T["loaded"], 16)
                sp.dma_start(relv[:], ins["relv"]).then_inc(T["loaded"], 16)
                sp.dma_start(wproj[:], ins["wproj"]).then_inc(T["loaded"], 16)
                sp.dma_start(wroute[:], ins["wroute"]).then_inc(T["loaded"], 16)
                sp.dma_start(self.mixrows[:], ins["mixrows"]).then_inc(T["loaded"], 16)
                sp.dma_start(self.mixscale[:], ins["mixscale"]).then_inc(T["loaded"], 16)
                sp.dma_start(self.w1[:], ins["moe_w1"]).then_inc(T["w1_loaded"], 16)

            @block.gpsimd
            def _(g):
                neg_half = self.c("neg_half")

                def gather_words(b, first=False):
                    if not first:
                        g.wait_ge(S["word_free"], 1)
                        g.sem_inc(S["word_free"], -1)
                    g.tensor_copy(idw[:], ids[:, bass.ds(b, 1)]).then_inc(T["pool"], 1)
                    g.wait_ge(T["pool"], 1)
                    g.sem_inc(T["pool"], -1)
                    g.indirect_dma_start(out=wrow[:], out_offset=None, in_=ins["word_emb"],
                                         in_offset=bass.IndirectOffsetOnAxis(ap=idw[:, 0:1], axis=0)
                                         ).then_inc(S["word_in"], 16)

                def gather_vectors(b, first=False):
                    if not first:
                        g.wait_ge(S["wvec_free"], 1)
                        g.sem_inc(S["wvec_free"], -1)
                    g.tensor_copy(idv[:], ids[:, bass.ds(b + B, 1)]).then_inc(T["pool"], 1)
                    g.wait_ge(T["pool"], 1)
                    g.sem_inc(T["pool"], -1)
                    g.indirect_dma_start(out=vrow[:, 0:WD], out_offset=None, in_=ins["wvec"],
                                         in_offset=bass.IndirectOffsetOnAxis(ap=idv[:, 0:1], axis=0)
                                         ).then_inc(S["wvec_in"], 16)

                def gather(b, first=False):
                    gather_words(b, first)
                    gather_vectors(b, first)

                def word_norm():
                    inverse_root(g, self.ln, T, self.c("eps12"), neg_half)

                def y_norm():
                    inverse_root(g, self.ln, T, self.c("eps5"), neg_half)

                def tail_norm():
                    inverse_root(g, self.ln, T, self.c("eps5"), neg_half)

                def scatter():
                    g.wait_ge(S["slot_ready"], 1)
                    g.sem_inc(S["slot_ready"], -1)
                    for ix in (ids1, ids2):
                        g.indirect_dma_start(out=self.zslots, out_offset=bass.IndirectOffsetOnAxis(ap=ix[:, 0:1], axis=0),
                                             in_=z[:], in_offset=None).then_inc(S["z_scattered"], 16)

                g.wait_ge(S["ids_ready"], 1)
                g.sem_inc(S["ids_ready"], -1)
                g.wait_ge(T["loaded"], 16 * NW)
                gather(0, first=True)
                word_norm()
                gather(1)
                y_norm()
                word_norm()
                gather(2)
                y_norm()

                def step(b, routed, fetch, embed):
                    if routed:
                        tail_norm()
                    if embed:
                        word_norm()
                    if fetch:
                        gather(b + 3)
                    if embed:
                        y_norm()
                    if routed:
                        scatter()
                step(0, False, True, True)
                with g.Fori(1, B - 3) as b:
                    step(b, True, True, True)
                step(B - 3, True, False, True)
                step(B - 2, True, False, False)
                step(B - 1, True, False, False)
                tail_norm()
                scatter()

            @block.scalar
            def _(act):
                act.wait_ge(T["loaded"], 16 * NW)
                act.activation(negb[:], self.r("gateb"), ACT.Copy, scale=-1.0).then_inc(T["act"], 1)
                act.wait_ge(T["act"], 1)
                act.sem_inc(T["act"], -1)

                def vrowT_evac():
                    act.wait_ge(S["vrowT_ps"], 1)
                    act.sem_inc(S["vrowT_ps"], -1)
                    act.activation(vrowT[:], ps[7][0:WD + 1, 0:P], ACT.Copy).then_inc(S["vrowT_in"], 1)

                def gate_exp():
                    act.wait_ge(S["gate_z"], 1)
                    act.sem_inc(S["gate_z"], -1)
                    act.activation(zs[:, 1:2], zs[:, 0:1], ACT.Exp, bias=negb[:], scale=-1.0).then_inc(S["gate_e"], 1)

                def yT_evac():
                    act.wait_ge(S["yT_ps"], 1)
                    act.sem_inc(S["yT_ps"], -1)
                    act.activation(yT[:], ps[7][0:DH, 0:2 * P], ACT.Copy).then_inc(S["yT_in"], 1)

                def q_evac():
                    act.wait_ge(S["qk_ps"], 2)
                    act.sem_inc(S["qk_ps"], -2)
                    for bank, n in ((3, 4), (4, 2)):
                        a = 0 if bank == 3 else 4
                        act.activation(qT[:, a * P:(a + n) * P], ps[bank][:, 0:n * P], ACT.Copy, scale=HD0 ** -0.5)
                    for bank, n in ((3, 4), (4, 2)):
                        a = 0 if bank == 3 else 4
                        for e in range(2):
                            last = act.activation(by_parity(qa, e)[0:64, a:a + n, :],
                                                  ps[bank][64 * e:64 * e + 64, 0:n * P].rearrange("p (h t) -> p h t", t=P),
                                                  ACT.Copy, scale=HD0 ** -0.5)
                    last.then_inc(S["q_in"], 1)

                def v_evac(first=False):
                    if not first:
                        act.wait_ge(S["values_done"], 1)
                        act.sem_inc(S["values_done"], -1)
                    for i in range(2):
                        act.wait_ge(S["v_ps"], 1)
                        act.sem_inc(S["v_ps"], -1)
                        act.activation(vv[:, 384 * i:384 * i + 384], ps[i][:, 0:384], ACT.Copy).then_inc(S["v_in"], 1)

                def softmax():
                    for g in range(3):
                        act.wait_ge(S["nmax_ready"], 1)
                        act.sem_inc(S["nmax_ready"], -1)
                        for k in range(4):
                            n = 4 * g + k
                            last = act.activation(probs[:, P * n:P * n + P], ps[g][:, P * k:P * k + P], ACT.Exp,
                                                  bias=nmax[:, n:n + 1], accum_out=psum_[:, n:n + 1])
                        last.then_inc(S["exp_done"], 1)

                def pT_evac():
                    for g in range(3):
                        act.wait_ge(S["pT_ps"], 1)
                        act.sem_inc(S["pT_ps"], -1)
                        act.activation(probsT[:, 512 * g:512 * g + 512], ps[g][:], ACT.Copy).then_inc(S["pT_in"], 1)

                def zT_evac():
                    act.wait_ge(S["zT_ps"], 1)
                    act.sem_inc(S["zT_ps"], -1)
                    act.activation(zT[0:DH, :], ps[7][0:DH, 2 * P:4 * P], ACT.Copy).then_inc(S["zT_in"], 1)

                def route_exp():
                    act.wait_ge(S["rt_max"], 1)
                    act.sem_inc(S["rt_max"], -1)
                    act.activation(prob8[:], lg[:, 0:8], ACT.Exp, bias=rt[:, 0:1], accum_out=rt[:, 1:2]).then_inc(S["rt_exp"], 1)

                vrowT_evac()
                gate_exp()
                yT_evac()
                q_evac()
                v_evac(first=True)
                vrowT_evac()
                gate_exp()
                yT_evac()

                def step(route, one, two):
                    softmax()
                    if one:
                        q_evac()
                    pT_evac()
                    if two:
                        vrowT_evac()
                    if route:
                        zT_evac()
                    if two:
                        gate_exp()
                    if route:
                        route_exp()
                    if one:
                        v_evac()
                    if two:
                        yT_evac()
                    if not one:
                        act.wait_ge(S["values_done"], 1)
                        act.sem_inc(S["values_done"], -1)
                step(False, True, True)
                with act.Fori(1, B - 2) as b:
                    step(True, True, True)
                step(True, True, False)
                step(True, False, False)
                zT_evac()
                route_exp()

            @block.vector
            def _(v):
                def own(ins_):
                    ins_.then_inc(T["dve"], 1)
                    v.wait_ge(T["dve"], 1)
                    v.sem_inc(T["dve"], -1)

                v.wait_ge(T["loaded"], 16 * NW)
                v.memset(zT[DH:DH + 1, :], 1.0)
                v.memset(vrow[:, WD:WD + 1], 1.0)
                v.memset(self.feats[:], 1.0)
                v.tensor_copy(ka[64:88, :].rearrange("p (h t) -> p h t", t=P),
                              self.c("ohk", slice(64, 88)).unsqueeze(1).to_broadcast([24, H0, P]))
                v.wait_ge(S["ids_loaded"], 32)
                v.tensor_copy(ids_f[:], ids_in[:]).then_inc(S["ids_float"], 1)
                v.tensor_copy(self.slotbase[:], self.c("ebase"))
                own(v.tensor_tensor(postype[:], postype[:], self.r("type"), ALU.add))
                v.wait_ge(S["ids_ps"], 1)
                v.sem_inc(S["ids_ps"], -1)
                v.tensor_copy(ids[:], ps[7][:, 0:2 * B]).then_inc(S["ids_ready"], 1)

                def embed(b):
                    v.wait_ge(S["word_in"], 16 * (b + 1))
                    own(v.tensor_tensor(emb[:], wrow[:], postype[:], ALU.add))
                    v.sem_inc(S["word_free"], 1)
                    layer_norm(v, self.ln, T, emb[:], nrm[:], T["dve"])
                    v.wait_ge(T["dve"], 1)
                    v.sem_inc(T["dve"], -1)
                    own(v.tensor_tensor(nrm[:], nrm[:], self.r("gamma"), ALU.mult))
                    own(v.tensor_tensor(tok[:], nrm[:], self.r("beta"), ALU.add))
                    v.tensor_tensor_reduce(out=junk[:], in0=tok[:], in1=self.r("gatew"), scale=1.0, scalar=0.0,
                                           op0=ALU.mult, op1=ALU.add, accum_out=zs[:, 0:1]).then_inc(S["gate_z"], 1)

                def gate(b, first=False):
                    v.wait_ge(S["gate_e"], 1)
                    v.sem_inc(S["gate_e"], -1)
                    own(v.tensor_scalar(zs[:, 2:3], zs[:, 1:2], 1.0, None, ALU.add))
                    own(v.reciprocal(zs[:, 3:4], zs[:, 2:3]))
                    v.wait_ge(S["g_ps"], 1)
                    v.sem_inc(S["g_ps"], -1)
                    own(v.tensor_tensor(nrm[:], ps[7][:, P:P + D], tok[:], ALU.subtract))
                    own(v.scalar_tensor_tensor(out=h0[:], in0=nrm[:], scalar=zs[:, 3:4], in1=tok[:],
                                               op0=ALU.mult, op1=ALU.add))
                    v.tensor_tensor(h[:, bass.ds(b * D, D)], h0[:], self.r("bproj"), ALU.add)
                    if not first:
                        v.wait_ge(S["y_free"], 1)
                        v.sem_inc(S["y_free"], -1)
                    layer_norm(v, self.ln, T, h0[:], y[:], S["y_ready"])

                def k_evac():
                    v.wait_ge(S["k_ps"], 1)
                    v.sem_inc(S["k_ps"], -1)
                    for bank, a, n in ((5, 0, 4), (6, 4, 2)):
                        for e in range(2):
                            last = v.tensor_copy(by_parity(ka, e)[0:64, a:a + n, :],
                                                 ps[bank][64 * e:64 * e + 64, 0:n * P].rearrange("p (h t) -> p h t", t=P))
                    last.then_inc(S["k_in"], 1)

                def qr_evac():
                    v.wait_ge(S["qr_ps"], 1)
                    v.sem_inc(S["qr_ps"], -1)
                    for bank in range(2):
                        lo, hi = ranges[bank]
                        for e in range(2):
                            last = v.tensor_copy(by_parity(qa, e)[64:88, :, lo:hi],
                                                 banked(ps[3 + bank], bank, slice(32 * e, 32 * e + 24)))
                    last.then_inc(S["qr_in"], 1)

                def pair_evac(src, dst, rows, ready, done):
                    v.wait_ge(S[ready], 1)
                    v.sem_inc(S[ready], -1)
                    for bank in range(2):
                        lo, hi = ranges[bank]
                        last = v.tensor_copy(dst[:].rearrange("p (h t) -> p h t", t=P)[:, :, lo:hi], banked(ps[src[bank]], bank, rows))
                    last.then_inc(S[done], 1)

                def maxima():
                    for g in range(3):
                        v.wait_ge(S["s_ps"], 1)
                        v.sem_inc(S["s_ps"], -1)
                        v.tensor_reduce(out=nmax[:, 4 * g:4 * g + 4], in_=ps[g][:].rearrange("p (h t) -> p h t", t=P),
                                        op=ALU.max, axis=AX, negate=True).then_inc(S["nmax_ready"], 1)

                def normalise():
                    for g in range(3):
                        v.wait_ge(S["exp_done"], 1)
                        v.sem_inc(S["exp_done"], -1)
                        own(v.reciprocal(rinv[:, 4 * g:4 * g + 4], psum_[:, 4 * g:4 * g + 4]))
                        e4 = probs[:, 512 * g:512 * g + 512].rearrange("p (h t) -> p h t", t=P)
                        v.tensor_tensor(e4, e4, rinv[:, 4 * g:4 * g + 4].unsqueeze(2).to_broadcast([P, 4, P]),
                                        ALU.mult).then_inc(S["probs_ready"], 1)

                def add_proj(b):
                    v.wait_ge(S["proj_ps"], 1)
                    v.sem_inc(S["proj_ps"], -1)
                    own(v.tensor_tensor(h[:, bass.ds(b * D, D)], h[:, bass.ds(b * D, D)], ps[5][:, 0:D], ALU.add))
                    v.sem_inc(S["proj_free"], 1)

                def tail_norm(b, first=False):
                    if not first:
                        v.wait_ge(S["z_scattered"], 32 * b)
                        v.wait_ge(S["z_free"], 1)
                        v.sem_inc(S["z_free"], -1)
                    norm_apply(v, self.ln, T, h[:, bass.ds(b * D, D)], z[:], S["z_ready"])

                def choose(b):
                    v.wait_ge(S["lg_ps"], 1)
                    v.sem_inc(S["lg_ps"], -1)
                    own(v.tensor_copy(lg[:], ps[2][:, 0:9]))
                    v.tensor_copy(self.vall[:, bass.ds(b, 1)], lg[:, 8:9])
                    v.tensor_reduce(out=rt[:, 0:1], in_=lg[:, 0:8], op=ALU.max, axis=AX, negate=True).then_inc(S["rt_max"], 1)
                    v.wait_ge(S["rt_exp"], 1)
                    v.sem_inc(S["rt_exp"], -1)
                    own(v.reciprocal(rt[:, 2:3], rt[:, 1:2]))
                    own(v.tensor_scalar(prob8[:], prob8[:], rt[:, 2:3], None, ALU.mult))
                    own(v.max(out=top8[:], in_=prob8[:]))
                    own(v.max_index(out=top8i[:], in_max=top8[:], in_values=prob8[:]))
                    own(v.tensor_copy(top2f[:], top8i[:, 0:2]))
                    v.tensor_scalar(oh1[:], self.c("iota8"), top2f[:, 0:1], None, ALU.is_equal)
                    own(v.tensor_scalar(oh2[:], self.c("iota8"), top2f[:, 1:2], None, ALU.is_equal))
                    v.tensor_tensor(both[:], oh1[:], oh2[:], ALU.add).then_inc(S["chosen"], 1)
                    own(v.tensor_tensor(rt[:, 3:4], top8[:, 0:1], top8[:, 1:2], ALU.add))
                    own(v.reciprocal(rt[:, 2:3], rt[:, 3:4]))
                    own(v.tensor_scalar(w2s[:], top8[:, 0:2], rt[:, 2:3], None, ALU.mult))
                    v.tensor_copy(self.mixw[:, bass.ds(2 * b, 2)], w2s[:])
                    own(v.tensor_scalar(cmb[:], oh1[:], w2s[:, 0:1], None, ALU.mult))
                    v.scalar_tensor_tensor(out=self.feats[:, bass.ds(11 * b, 8)], in0=oh2[:], scalar=w2s[:, 1:2], in1=cmb[:],
                                           op0=ALU.mult, op1=ALU.add)

                def place(b):
                    v.wait_ge(S["rank_ps"], 1)
                    v.sem_inc(S["rank_ps"], -1)
                    own(v.tensor_tensor(rank[:], ps[6][:, 0:8], self.slotbase[:], ALU.add))
                    own(v.tensor_tensor(self.slotbase[:], self.slotbase[:], ps[6][:, 8:16], ALU.add))
                    v.sem_inc(S["rank_free"], 1)
                    v.tensor_tensor_reduce(out=cmb[:], in0=oh1[:], in1=rank[:], scale=1.0, scalar=0.0, op0=ALU.mult,
                                           op1=ALU.add, accum_out=s2f[:, 0:1])
                    own(v.tensor_tensor_reduce(out=top8[:], in0=oh2[:], in1=rank[:], scale=1.0, scalar=0.0, op0=ALU.mult,
                                               op1=ALU.add, accum_out=s2f[:, 1:2]))
                    v.tensor_copy(self.slots[:, bass.ds(2 * b, 2)], s2f[:])
                    v.tensor_copy(ids1[:], s2f[:, 0:1])
                    v.tensor_copy(ids2[:], s2f[:, 1:2]).then_inc(S["slot_ready"], 1)

                embed(0)
                gate(0, first=True)
                k_evac()
                qr_evac()
                embed(1)
                gate(1)

                def step(b, routed, one, two, first_tail=False):
                    maxima()
                    if routed:
                        add_proj(b - 1)
                        norm_statistics(v, self.ln, T, h[:, bass.ds((b - 1) * D, D)])
                    normalise()
                    if one:
                        k_evac()
                    if routed:
                        tail_norm(b - 1, first=first_tail)
                    if two:
                        embed(b + 2)
                    if one:
                        qr_evac()
                    pair_evac((5, 6), avT, slice(0, 64), "av_ps", "av_in")
                    if routed:
                        choose(b - 1)
                    if two:
                        gate(b + 2)
                    if routed:
                        place(b - 1)
                    pair_evac((3, 4), oT, slice(0, P), "o_ps", "o_in")
                step(0, False, True, True)
                step(1, True, True, True, first_tail=True)
                with v.Fori(2, B - 2) as b:
                    step(b, True, True, True)
                step(B - 2, True, True, False)
                step(B - 1, True, False, False)
                add_proj(B - 1)
                norm_statistics(v, self.ln, T, h[:, (B - 1) * D:B * D])
                tail_norm(B - 1)
                choose(B - 1)
                place(B - 1)
                v.wait_ge(S["z_scattered"], 32 * B)

            @block.tensor
            def _(pe):
                ident = self.c("ident")
                pe.wait_ge(T["loaded"], 16 * NW)
                pe.wait_ge(S["ids_float"], 1)
                pe.sem_inc(S["ids_float"], -1)
                pe.transpose(ps[7][:, 0:B], ids_f[:, 0:P], ident[0:B, 0:B])
                pe.transpose(ps[7][:, B:2 * B], ids_f[:, P:2 * P], ident[0:B, 0:B]).then_inc(S["ids_ps"], 1)

                def vrow_T(b):
                    pe.wait_ge(S["wvec_in"], 16 * (b + 1))
                    pe.transpose(ps[7][0:WD + 1, 0:P], vrow[:], ident).then_inc(S["vrowT_ps"], 1)

                def word_proj():
                    pe.wait_ge(S["vrowT_in"], 1)
                    pe.sem_inc(S["vrowT_in"], -1)
                    pe.sem_inc(S["wvec_free"], 1)
                    pe.matmul(ps[7][:, P:P + D], vrowT[:], g2b[:], start=True, stop=True).then_inc(S["g_ps"], 1)

                def y_T():
                    pe.wait_ge(S["y_ready"], 1)
                    pe.sem_inc(S["y_ready"], -1)
                    for c in range(2):
                        last = pe.transpose(ps[7][0:DH, P * c:P * c + P], y[:, DH * c:DH * c + DH], ident)
                    last.then_inc(S["yT_ps"], 1)

                def qk_proj(before_k=None):
                    pe.wait_ge(S["yT_in"], 1)
                    pe.sem_inc(S["yT_in"], -1)
                    pe.sem_inc(S["y_free"], 1)
                    for t in range(12):
                        which, m = t // 6, t % 6
                        if t == 6 and before_k:
                            before_k()
                        for c in range(2):
                            a = which * 2 * F + c * F + m * P
                            last = pe.matmul(ps[3 + 2 * which + m // 4][:, (m % 4) * P:(m % 4) * P + P], wqkv[:, a:a + P],
                                             yT[:, P * c:P * c + P], start=(c == 0), stop=(c == 1))
                        if t == 3 or t == 5:
                            last.then_inc(S["qk_ps"], 1)
                        if t == 11:
                            last.then_inc(S["k_ps"], 1)

                def groups(bank):
                    return [(g, group_cols(g, bank)) for g in range(NGV + NGH) if group_cols(g, bank) is not None]

                def query_relations():
                    pe.wait_ge(S["q_in"], 1)
                    pe.sem_inc(S["q_in"], -1)
                    q3 = heads(qT)
                    for bank in range(2):
                        o = banked(ps[3 + bank], bank, slice(0, 64))
                        gs = groups(bank)
                        for n, (g, cols) in enumerate(gs):
                            last = pe.matmul(o[:, :, bank_slice(cols, bank)], relk[:, 64 * g:64 * g + 64], q3[:, :, cols],
                                             start=(n == 0), stop=(n == len(gs) - 1), skip_group_check=True)
                    last.then_inc(S["qr_ps"], 1)

                def v_proj():
                    for i in range(2):
                        for c in range(2):
                            a = 4 * F + c * F + 384 * i
                            last = pe.matmul(ps[i][:, 0:384], yT[:, P * c:P * c + P], wqkv[:, a:a + 384],
                                             start=(c == 0), stop=(c == 1))
                        last.then_inc(S["v_ps"], 1)

                def scores():
                    for n in range(H0):
                        last = pe.matmul(ps[n // 4][:, (n % 4) * P:(n % 4) * P + P], qa[:, P * n:P * n + P],
                                         ka[:, P * n:P * n + P], start=True, stop=True)
                        if n % 4 == 3:
                            last.then_inc(S["s_ps"], 1)

                def probs_T():
                    for g in range(3):
                        pe.wait_ge(S["probs_ready"], 1)
                        pe.sem_inc(S["probs_ready"], -1)
                        for k in range(4):
                            n = 4 * g + k
                            last = pe.transpose(ps[g][:, P * k:P * k + P], probs[:, P * n:P * n + P], ident)
                        last.then_inc(S["pT_ps"], 1)

                def probs_by_place():
                    pe.wait_ge(S["pT_in"], 3)
                    pe.sem_inc(S["pT_in"], -3)
                    pT = probsT[:].rearrange("p (h e t) -> p h e t", e=2, t=P)
                    for bank in range(2):
                        lo, hi = ranges[bank]
                        for e in range(2):
                            last = pe.matmul(banked(ps[5 + bank], bank, slice(32 * e, 32 * e + 32)), self.c("ohv"),
                                             pT[:, :, e, lo:hi], start=True, stop=True)
                    last.then_inc(S["av_ps"], 1)

                def values():
                    for bank in range(2):
                        lo, hi = ranges[bank]
                        for e in range(2):
                            for p_ in range(PAIRS):
                                n = 2 * p_ + e
                                last = pe.matmul(banked(ps[3 + bank], bank, slice(64 * e, 64 * e + 64))[:, p_, :],
                                          vv[:, 64 * n:64 * n + 64], probsT[:, P * n + lo:P * n + hi],
                                          start=(p_ == 0), stop=False, skip_group_check=True)
                    last.then_inc(S["values_done"], 1)

                def value_relations(between=None):
                    pe.wait_ge(S["av_in"], 1)
                    pe.sem_inc(S["av_in"], -1)
                    a3 = heads(avT)
                    for bank in range(2):
                        if bank and between:
                            between()
                        o = banked(ps[3 + bank], bank, slice(0, P))
                        gs = groups(bank)
                        for n, (g, cols) in enumerate(gs):
                            last = pe.matmul(o[:, :, bank_slice(cols, bank)], relv[:, P * g:P * g + P], a3[:, :, cols],
                                             start=False, stop=(n == len(gs) - 1), skip_group_check=True)
                    last.then_inc(S["o_ps"], 1)

                def out_proj():
                    pe.wait_ge(S["o_in"], 1)
                    pe.sem_inc(S["o_in"], -1)
                    for m in range(MT):
                        last = pe.matmul(ps[5][:, 0:D], oT[:, P * m:P * m + P], wproj[:, D * m:D * m + D],
                                         start=(m == 0), stop=(m == MT - 1))
                    last.then_inc(S["proj_ps"], 1)

                def z_T():
                    pe.wait_ge(S["z_ready"], 1)
                    pe.sem_inc(S["z_ready"], -1)
                    for c in range(2):
                        last = pe.transpose(ps[7][0:DH, P * (2 + c):P * (3 + c)], z[:, DH * c:DH * c + DH], ident)
                    last.then_inc(S["zT_ps"], 1)

                def zT_arrived():
                    pe.wait_ge(S["zT_in"], 1)
                    pe.sem_inc(S["zT_in"], -1)
                    pe.sem_inc(S["z_free"], 1)

                def route_logits():
                    for c in range(2):
                        k = DH + c
                        last = pe.matmul(ps[2][:, 0:9], zT[0:k, P * c:P * c + P], wroute[0:k, 9 * c:9 * c + 9],
                                         start=(c == 0), stop=(c == 1))
                    last.then_inc(S["lg_ps"], 1)

                def ranks():
                    pe.wait_ge(S["chosen"], 1)
                    pe.sem_inc(S["chosen"], -1)
                    pe.matmul(ps[6][:, 0:8], self.c("tri"), both[:], start=True, stop=True)
                    pe.matmul(ps[6][:, 8:16], self.c("ones"), both[:], start=True, stop=True).then_inc(S["rank_ps"], 1)

                vrow_T(0)
                word_proj()
                y_T()
                qk_proj()
                query_relations()
                pe.wait_ge(S["k_in"], 1)
                pe.sem_inc(S["k_in"], -1)
                v_proj()
                pe.wait_ge(S["qr_in"], 1)
                pe.sem_inc(S["qr_in"], -1)
                vrow_T(1)
                word_proj()
                y_T()

                def step(b, route, one, two, first=False, first_route=False):
                    pe.wait_ge(S["v_in"], 2)
                    pe.sem_inc(S["v_in"], -2)
                    scores()

                    def banks_free():
                        if not first:
                            pe.wait_ge(S["proj_free"], 1)
                            pe.sem_inc(S["proj_free"], -1)
                        if route and not first_route:
                            pe.wait_ge(S["rank_free"], 1)
                            pe.sem_inc(S["rank_free"], -1)
                    if one:
                        qk_proj(before_k=banks_free)
                    else:
                        banks_free()
                    probs_T()
                    if one:
                        query_relations()
                    if route:
                        z_T()
                    if two:
                        vrow_T(b + 2)
                    if one:
                        pe.wait_ge(S["k_in"], 1)
                        pe.sem_inc(S["k_in"], -1)
                    probs_by_place()
                    if route:
                        zT_arrived()
                    if two:
                        word_proj()
                    if route:
                        route_logits()
                    if one:
                        v_proj()
                        pe.wait_ge(S["qr_in"], 1)
                        pe.sem_inc(S["qr_in"], -1)
                    values()
                    value_relations(between=ranks if route else None)
                    if two:
                        y_T()
                    out_proj()
                step(0, False, True, True, first=True)
                step(1, True, True, True, first_route=True)
                with pe.Fori(2, B - 2) as b:
                    step(b, True, True, True)
                step(B - 2, True, True, False)
                step(B - 1, True, False, False)
                pe.wait_ge(S["proj_free"], 1)
                pe.sem_inc(S["proj_free"], -1)
                pe.wait_ge(S["rank_free"], 1)
                pe.sem_inc(S["rank_free"], -1)
                z_T()
                zT_arrived()
                route_logits()
                ranks()

    def experts(self):
        nc, ins, ps, T = self.nc, self.ins, self.ps, self.S
        with ExitStack() as ctx:
            def sb(name, shape, dt=F32):
                return ctx.enter_context(nc.sbuf_tensor(name, shape, dt))
            w2 = sb("moe_w2", [P, E * MT * D])
            coef = sb("coef", [P, TILES * 4])
            state = sb("state", [P, TILES * 4])

            def places(t, even, odd, n):
                v8 = t[:].rearrange("p (u c) -> p u c", c=8)
                return v8[:, 0:n // 2, even:odd + 5:odd + 4 - even]
            tile_row, tile_expert = sb("tile_row", [1, TILES], I32), sb("tile_expert", [1, TILES], I32)
            region_end = sb("region_end", [1, E], I32)
            zeros = sb("zeros", [P, D])
            vclip = sb("vclip", [P, B])
            zt = [sb(f"zt{p}", [P, D]) for p in range(2)]
            zT = [sb(f"zT{p}", [DH + 1, 2 * P]) for p in range(2)]
            hid2, hT2 = sb("hid", [P, 2 * F]), sb("hT", [P, 2 * F])
            hid = [hid2[:, F * p:F * p + F] for p in range(2)]
            hT = [hT2[:, F * p:F * p + F] for p in range(2)]
            yt = [sb(f"yt{p}", [P, D]) for p in range(2)]
            sq, nrm2, inv = sb("sq", [P, 2]), sb("nrm2", [P, 1]), sb("inv", [P, 1])
            big, big2 = hid2[0:1, 0:TILES * E], hT2[0:1, 0:TILES * E]
            t8 = sb("t8", [P, 6 * E])
            moved = sb("moved", [P, 2 * B])
            tt = sb("tt", [1, 4 * TILES])
            S = self.sems(ctx, "planned", "vclipped", "v_turned", "filled", "w2_loaded", "gelu_warm",
                          *(f"{n}{p}" for n in ("zt_in", "zt_free", "zT_ps", "zT_in", "h_ps", "h_in", "hT_ps", "hT_in", "y_ps", "y_in", "y_out")
                            for p in range(2)))
            S2 = self.sems(ctx, "state_split", "state_T", "state_in", "e_ps")
            dcomp = [hid2[:, 0:P], hid2[:, P:2 * P]]
            xs = [sb(f"xs{i}", [P, P]) for i in range(2)]
            fin = [sb(f"fin{i}", [P, B]) for i in range(4)]

            with nc.Block() as block:
                @block.sync
                def _(sp):
                    sp.dma_start(w2[:], ins["moe_w2"]).then_inc(S["w2_loaded"], 16)
                    for t, n, name in ((self.w_qk, 2, "wqk1"), (self.w_vo, 2, "wvo1"), (self.w_up, 1, "moe0_w1"), (self.w_down, 1, "moe0_w2")):
                        sp.dma_start(t[:], ins[name]).then_inc(T["l1_loaded"], 16)
                    sp.wait_ge(S["planned"], 1)
                    sp.sem_inc(S["planned"], -1)
                    for e in range(E):
                        r = sp.value_load(region_end[0:1, e:e + 1], min_val=0, max_val=E * CAP)
                        sp.dma_start(self.zslots[bass.ds(r, P), :], zeros[:]).then_inc(S["filled"], 16)
                        sp.dma_start(self.zslots[DUMP + P * e:DUMP + P * e + P, :], zeros[:]).then_inc(S["filled"], 16)
                    sp.wait_ge(S["filled"], 32 * E)
                    sp.wait_ge(T["w1_loaded"], 16)
                    sp.wait_ge(S["w2_loaded"], 16)
                    sp.wait_ge(T["l1_loaded"], 64)

                @block.vector
                def _(v):
                    def own(i):
                        i.then_inc(T["dve"], 1)
                        v.wait_ge(T["dve"], 1)
                        v.sem_inc(T["dve"], -1)
                    v.memset(zeros[:], 0.0)
                    for p in range(2):
                        v.memset(zT[p][DH:DH + 1, :], 1.0)
                    v.tensor_scalar(vclip[:], self.vall[:], -V_MAX, V_MAX, ALU.max, ALU.min).then_inc(S["vclipped"], 1)
                    total, tiles, incl, excl, shift, step = (t8[:, E * i:E * i + E] for i in range(6))
                    own(v.tensor_tensor(total, self.slotbase[:], self.c("ebase"), ALU.subtract))
                    m = hid2[:, 0:E * B].rearrange("p (e k) -> p e k", k=B)
                    own(v.tensor_tensor(m, total.unsqueeze(2).to_broadcast([P, E, B]),
                                        self.c("step128")[:, 0:B].unsqueeze(1).to_broadcast([P, E, B]), ALU.is_gt))
                    own(v.tensor_reduce(out=tiles, in_=m, op=ALU.add, axis=AX))
                    own(v.tensor_tensor_scan(incl, self.c("ones")[:, 0:E], tiles, 0.0, ALU.mult, ALU.add))
                    own(v.tensor_tensor(excl, incl, tiles, ALU.subtract))
                    own(v.tensor_scalar(shift, excl, -float(P), None, ALU.mult))
                    own(v.tensor_tensor(shift, shift, self.c("ebase"), ALU.add))
                    own(v.tensor_tensor(step[:, 1:E], shift[:, 0:E - 1], shift[:, 1:E], ALU.subtract))
                    own(v.tensor_copy(moved[:], self.slots[:]))
                    for e in range(1, E):
                        past = hT2[:, 0:2 * B]
                        own(v.tensor_scalar(past, self.slots[:], float(e * CAP), step[:, e:e + 1], ALU.is_ge, ALU.mult))
                        own(v.tensor_tensor(moved[:], moved[:], past, ALU.add))
                    v.tensor_copy(self.yrows[:], moved[:])
                    own(v.tensor_scalar(total, excl, float(P), None, ALU.mult))
                    own(v.tensor_scalar(incl, incl, float(P), None, ALU.mult))
                    total, incl, shift = total[0:1], incl[0:1], shift[0:1]
                    t128 = self.c("step128", slice(0, 1))
                    m1, m2 = (b_.rearrange("p (t e) -> p t e", e=E) for b_ in (big, big2))
                    tb = t128.unsqueeze(2).to_broadcast([1, TILES, E])

                    def eb(a):
                        return a.unsqueeze(1).to_broadcast([1, TILES, E])
                    v.tensor_tensor(m1, tb, eb(total), ALU.is_ge)
                    own(v.tensor_tensor(m2, tb, eb(incl), ALU.is_ge))
                    own(v.tensor_tensor(m1, m1, m2, ALU.subtract))
                    used, start, name, row = (tt[:, TILES * i:TILES * i + TILES] for i in range(4))
                    own(v.tensor_reduce(out=used, in_=m1, op=ALU.add, axis=AX))
                    own(v.tensor_tensor(m2, m1, eb(shift), ALU.mult))
                    own(v.tensor_reduce(out=start, in_=m2, op=ALU.add, axis=AX))
                    own(v.tensor_tensor(m2, m1, eb(self.c("iota8", slice(0, 1))), ALU.mult))
                    own(v.tensor_reduce(out=name, in_=m2, op=ALU.add, axis=AX))
                    own(v.tensor_scalar(used, used, -float(DUMP - 2 * B * P), float(DUMP - 2 * B * P), ALU.mult, ALU.add))
                    own(v.tensor_tensor(row, start, t128, ALU.add))
                    own(v.tensor_tensor(row, row, used, ALU.add))
                    v.tensor_copy(tile_row[:], row)
                    v.tensor_copy(tile_expert[:], name)
                    v.tensor_copy(region_end[:], self.slotbase[0:1, :]).then_inc(S["planned"], 1)
                    own(v.memset(coef[:], -1.0))
                    u0 = P // 2
                    c8 = coef[:].rearrange("p (u c) -> p u c", c=8)
                    for at, value in ((0, -2.0), (6, -2.0), (2, 2.0), (4, 2.0)):
                        v.memset(c8[:, u0:TILES // 2, at:at + 1], value)
                    v.wait_ge(S["v_turned"], 1)
                    v.sem_inc(S["v_turned"], -1)
                    turned = ps[0][:, 0:P].rearrange("p (u c) -> p u c", c=2)
                    v.tensor_scalar(places(coef, 0, 2, P), turned, -2.0, None, ALU.add)
                    own(v.tensor_scalar(c8[:, 0:u0, 2:5:2], turned, -1.0, 2.0, ALU.mult, ALU.add))
                    own(v.tensor_copy(state[:, 0:4], coef[:, 0:4]))

                @block.tensor
                def _(pe):
                    pe.wait_ge(S["vclipped"], 1)
                    pe.sem_inc(S["vclipped"], -1)
                    pe.matmul(ps[0][0:B, 0:P], vclip[:], self.c("ident"), start=True, stop=True)
                    pe.matmul(ps[0][B:2 * B, 0:P], vclip[:], self.c("anti"), start=True, stop=True).then_inc(S["v_turned"], 1)

                @block.scalar
                def _(act):
                    act.activation(self.ln["ve"][:], self.c("ones")[:, 0:1], ACT.Gelu_apprx_tanh).then_inc(S["gelu_warm"], 1)
                    act.wait_ge(S["gelu_warm"], 1)

            with nc.Block() as block:
                @block.sync
                def _(sp):
                    def row_of(t):
                        return sp.value_load(tile_row[0:1, bass.ds(t, 1)], min_val=0, max_val=(E + 1) * CAP - P)

                    def load(t, p, first=False):
                        if not first:
                            sp.wait_ge(S[f"zt_free{p}"], 1)
                            sp.sem_inc(S[f"zt_free{p}"], -1)
                        sp.dma_start(zt[p][:], self.zslots[bass.ds(row_of(t), P), :]).then_inc(S[f"zt_in{p}"], 16)

                    def store(t, p):
                        sp.wait_ge(S[f"y_in{p}"], 1)
                        sp.sem_inc(S[f"y_in{p}"], -1)
                        sp.dma_start(self.yslots[bass.ds(P * t, P), :], yt[p][:]).then_inc(S[f"y_out{p}"], 16)
                    load(0, 0, True)
                    load(1, 1, True)
                    with sp.Fori(0, TILES // 2 - 1) as u:
                        for p in range(2):
                            load(2 * u + p + 2, p)
                            store(2 * u + p, p)
                    for p in range(2):
                        store(TILES - 2 + p, p)
                    for p in range(2):
                        sp.wait_ge(S[f"y_out{p}"], 16)
                        sp.sem_inc(S[f"y_out{p}"], -16)

                @block.scalar
                def _(act):
                    def gelu(p):
                        for i in range(2):
                            act.wait_ge(S[f"h_ps{p}"], 1)
                            act.sem_inc(S[f"h_ps{p}"], -1)
                            act.activation(hid[p][:, HF * i:HF * i + HF], ps[2 * p + i][:, 0:HF],
                                           ACT.Gelu_apprx_tanh).then_inc(S[f"h_in{p}"], 1)
                    with act.Fori(0, TILES // 2) as _u:
                        gelu(0)
                        gelu(1)

                @block.vector
                def _(v):
                    def own(i):
                        i.then_inc(T["dve"], 1)
                        v.wait_ge(T["dve"], 1)
                        v.sem_inc(T["dve"], -1)

                    def zT_evac(p):
                        v.wait_ge(S[f"zT_ps{p}"], 1)
                        v.sem_inc(S[f"zT_ps{p}"], -1)
                        v.tensor_copy(zT[p][0:DH, :], ps[6 + p][0:DH, 0:2 * P]).then_inc(S[f"zT_in{p}"], 1)

                    def hT_evac(p):
                        for i in range(2):
                            v.wait_ge(S[f"hT_ps{p}"], 1)
                            v.sem_inc(S[f"hT_ps{p}"], -1)
                            v.tensor_copy(hT[p][:, HF * i:HF * i + HF], ps[2 * p + i][:, 0:HF]).then_inc(S[f"hT_in{p}"], 1)

                    def y_evac(p, first=False):
                        v.wait_ge(S[f"y_ps{p}"], 1)
                        v.sem_inc(S[f"y_ps{p}"], -1)
                        if not first:
                            v.wait_ge(S[f"y_out{p}"], 16)
                            v.sem_inc(S[f"y_out{p}"], -16)
                        v.tensor_copy(yt[p][:], ps[4 + p][:, 0:D]).then_inc(S[f"y_in{p}"], 1)

                    def recur(s):
                        own(v.tensor_tensor(sq[:], state[:, bass.ds(4 * s - 4, 2)], state[:, bass.ds(4 * s - 4, 2)], ALU.mult))
                        own(v.tensor_tensor(nrm2[:], sq[:, 0:1], sq[:, 1:2], ALU.add))
                        own(v.reciprocal(inv[:], nrm2[:]))
                        own(v.scalar_tensor_tensor(out=state[:, bass.ds(4 * s, 4)], in0=state[:, bass.ds(4 * s - 4, 4)],
                                                   scalar=inv[:], in1=coef[:, bass.ds(4 * s, 4)], op0=ALU.mult, op1=ALU.add))
                    zT_evac(0)
                    zT_evac(1)
                    for p in range(2):
                        zT_evac(p)
                        hT_evac(p)
                        y_evac(p, True)
                        recur(p + 1)
                    with v.Fori(1, TILES // 2 - 1) as u:
                        for p in range(2):
                            zT_evac(p)
                            hT_evac(p)
                            y_evac(p)
                            recur(2 * u + p + 1)
                    for p in range(2):
                        hT_evac(p)
                        y_evac(p)

                @block.tensor
                def _(pe):
                    def turn(p):
                        pe.wait_ge(S[f"zt_in{p}"], 16)
                        pe.sem_inc(S[f"zt_in{p}"], -16)
                        for c in range(2):
                            last = pe.transpose(ps[6 + p][0:DH, P * c:P * c + P], zt[p][:, DH * c:DH * c + DH], self.c("ident"))
                        last.then_inc(S[f"zT_ps{p}"], 1)

                    def expert_of(t):
                        return pe.value_load(tile_expert[0:1, bass.ds(t, 1)], min_val=0, max_val=E - 1)

                    def up(t, p, free=True):
                        e = expert_of(t)
                        pe.wait_ge(S[f"zT_in{p}"], 1)
                        pe.sem_inc(S[f"zT_in{p}"], -1)
                        if free:
                            pe.sem_inc(S[f"zt_free{p}"], 1)
                        for i in range(2):
                            for c in range(2):
                                k = DH + c
                                last = pe.matmul(ps[2 * p + i][:, 0:HF], zT[p][0:k, P * c:P * c + P],
                                                 self.w1[0:k, bass.ds(e * (2 * F) + (c * F + i * HF), HF)],
                                                 start=(c == 0), stop=(c == 1))
                            last.then_inc(S[f"h_ps{p}"], 1)

                    def hidden_T(p):
                        for i in range(2):
                            pe.wait_ge(S[f"h_in{p}"], 1)
                            pe.sem_inc(S[f"h_in{p}"], -1)
                            for m in range(3):
                                n = 3 * i + m
                                last = pe.transpose(ps[2 * p + i][:, P * m:P * m + P], hid[p][:, P * n:P * n + P], self.c("ident"))
                            last.then_inc(S[f"hT_ps{p}"], 1)

                    def down(t, p):
                        e = expert_of(t)
                        pe.wait_ge(S[f"hT_in{p}"], 2)
                        pe.sem_inc(S[f"hT_in{p}"], -2)
                        for m in range(MT):
                            last = pe.matmul(ps[4 + p][:, 0:D], hT[p][:, P * m:P * m + P],
                                             w2[:, bass.ds(e * (MT * D) + m * D, D)], start=(m == 0), stop=(m == MT - 1))
                        last.then_inc(S[f"y_ps{p}"], 1)
                    turn(0)
                    turn(1)
                    up(0, 0)
                    with pe.Fori(0, TILES // 2 - 1) as u:
                        for p in range(2):
                            turn(p)
                            hidden_T(p)
                            up(2 * u + p + 1, 1 - p)
                            down(2 * u + p, p)
                    hidden_T(0)
                    up(TILES - 1, 1, free=False)
                    down(TILES - 2, 0)
                    hidden_T(1)
                    down(TILES - 1, 1)

            with nc.Block() as block:
                @block.tensor
                def _(pe):
                    pe.wait_ge(S2["state_split"], 1)
                    pe.sem_inc(S2["state_split"], -1)
                    for i in range(2):
                        pe.transpose(ps[i][:, 0:P], dcomp[i][:], self.c("ident")).then_inc(S2["state_T"], 1)
                    for i in range(2):
                        pe.wait_ge(S2["state_in"], 1)
                        pe.sem_inc(S2["state_in"], -1)
                        pe.matmul(ps[2 + i][:, 0:B], self.c("anti"), xs[i][:, B:2 * B], start=True, stop=True).then_inc(S2["e_ps"], 1)

                @block.vector
                def _(v):
                    def own(i):
                        i.then_inc(T["dve"], 1)
                        v.wait_ge(T["dve"], 1)
                        v.sem_inc(T["dve"], -1)
                    v.tensor_copy(dcomp[0][:].rearrange("p (u c) -> p u c", c=2), places(state, 0, 2, P))
                    v.tensor_copy(dcomp[1][:].rearrange("p (u c) -> p u c", c=2),
                                  state[:, 0:4 * P].rearrange("p (u c) -> p u c", c=8)[:, :, 1:6:4]).then_inc(S2["state_split"], 1)
                    for i in range(2):
                        v.wait_ge(S2["state_T"], 1)
                        v.sem_inc(S2["state_T"], -1)
                        v.tensor_copy(xs[i][:], ps[i][:, 0:P]).then_inc(S2["state_in"], 1)
                    re, im, n, t = (f[:] for f in fin)
                    v.wait_ge(S2["e_ps"], 1)
                    v.sem_inc(S2["e_ps"], -1)
                    own(v.tensor_tensor(re, ps[2][:, 0:B], xs[0][:, 0:B], ALU.add))
                    own(v.tensor_tensor(re, re, vclip[:], ALU.subtract))
                    own(v.tensor_scalar(re, re, 2.0, None, ALU.add))
                    v.wait_ge(S2["e_ps"], 1)
                    v.sem_inc(S2["e_ps"], -1)
                    own(v.tensor_tensor(im, ps[3][:, 0:B], xs[1][:, 0:B], ALU.add))
                    own(v.tensor_scalar(im, im, 1.0, None, ALU.add))
                    own(v.tensor_tensor(n, re, re, ALU.mult))
                    own(v.tensor_tensor(t, im, im, ALU.mult))
                    own(v.tensor_tensor(n, n, t, ALU.add))
                    own(v.reciprocal(t, n))
                    own(v.tensor_tensor(re, re, t, ALU.mult))
                    own(v.tensor_scalar(im, im, -1.0, None, ALU.mult))
                    own(v.tensor_tensor(im, im, t, ALU.mult))
                    f3 = self.feats[:].rearrange("p (b c) -> p b c", c=11)
                    v.tensor_scalar(f3[:, :, 8], re, -FEAT_CLAMP, FEAT_CLAMP, ALU.max, ALU.min)
                    own(v.tensor_scalar(f3[:, :, 9], im, -FEAT_CLAMP, FEAT_CLAMP, ALU.max, ALU.min))
                    own(v.tensor_tensor(self.mixrows[:], self.mixrows[:], self.mixscale[:], ALU.mult))

    def differential_attention(self):
        nc, ins, ps, h, T = self.nc, self.ins, self.ps, self.h, self.S
        with ExitStack() as ctx:
            def sb(name, shape, dt=F32):
                return ctx.enter_context(nc.sbuf_tensor(name, shape, dt))
            idx = [sb(f"idx{i}", [P, 1], I32) for i in range(2)]
            yrow = [sb(f"yrow{i}", [P, D]) for i in range(2)]
            w2s = sb("c_w2s", [P, 2])
            fcur = sb("fcur", [P, 11])
            fT = sb("fT", [11, P])
            y = sb("c_y", [P, D])
            yT = sb("c_yT", [DH + 1, 2 * P])
            qT, kT = sb("c_qT", [P, F]), sb("c_kT", [P, F])
            vv = sb("c_v", [P, D])
            sc = sb("sc", [P, NSUB * P])
            nmax, sums, rs = sb("c_nmax", [P, NSUB]), sb("c_sums", [P, NSUB]), sb("c_rs", [P, NSUB])
            diff = sb("diff", [P, H1 * P])
            diffT = sb("diffT", [P, H1 * P])
            cx, cx2 = sb("cx", [P, D]), sb("cx2", [P, D])
            cxT = sb("cxT", [DH + 1, 2 * P])
            ms, rr = sb("ms", [P, H1]), sb("rr", [P, H1])
            lam = sb("lam", [P, 8])
            ljunk = sb("ljunk", [P, HS])
            S = self.sems(ctx, "lam_in", "lam_e", "y_in", "y_read", "rows_free", "f_free", "f_ready", "fT_ps", "fT_in", "f_ps",
                          "y_ready", "y_free", "yT_ps", "yT_in", "q_ps", "q_in", "k_ps", "k_in", "v_ps", "v_in",
                          "s_ps", "clamped", "nmax", "exp_done", "odd_ready", "odd_scaled", "diff_ready", "dT_ps", "dT_in",
                          "ctx_ps", "ms_ready", "rr_ready", "cx_ready", "cxT_ps", "cxT_in", "o_ps", "o_free", "fcur_free")
            block = ctx.enter_context(nc.Block())

            @block.gpsimd
            def _(g):
                def gather(b, first=False):
                    if not first:
                        g.wait_ge(S["rows_free"], 1)
                        g.sem_inc(S["rows_free"], -1)
                    for i in range(2):
                        g.tensor_copy(idx[i][:], self.yrows[:, bass.ds(2 * b + i, 1)]).then_inc(T["pool"], 1)
                        g.wait_ge(T["pool"], 1)
                        g.sem_inc(T["pool"], -1)
                        g.indirect_dma_start(out=yrow[i][:], out_offset=None, in_=self.yslots,
                                             in_offset=bass.IndirectOffsetOnAxis(ap=idx[i][:, 0:1], axis=0)).then_inc(S["y_in"], 16)

                def norm():
                    inverse_root(g, self.ln, T, self.c("eps5"), self.c("neg_half"))

                def scale_odd(r):
                    g.wait_ge(S["odd_ready"], 1)
                    g.sem_inc(S["odd_ready"], -1)
                    o = sc[:].rearrange("p (h e t) -> p e h t", e=2, t=P)[:, 1, 6 * r:6 * r + 6, :]
                    c_ = rs[:].rearrange("p (h e) -> p e h", e=2)[:, 1, 6 * r:6 * r + 6]
                    g.tensor_tensor(o, o, c_.unsqueeze(2).to_broadcast([P, 6, P]), ALU.mult).then_inc(S["odd_scaled"], 1)

                def rms():
                    g.wait_ge(S["ms_ready"], 1)
                    g.sem_inc(S["ms_ready"], -1)
                    g.tensor_tensor(rr[:], ms[:], self.c("neg_half").to_broadcast([P, H1]), ALU.pow).then_inc(S["rr_ready"], 1)

                gather(0, True)
                gather(1)
                norm()
                gather(2)
                norm()

                def step(b, prev, cur, two, three):
                    if prev:
                        rms()
                    if cur:
                        scale_odd(0)
                    if two:
                        norm()
                    if cur:
                        scale_odd(1)
                    if three:
                        gather(b + 3)
                step(0, False, True, True, True)
                with g.Fori(1, B - 3) as b:
                    step(b, True, True, True, True)
                step(B - 3, True, True, True, False)
                step(B - 2, True, True, False, False)
                step(B - 1, True, True, False, False)
                step(B, True, False, False, False)

            @block.scalar
            def _(act):
                act.wait_ge(S["lam_in"], 1)
                act.sem_inc(S["lam_in"], -1)
                act.activation(lam[:, 2:4], lam[:, 0:2], ACT.Exp).then_inc(S["lam_e"], 1)

                def fT_evac():
                    act.wait_ge(S["fT_ps"], 1)
                    act.sem_inc(S["fT_ps"], -1)
                    act.activation(fT[:], ps[2][0:11, 0:P], ACT.Copy).then_inc(S["fT_in"], 1)

                def yT_evac():
                    act.wait_ge(S["yT_ps"], 1)
                    act.sem_inc(S["yT_ps"], -1)
                    act.activation(yT[0:DH, :], ps[7][0:DH, 2 * P:4 * P], ACT.Copy).then_inc(S["yT_in"], 1)

                def kq_evac():
                    act.wait_ge(S["k_ps"], 1)
                    act.sem_inc(S["k_ps"], -1)
                    act.activation(kT[:, 0:4 * P], ps[6][:], ACT.Copy)
                    act.activation(kT[:, 4 * P:6 * P], ps[7][:, 0:2 * P], ACT.Copy).then_inc(S["k_in"], 1)
                    act.wait_ge(S["q_ps"], 1)
                    act.sem_inc(S["q_ps"], -1)
                    act.activation(qT[:, 0:4 * P], ps[4][:], ACT.Copy, scale=HS ** -0.5)
                    act.activation(qT[:, 4 * P:6 * P], ps[5][:, 0:2 * P], ACT.Copy, scale=HS ** -0.5).then_inc(S["q_in"], 1)

                def exps():
                    for r in range(2):
                        act.wait_ge(S["nmax"], 1)
                        act.sem_inc(S["nmax"], -1)
                        for s in range(12 * r, 12 * r + 12):
                            last = act.activation(sc[:, P * s:P * s + P], sc[:, P * s:P * s + P], ACT.Exp,
                                                  bias=nmax[:, s:s + 1], accum_out=sums[:, s:s + 1])
                        last.then_inc(S["exp_done"], 1)

                def dT_evac():
                    for r in range(2):
                        act.wait_ge(S["dT_ps"], 1)
                        act.sem_inc(S["dT_ps"], -1)
                        a = 6 * r
                        act.activation(diffT[:, P * a:P * (a + 4)], ps[4 + 2 * r][:], ACT.Copy)
                        act.activation(diffT[:, P * (a + 4):P * (a + 6)], ps[5 + 2 * r][:, 0:2 * P], ACT.Copy).then_inc(S["dT_in"], 1)

                def cxT_evac():
                    act.wait_ge(S["cxT_ps"], 1)
                    act.sem_inc(S["cxT_ps"], -1)
                    act.activation(cxT[0:DH, :], ps[3][0:DH, 0:2 * P], ACT.Copy).then_inc(S["cxT_in"], 1)

                fT_evac()
                yT_evac()
                kq_evac()
                fT_evac()

                def step(prev, cur, one, two):
                    if prev:
                        dT_evac()
                    if one:
                        yT_evac()
                    if cur:
                        exps()
                    if one:
                        kq_evac()
                    if two:
                        fT_evac()
                    if prev:
                        cxT_evac()
                step(False, True, True, True)
                with act.Fori(1, B - 2) as _b:
                    step(True, True, True, True)
                step(True, True, True, False)
                step(True, True, False, False)
                step(True, False, False, False)

            @block.vector
            def _(v):
                def own(i):
                    i.then_inc(T["dve"], 1)
                    v.wait_ge(T["dve"], 1)
                    v.sem_inc(T["dve"], -1)

                v.memset(yT[DH:DH + 1, :], 1.0)
                v.memset(cxT[DH:DH + 1, :], 1.0)
                lr = self.r("lam")
                for i in range(2):
                    own(v.tensor_tensor_reduce(out=ljunk[:], in0=lr[:, 16 * i:16 * i + 8], in1=lr[:, 16 * i + 8:16 * i + 16], scale=1.0,
                                               scalar=0.0, op0=ALU.mult, op1=ALU.add, accum_out=lam[:, i:i + 1]))
                v.sem_inc(S["lam_in"], 1)
                own(v.tensor_scalar(self.r("subln"), self.r("subln"), 1.0 - LAMBDA_INIT, None, ALU.mult))
                v.wait_ge(S["lam_e"], 1)
                v.sem_inc(S["lam_e"], -1)
                own(v.tensor_tensor(lam[:, 4:5], lam[:, 3:4], lam[:, 2:3], ALU.subtract))
                own(v.tensor_scalar(lam[:, 5:6], lam[:, 4:5], -LAMBDA_INIT, None, ALU.add))

                def mix(b, first=False):
                    hb = h[:, bass.ds(b * D, D)]
                    if not first:
                        v.wait_ge(S["fcur_free"], 1)
                        v.sem_inc(S["fcur_free"], -1)
                    own(v.tensor_copy(w2s[:], self.mixw[:, bass.ds(2 * b, 2)]))
                    v.tensor_copy(fcur[:], self.feats[:, bass.ds(11 * b, 11)]).then_inc(S["f_ready"], 1)
                    v.wait_ge(S["y_in"], 32 * (b + 1))
                    own(v.tensor_copy(cx2[:, 0:1], w2s[:, 0:1]))
                    for i in range(2):
                        own(v.scalar_tensor_tensor(out=hb, in0=yrow[i][:], scalar=w2s[:, i:i + 1], in1=hb, op0=ALU.mult, op1=ALU.add))
                    v.sem_inc(S["rows_free"], 1)

                def add_spectral(b):
                    hb = h[:, bass.ds(b * D, D)]
                    v.wait_ge(S["f_ps"], 1)
                    v.sem_inc(S["f_ps"], -1)
                    own(v.tensor_tensor(hb, hb, ps[2][:, 0:D], ALU.add))
                    v.sem_inc(S["f_free"], 1)
                    norm_statistics(v, self.ln, T, hb)

                def make_y(b, first=False):
                    if not first:
                        v.wait_ge(S["y_free"], 1)
                        v.sem_inc(S["y_free"], -1)
                    norm_apply(v, self.ln, T, h[:, bass.ds(b * D, D)], y[:], S["y_ready"])

                def v_evac():
                    v.wait_ge(S["v_ps"], 1)
                    v.sem_inc(S["v_ps"], -1)
                    v.tensor_copy(vv[:], ps[5][:, 2 * P:2 * P + D]).then_inc(S["v_in"], 1)

                def softmax_front():
                    for r in range(2):
                        o = sc[:, 12 * P * r:12 * P * (r + 1)].rearrange("p (m r t) -> p r m t", r=4, t=P)
                        for q in range(4):
                            v.wait_ge(S["s_ps"], 1)
                            v.sem_inc(S["s_ps"], -1)
                            v.tensor_scalar(o[:, q], ps[q][:, 0:3 * P].rearrange("p (m t) -> p m t", t=P), -BIG, BIG,
                                            ALU.max, ALU.min).then_inc(S["clamped"], 1)
                        own(v.tensor_copy(ljunk[:, 0:1], lam[:, 5:6]))
                        v.tensor_reduce(out=nmax[:, 12 * r:12 * r + 12],
                                        in_=sc[:, 12 * P * r:12 * P * (r + 1)].rearrange("p (s t) -> p s t", t=P),
                                        op=ALU.max, axis=AX, negate=True).then_inc(S["nmax"], 1)

                def odd_scales(r):
                    v.wait_ge(S["exp_done"], 1)
                    v.sem_inc(S["exp_done"], -1)
                    own(v.reciprocal(rs[:, 12 * r:12 * r + 12], sums[:, 12 * r:12 * r + 12]))
                    odd = rs[:].rearrange("p (h e) -> p e h", e=2)[:, 1, 6 * r:6 * r + 6]
                    v.tensor_scalar(odd, odd, lam[:, 5:6], None, ALU.mult).then_inc(S["odd_ready"], 1)

                def differences(r):
                    v.wait_ge(S["odd_scaled"], 1)
                    v.sem_inc(S["odd_scaled"], -1)
                    for n in range(6 * r, 6 * r + 6):
                        s = 2 * n
                        last = v.scalar_tensor_tensor(out=diff[:, P * n:P * n + P], in0=sc[:, P * s:P * s + P],
                                                      scalar=rs[:, s:s + 1], in1=sc[:, P * (s + 1):P * (s + 2)],
                                                      op0=ALU.mult, op1=ALU.add)
                    own(last)
                    v.sem_inc(S["diff_ready"], 1)

                def mean_squares(cur):
                    v.wait_ge(S["ctx_ps"], 1)
                    v.sem_inc(S["ctx_ps"], -1)
                    own(v.tensor_copy(cx[:], ps[0][:, 0:D]))
                    if cur:
                        v_evac()
                    own(v.tensor_tensor(cx2[:], cx[:], cx[:], ALU.mult))
                    own(v.tensor_reduce(out=ms[:], in_=cx2[:].rearrange("p (h d) -> p h d", d=HV), op=ALU.add, axis=AX))
                    v.tensor_scalar(ms[:], ms[:], 1.0 / HV, 1e-5, ALU.mult, ALU.add).then_inc(S["ms_ready"], 1)

                def scale_context():
                    v.wait_ge(S["rr_ready"], 1)
                    v.sem_inc(S["rr_ready"], -1)
                    c3 = cx[:].rearrange("p (h d) -> p h d", d=HV)
                    own(v.tensor_tensor(c3, c3, rr[:].unsqueeze(2).to_broadcast([P, H1, HV]), ALU.mult))
                    v.tensor_tensor(cx[:], cx[:], self.r("subln"), ALU.mult).then_inc(S["cx_ready"], 1)

                def add_out(b):
                    hb = h[:, bass.ds(b * D, D)]
                    v.wait_ge(S["o_ps"], 1)
                    v.sem_inc(S["o_ps"], -1)
                    own(v.tensor_tensor(hb, hb, ps[3][:, 0:D], ALU.add))
                    v.sem_inc(S["o_free"], 1)

                mix(0, first=True)
                add_spectral(0)
                make_y(0, first=True)
                mix(1)
                add_spectral(1)
                make_y(1)

                def step(b, prev, cur, two):
                    if cur:
                        softmax_front()
                    if prev:
                        mean_squares(cur)
                    elif cur:
                        v_evac()
                    if two:
                        mix(b + 2)
                    if prev:
                        scale_context()
                    if cur:
                        odd_scales(0)
                    if two:
                        add_spectral(b + 2)
                    if cur:
                        odd_scales(1)
                    if two:
                        make_y(b + 2)
                    if cur:
                        differences(0)
                    if prev:
                        add_out(b - 1)
                    if cur:
                        differences(1)
                step(0, False, True, True)
                with v.Fori(1, B - 2) as b:
                    step(b, True, True, True)
                step(B - 2, True, True, False)
                step(B - 1, True, True, False)
                step(B, True, False, False)

            @block.tensor
            def _(pe):
                def features_T():
                    pe.wait_ge(S["f_ready"], 1)
                    pe.sem_inc(S["f_ready"], -1)
                    pe.transpose(ps[2][0:11, 0:P], fcur[:], self.c("ident")).then_inc(S["fT_ps"], 1)

                def features():
                    pe.wait_ge(S["fT_in"], 1)
                    pe.sem_inc(S["fT_in"], -1)
                    pe.sem_inc(S["fcur_free"], 1)
                    pe.matmul(ps[2][:, 0:D], fT[:], self.mixrows[:], start=True, stop=True).then_inc(S["f_ps"], 1)

                def y_T():
                    pe.wait_ge(S["y_ready"], 1)
                    pe.sem_inc(S["y_ready"], -1)
                    for c in range(2):
                        last = pe.transpose(ps[7][0:DH, P * (2 + c):P * (3 + c)], y[:, DH * c:DH * c + DH], self.c("ident"))
                    last.then_inc(S["yT_ps"], 1)

                def kq_proj(before_q=None):
                    pe.wait_ge(S["yT_in"], 1)
                    pe.sem_inc(S["yT_in"], -1)
                    pe.sem_inc(S["y_free"], 1)
                    for which, bank, ready in ((1, 6, "k_ps"), (0, 4, "q_ps")):
                        if which == 0 and before_q:
                            before_q()
                        for m in range(MT):
                            for c in range(2):
                                k = DH + c
                                a = which * 2 * F + c * F + m * P
                                last = pe.matmul(ps[bank + m // 4][:, P * (m % 4):P * (m % 4) + P], self.w_qk[0:k, a:a + P],
                                                 yT[0:k, P * c:P * c + P], start=(c == 0), stop=(c == 1))
                        last.then_inc(S[ready], 1)

                def v_proj():
                    for c in range(2):
                        k = DH + c
                        last = pe.matmul(ps[5][:, 2 * P:2 * P + D], yT[0:k, P * c:P * c + P], self.w_vo[0:k, c * D:c * D + D],
                                         start=(c == 0), stop=(c == 1))
                    last.then_inc(S["v_ps"], 1)

                def scores(r, q):
                    for m in range(3):
                        t = 3 * r + m
                        last = pe.matmul(ps[q][:, P * m:P * m + P], qT[32 * q:32 * q + HS, P * t:P * t + P],
                                         kT[32 * q:32 * q + HS, P * t:P * t + P], start=True, stop=True)
                    last.then_inc(S["s_ps"], 1)

                def diff_T(r):
                    pe.wait_ge(S["diff_ready"], 1)
                    pe.sem_inc(S["diff_ready"], -1)
                    for k in range(6):
                        n = 6 * r + k
                        last = pe.transpose(ps[4 + 2 * r + k // 4][:, P * (k % 4):P * (k % 4) + P],
                                            diff[:, P * n:P * n + P], self.c("ident"))
                    last.then_inc(S["dT_ps"], 1)

                def contexts():
                    for r in range(2):
                        pe.wait_ge(S["dT_in"], 1)
                        pe.sem_inc(S["dT_in"], -1)
                        for k in range(6):
                            n = 6 * r + k
                            last = pe.matmul(ps[0][:, HV * n:HV * n + HV], diffT[:, P * n:P * n + P], vv[:, HV * n:HV * n + HV],
                                             start=True, stop=True)
                    last.then_inc(S["ctx_ps"], 1)

                def context_T():
                    pe.wait_ge(S["cx_ready"], 1)
                    pe.sem_inc(S["cx_ready"], -1)
                    for c in range(2):
                        last = pe.transpose(ps[3][0:DH, P * c:P * c + P], cx[:, DH * c:DH * c + DH], self.c("ident"))
                    last.then_inc(S["cxT_ps"], 1)

                def out_proj():
                    pe.wait_ge(S["cxT_in"], 1)
                    pe.sem_inc(S["cxT_in"], -1)
                    for c in range(2):
                        k = DH + c
                        last = pe.matmul(ps[3][:, 0:D], cxT[0:k, P * c:P * c + P], self.w_vo[0:k, 2 * D + c * D:2 * D + c * D + D],
                                         start=(c == 0), stop=(c == 1))
                    last.then_inc(S["o_ps"], 1)

                features_T()
                features()
                y_T()
                kq_proj()
                pe.wait_ge(S["f_free"], 1)
                pe.sem_inc(S["f_free"], -1)
                features_T()
                features()

                def step(prev, cur, one, two, second=False, spectral=True):
                    if cur:
                        pe.wait_ge(S["k_in"], 1)
                        pe.sem_inc(S["k_in"], -1)
                        pe.wait_ge(S["q_in"], 1)
                        pe.sem_inc(S["q_in"], -1)
                        for q in range(4):
                            if q == 2 and spectral:
                                pe.wait_ge(S["f_free"], 1)
                                pe.sem_inc(S["f_free"], -1)
                            if q == 3 and prev and not second:
                                pe.wait_ge(S["o_free"], 1)
                                pe.sem_inc(S["o_free"], -1)
                            scores(0, q)
                        v_proj()
                    if prev:
                        diff_T(0)
                    if one:
                        y_T()
                    if prev:
                        diff_T(1)
                    if cur:
                        for q in range(4):
                            pe.wait_ge(S["clamped"], 1)
                            pe.sem_inc(S["clamped"], -1)
                            scores(1, q)
                        pe.wait_ge(S["clamped"], 1)
                        pe.sem_inc(S["clamped"], -1)
                    if prev:
                        contexts()

                    def v_read():
                        pe.wait_ge(S["v_in"], 1)
                        pe.sem_inc(S["v_in"], -1)
                    if one:
                        kq_proj(before_q=v_read)
                    elif cur:
                        v_read()
                    if cur:
                        pe.wait_ge(S["clamped"], 3)
                        pe.sem_inc(S["clamped"], -3)
                    if two:
                        features_T()
                    if prev:
                        if not cur:
                            pe.wait_ge(S["o_free"], 1)
                            pe.sem_inc(S["o_free"], -1)
                        context_T()
                    if two:
                        features()
                    if prev:
                        out_proj()
                step(False, True, True, True)
                step(True, True, True, True, second=True)
                with pe.Fori(2, B - 2) as _b:
                    step(True, True, True, True)
                step(True, True, True, False)
                step(True, True, False, False, spectral=False)
                step(True, False, False, False)
                pe.wait_ge(S["o_free"], 1)
                pe.sem_inc(S["o_free"], -1)

    def feed_forward(self):
        nc, ins, ps, h, T = self.nc, self.ins, self.ps, self.h, self.S
        NG, W = B // GRP, GRP * P
        with ExitStack() as ctx:
            def sb(name, shape, dt=F32):
                return ctx.enter_context(nc.sbuf_tensor(name, shape, dt))
            a2 = sb("a2", [P, 5 * MT * D])
            gates_w = sb("gates_w", [DH, 2 * 2 * NCLS])
            z4 = sb("z4", [P, GRP * D])
            zT = sb("d_zT", [DH + 1, 2 * W])
            zc = sb("zc", [DH + 1, 2 * NCLS * B])
            hT = sb("d_hT", [P, MT * W])
            ob = sb("ob", [P, GRP * D])
            hc = sb("hc", [B, NCLS * D])
            hcT = [sb(f"hcT{i}", [P, MT * B]) for i in range(2)]
            gt = [sb(f"gt{i}", [B, 2 * NCLS]) for i in range(3)]
            g6 = [sb(f"g6_{i}", [B, NCLS]) for i in range(3)]
            eo = sb("eo", [B, D])
            S = self.sems(ctx, "cls_loaded", "gelu_warm", "z_ready", "z_free", "zT_ps", "zT_in", "zT_free", "h_ps", "h_in", "y_ps", "y_in",
                          "ob_ready", "ob_out", "hc_in", "gates_ps", "gates_m", "gates_e", "zc_ready", "u_ps", "u_in", "e_ps", "e_free", "cls_done")

            with nc.Block() as block:
                @block.sync
                def _(sp):
                    sp.dma_start(self.w1[:, 0:5 * 2 * F], ins["a1"]).then_inc(S["cls_loaded"], 16)
                    sp.dma_start(a2[:], ins["a2"]).then_inc(S["cls_loaded"], 16)
                    sp.dma_start(gates_w[:], ins["gates_w"]).then_inc(S["cls_loaded"], 16)
                    for i in range(NCLS):
                        sp.dma_start(hc[:, D * i:D * i + D], h[i:i + 1, :].rearrange("o (b d) -> o b d", d=D)).then_inc(S["hc_in"], 16)
                    o = ob[NCLS:P, :].rearrange("p (b d) -> p b d", d=D)
                    with sp.Fori(0, NG) as g:
                        sp.wait_ge(S["ob_ready"], 1)
                        sp.sem_inc(S["ob_ready"], -1)
                        sp.dma_start(self.out[bass.ds(GRP * g, GRP), NCLS:P, :].rearrange("b s d -> s b d"), o).then_inc(S["ob_out"], 16)
                    sp.wait_ge(S["cls_done"], 1)
                    sp.sem_inc(S["cls_done"], -1)
                    sp.wait_ge(S["ob_out"], 16)
                    sp.sem_inc(S["ob_out"], -16)
                    sp.dma_start(self.out[:, 0:NCLS, :], hc[:].rearrange("p (i d) -> p i d", d=D)).then_inc(S["ob_out"], 16)
                    sp.wait_ge(S["ob_out"], 16)
                    sp.sem_inc(S["ob_out"], -16)

                @block.gpsimd
                def _(g):
                    with g.Fori(0, B) as _b:
                        inverse_root(g, self.ln, T, self.c("eps5"), self.c("neg_half"))

                @block.scalar
                def _(act):
                    act.activation(gt[2][:, 0:1], self.c("ones", slice(0, B))[:, 0:1], ACT.Gelu).then_inc(S["gelu_warm"], 1)
                    act.wait_ge(S["gelu_warm"], 1)

                    def group():
                        act.wait_ge(S["zT_ps"], 1)
                        act.sem_inc(S["zT_ps"], -1)
                        for c in range(2):
                            last = act.activation(zT[0:DH, W * c:W * c + W], ps[c][0:DH, :], ACT.Copy)
                        last.then_inc(S["zT_in"], 1)

                    def gelus():
                        for m in range(MT):
                            act.wait_ge(S["h_ps"], 1)
                            act.sem_inc(S["h_ps"], -1)
                            act.activation(hT[:, W * m:W * m + W], ps[2 + (m + 2) % MT][:], ACT.Gelu).then_inc(S["h_in"], 1)
                    group()
                    with act.Fori(0, NG - 1) as _g:
                        gelus()
                        group()
                    gelus()
                    act.wait_ge(S["gates_m"], 1)
                    act.sem_inc(S["gates_m"], -1)
                    act.activation(gt[1][:], gt[0][:], ACT.Exp).then_inc(S["gates_e"], 1)
                    for n in range(2 * NCLS):
                        act.wait_ge(S["u_ps"], 1)
                        act.sem_inc(S["u_ps"], -1)
                        act.activation(hcT[n % 2][:], ps[4 + n % 2][:, 0:MT * B], ACT.Gelu).then_inc(S["u_in"], 1)

                @block.vector
                def _(v):
                    def own(i):
                        i.then_inc(T["dve"], 1)
                        v.wait_ge(T["dve"], 1)
                        v.sem_inc(T["dve"], -1)
                    for c in range(2):
                        v.memset(zT[DH:DH + 1, W * c:W * c + W], 1.0)
                    v.memset(zc[DH:DH + 1, :], 1.0)

                    def norms(g):
                        for j in range(GRP):
                            layer_norm(v, self.ln, T, h[:, bass.ds((GRP * g + j) * D, D)], z4[:, D * j:D * j + D], S["z_ready"])

                    def keep_class_tokens(g):
                        v.wait_ge(S["zT_free"], 1)
                        v.sem_inc(S["zT_free"], -1)
                        z3 = zT[0:DH, :].rearrange("p (c b t) -> p c b t", c=2, t=P)
                        zc3 = zc[0:DH, :].rearrange("p (b c i) -> p b c i", c=2, i=NCLS)
                        for c in range(2):
                            last = v.tensor_copy(zc3[:, bass.ds(GRP * g, GRP), c, :], z3[:, c, :, 0:NCLS])
                        last.then_inc(S["zc_ready"], 1)

                    def outputs(g, first=False):
                        for j in range(GRP):
                            if j % 2 == 0:
                                v.wait_ge(S["y_ps"], 1)
                                v.sem_inc(S["y_ps"], -1)
                            if j == 0 and not first:
                                v.wait_ge(S["ob_out"], 16)
                                v.sem_inc(S["ob_out"], -16)
                            o = ob[:, D * j:D * j + D]
                            own(v.tensor_tensor(o, ps[2 + j // 2][:, D * (j % 2):D * (j % 2) + D], self.r("moe0_b2"), ALU.add))
                            i = v.tensor_tensor(o, o, h[:, bass.ds((GRP * g + j) * D, D)], ALU.add)
                            if j % 2:
                                own(i)
                                v.sem_inc(S["y_in"], 1)
                        v.sem_inc(S["ob_ready"], 1)
                    norms(0)
                    keep_class_tokens(0)
                    v.wait_ge(S["z_free"], 1)
                    v.sem_inc(S["z_free"], -1)
                    norms(1)
                    keep_class_tokens(1)
                    outputs(0, first=True)
                    with v.Fori(1, NG - 1) as g:
                        v.wait_ge(S["z_free"], 1)
                        v.sem_inc(S["z_free"], -1)
                        norms(g + 1)
                        keep_class_tokens(g + 1)
                        outputs(g)
                    outputs(NG - 1)
                    l3, e3, m3 = (t[:].rearrange("p (i k) -> p i k", k=2) for t in gt)
                    mx, den, inv = (t[:] for t in g6)

                    def wide(a):
                        return a.unsqueeze(2).to_broadcast([B, NCLS, 2])
                    v.wait_ge(S["gates_ps"], 1)
                    v.sem_inc(S["gates_ps"], -1)
                    own(v.tensor_copy(gt[0][:], ps[0][0:B, 0:2 * NCLS]))
                    own(v.tensor_reduce(out=mx, in_=l3, op=ALU.max, axis=AX))
                    v.tensor_tensor(l3, l3, wide(mx), ALU.subtract).then_inc(S["gates_m"], 1)
                    v.wait_ge(S["gates_e"], 1)
                    v.sem_inc(S["gates_e"], -1)
                    own(v.tensor_reduce(out=den, in_=e3, op=ALU.add, axis=AX))
                    own(v.reciprocal(inv, den))
                    own(v.tensor_tensor(e3, e3, wide(inv), ALU.mult))
                    own(v.tensor_reduce(out=mx, in_=e3, op=ALU.min, axis=AX))
                    own(v.tensor_tensor(m3, e3, wide(mx), ALU.is_gt))
                    own(v.tensor_tensor(e3, e3, m3, ALU.mult))
                    own(v.tensor_reduce(out=den, in_=e3, op=ALU.add, axis=AX))
                    own(v.tensor_scalar(den, den, 1e-6, None, ALU.max))
                    own(v.reciprocal(inv, den))
                    own(v.tensor_tensor(e3, e3, wide(inv), ALU.mult))
                    v.wait_ge(S["hc_in"], 16 * NCLS)
                    for n in range(2 * NCLS):
                        i, k = n // 2, n % 2
                        c = CLS_PAIRS[i][k][1]
                        v.wait_ge(S["e_ps"], 1)
                        v.sem_inc(S["e_ps"], -1)
                        own(v.tensor_tensor(eo[:], ps[6 + n % 2][0:B, 0:D], self.r("a2_b")[0:B, D * c:D * c + D], ALU.add))
                        v.sem_inc(S["e_free"], 1)
                        hi = hc[:, D * i:D * i + D]
                        own(v.scalar_tensor_tensor(out=hi, in0=eo[:], scalar=gt[1][:, n:n + 1], in1=hi, op0=ALU.mult, op1=ALU.add))
                    v.sem_inc(S["cls_done"], 1)

                @block.tensor
                def _(pe):
                    ident = self.c("ident")

                    def turn():
                        pe.wait_ge(S["z_ready"], GRP)
                        pe.sem_inc(S["z_ready"], -GRP)
                        for c in range(2):
                            for j in range(GRP):
                                last = pe.transpose(ps[c][0:DH, P * j:P * j + P], z4[:, D * j + DH * c:D * j + DH * c + DH], ident)
                        last.then_inc(S["zT_ps"], 1)

                    def up(first=False):
                        for m in range(MT):
                            if not first and m == MT - 2:
                                pe.wait_ge(S["y_in"], 2)
                                pe.sem_inc(S["y_in"], -2)
                            for c in range(2):
                                k = DH + c
                                last = pe.matmul(ps[2 + (m + 2) % MT][:], self.w_up[0:k, c * F + m * P:c * F + m * P + P],
                                                 zT[0:k, W * c:W * c + W], start=(c == 0), stop=(c == 1))
                            last.then_inc(S["h_ps"], 1)

                    def turned():
                        pe.wait_ge(S["zT_in"], 1)
                        pe.sem_inc(S["zT_in"], -1)
                        pe.sem_inc(S["z_free"], 1)
                        pe.sem_inc(S["zT_free"], 1)

                    def down():
                        for j in range(GRP):
                            for m in range(MT):
                                last = pe.matmul(ps[2 + j // 2][:, D * (j % 2):D * (j % 2) + D], hT[:, W * m + P * j:W * m + P * j + P],
                                                 self.w_down[:, D * m:D * m + D], start=(m == 0), stop=(m == MT - 1))
                            if j % 2:
                                last.then_inc(S["y_ps"], 1)

                    turn()
                    turned()
                    up(first=True)

                    def step(more=True):
                        if more:
                            pe.wait_ge(S["zc_ready"], 1)
                            pe.sem_inc(S["zc_ready"], -1)
                            turn()
                        pe.wait_ge(S["h_in"], MT)
                        pe.sem_inc(S["h_in"], -MT)
                        down()
                        if more:
                            turned()
                            up()
                    with pe.Fori(0, NG - 1) as _g:
                        step()
                    step(more=False)
                    pe.wait_ge(S["cls_loaded"], 48)
                    pe.wait_ge(S["zc_ready"], 1)
                    pe.sem_inc(S["zc_ready"], -1)
                    zc3 = zc[:].rearrange("p (b c i) -> p c i b", c=2, i=NCLS)
                    for i in range(NCLS):
                        for c in range(2):
                            last = pe.matmul(ps[0][0:B, 2 * i:2 * i + 2], zc3[0:DH, c, i], gates_w[:, 2 * NCLS * c + 2 * i:2 * NCLS * c + 2 * i + 2],
                                             start=(c == 0), stop=(c == 1))
                    last.then_inc(S["gates_ps"], 1)

                    def cls_up(n):
                        a = CLS_PAIRS[n // 2][n % 2][0]
                        for m in range(MT):
                            for c in range(2):
                                k = DH + c
                                w = 2 * F * a + c * F + m * P
                                last = pe.matmul(ps[4 + n % 2][:, B * m:B * m + B], self.w1[0:k, w:w + P], zc3[0:k, c, n // 2],
                                                 start=(c == 0), stop=(c == 1))
                        last.then_inc(S["u_ps"], 1)

                    def cls_down(n):
                        c = CLS_PAIRS[n // 2][n % 2][1]
                        pe.wait_ge(S["u_in"], 1)
                        pe.sem_inc(S["u_in"], -1)
                        if n >= 2:
                            pe.wait_ge(S["e_free"], 1)
                            pe.sem_inc(S["e_free"], -1)
                        for m in range(MT):
                            last = pe.matmul(ps[6 + n % 2][0:B, 0:D], hcT[n % 2][:, B * m:B * m + B],
                                             a2[:, MT * D * c + D * m:MT * D * c + D * m + D], start=(m == 0), stop=(m == MT - 1))
                        last.then_inc(S["e_ps"], 1)
                    cls_up(0)
                    for n in range(2 * NCLS):
                        if n + 1 < 2 * NCLS:
                            cls_up(n + 1)
                        cls_down(n)



def _halves(w, bias=None):
    import numpy as np
    n = w.shape[1]
    o = np.zeros((DH + 1, 2, n), np.float32)
    o[:DH, 0], o[:DH, 1] = w[:DH], w[DH:]
    if bias is not None:
        o[DH, 1] = bias
    return o


def _relation_tables(tv, th):
    import numpy as np
    o = np.zeros((NGV + NGH, 24, tv.shape[1]), np.float32)
    for g in range(NGV):
        for r in range(NV):
            o[g, r] = tv[r - g + 15] if g < NV else tv[0]
        o[g, 23] = tv[0]
    for g in range(NGH):
        for r in range(SIDE):
            o[NGV + g, NV + r] = th[r - g + 15] if g < SIDE else th[0]
        o[NGV + g, 23] = th[0]
    return o


def _constants():
    import numpy as np
    o = np.zeros((P, NCONST), np.float32)

    def put(name, a):
        at, w = CONSTS[name]
        o[:a.shape[0], at:at + w] = a
    put("ident", np.eye(P))
    put("anti", np.eye(P)[::-1])
    put("tri", np.triu(np.ones((P, P)), 1))
    put("ones", np.ones((P, P)))
    j = np.arange(1, P)
    place = np.zeros((24, P))
    place[(j - 1) // SIDE, j] = 1
    place[NV + (j - 1) % SIDE, j] = 1
    place[23, 0] = 1
    ohk = np.zeros((P, P))
    ohk[64:88] = place
    put("ohk", ohk)
    put("ohv", np.concatenate([place.T, np.zeros((P, 8))], 1))
    put("iota8", np.tile(np.arange(8.0), (P, 1)))
    put("ebase", np.tile(np.arange(8.0) * CAP, (P, 1)))
    put("step128", np.tile(P * np.arange(float(TILES)), (P, 1)))
    put("neg_half", np.full((P, 1), -0.5))
    put("eps12", np.full((P, 1), 1e-12))
    put("eps5", np.full((P, 1), 1e-5))
    return o


def _layout(x):
    import numpy as np
    x = {k: np.asarray(a) for k, a in x.items()}
    wqkv = np.stack([_halves(x["L0_attn_" + n])[:DH] for n in ("wq", "wk", "wv")], 1)
    rk = _relation_tables(x["L0_attn_rk_v"], x["L0_attn_rk_h"])
    rv = _relation_tables(x["L0_attn_rv_v"], x["L0_attn_rv_h"])
    relk = np.zeros((2, HD0, NGV + NGH, 2, 32), np.float32)
    relv = np.zeros((2, 32, NGV + NGH, 2, HD0), np.float32)
    for e in range(2):
        relk[e, :, :, e, 0:24] = rk.transpose(2, 0, 1)
        relv[e, 0:24, :, e, :] = rv.transpose(1, 0, 2)
    rows = np.zeros(NROW, np.float32)
    for name, a in (("type", x["L0_tok_type_emb"][0]), ("gamma", x["L0_tok_ln_gamma"]), ("beta", x["L0_tok_ln_beta"]),
                    ("gatew", x["L0_tok_gate_w"][0]), ("gateb", x["L0_tok_gate_b"]), ("bproj", x["L0_attn_bproj"]),
                    ("subln", np.tile(x["L1_attn_subln_w"], H1)),
                    ("moe0_b2", x["L1_ffn_moe0_b2"]), ("a2_b", x["L1_ffn_A2_b"].ravel()),
                    ("lam", np.concatenate([x["L1_attn_lambda_" + n] for n in ("q1", "k1", "q2", "k2")]))):
        at, w = ROWS[name]
        rows[at:at + w] = a
    wr = np.concatenate([x["L0_ffn_gate_w"], x["L0_ffn_v_w"][:, None]], 1)
    br = np.concatenate([x["L0_ffn_gate_b"], x["L0_ffn_v_b"].reshape(1)])
    def spread(w):
        o = np.zeros((w.shape[0], NSUB, 32), np.float32)
        o[:, :, :HS] = w.reshape(-1, NSUB, HS)
        return o.reshape(w.shape[0], -1)

    def proj1(n):
        w, b = x["L1_attn_W" + n], x["L1_attn_b" + n][None]
        return _halves(spread(w), spread(b)[0]) if n in "qk" else _halves(w, b[0])

    def down(w):
        return w.reshape(MT, P, D).transpose(1, 0, 2)

    ones = np.ones((8, D), np.float32)
    return {
        "mixrows": np.concatenate([x["L0_ffn_b2"], x["L0_ffn_out_w"], x["L0_ffn_out_b"][None]], 0),
        "mixscale": np.concatenate([ones] + [x["L0_ffn_bk_scale"][None]] * 3, 0),
        "moe_w2": np.stack([down(w) for w in x["L0_ffn_w2"]], 1).reshape(P, -1),
        "wqk1": np.stack([proj1("q"), proj1("k")], 1).reshape(DH + 1, -1),
        "wvo1": np.stack([proj1("v"), proj1("o")], 1).reshape(DH + 1, -1),
        "moe0_w1": _halves(x["L1_ffn_moe0_W1"], x["L1_ffn_moe0_b1"]).reshape(DH + 1, -1),
        "moe0_w2": down(x["L1_ffn_moe0_W2"]).reshape(P, -1),
        "a1": np.stack([_halves(x["L1_ffn_A1_W"][e], x["L1_ffn_A1_b"][e]) for e in range(5)], 1).reshape(DH + 1, -1),
        "a2": np.stack([down(w) for w in x["L1_ffn_A2_W"]], 1).reshape(P, -1),
        "gates_w": _halves(x["L1_ffn_G_W"].transpose(1, 0, 2).reshape(D, -1))[:DH].reshape(DH, -1),
        "x": x["x"], "itok": x["itok_BS_2_399970"], "word_emb": x["L0_tok_word_emb"], "wvec": x["L0_tok_wvec"],
        "consts": _constants(), "rows": rows, "ones": np.ones((1, 1024), np.float32), "pos": x["L0_tok_pos_emb"],
        "g2b": np.concatenate([x["L0_tok_g2b_w"].T, x["L0_tok_g2b_b"][None]], 0),
        "wqkv": wqkv.reshape(DH, -1),
        "relk": relk.reshape(P, -1), "relv": relv.reshape(64, -1),
        "wproj": x["L0_attn_wproj"].reshape(MT, P, D).transpose(1, 0, 2).reshape(P, -1),
        "wroute": _halves(wr, br).reshape(DH + 1, -1),
        "moe_w1": np.stack([_halves(x["L0_ffn_w1"][e], x["L0_ffn_b1"][e]) for e in range(E)], 1).reshape(DH + 1, -1),
    }


def kernel(**inputs):
    import numpy as _np
    import concourse.bacc as _bacc
    from concourse import mybir as _mybir
    from concourse.bass_utils import run_bass_kernel_spmd as _run

    nc = _bacc.Bacc("TRN2", target_bir_lowering=False, num_devices=1)
    arrays, args = {}, {}
    for name, a in _layout(inputs).items():
        a = _np.ascontiguousarray(a)
        arrays[f"in_{name}"] = a
        args[name] = nc.dram_tensor(f"in_{name}", a.shape, _mybir.dt.from_np(a.dtype), kind="ExternalInput").ap()
    out = nc.dram_tensor("out_0", (B, P, D), F32, kind="ExternalOutput").ap()
    Tower(nc, args, out).build()
    r = _run(nc, [arrays], core_ids=[0])
    return r.results[0]["out_0"]
```

```python
from contextlib import ExitStack

import concourse.bass as bass
from concourse import mybir

F32 = mybir.dt.float32
I32 = mybir.dt.int32
U32 = mybir.dt.uint32
ALU = mybir.AluOpType
ACT = mybir.ActivationFunctionType
AX = mybir.AxisListType.X

P = 128
B = 64
D = 192
DH = D // 2
F = 768
HF = F // 2
MT = F // P
WD = 75
H0, HD0 = 12, 64
PAIRS = H0 // 2
SIDE = 11
NV = (P - 2) // SIDE + 1
VC, HC = 2, 3
NGV, NGH = NV // VC, -(-SIDE // HC)
NG0 = NGV + NGH + 2
PLACE0 = VC * NV + HC * SIDE
PSTEP = 80
QSTEP = P + 16
CUT = 1 + 6 * SIDE
E = 8
CAP = B * P + P
TILES = 2 * B * P // P + E
DUMP = E * CAP
NSUB, HS = 24, 8
H1, HV = 12, 16
NCLS = 6
GRP = 4
QUAD = 4
ROUNDS = ((0, 8), (8, 12))
LAMBDA_INIT = 0.8 - 0.6
BIG = 3.4028234663852886e38
FEAT_CLAMP = 10.0
V_MAX = 3.0
CLS_PAIRS = [[(0, 3), (3, 0)], [(0, 4), (4, 0)], [(1, 3), (3, 1)], [(1, 4), (4, 1)], [(2, 3), (3, 2)], [(2, 4), (4, 2)]]

CONSTS = {}
_at = 0
for _n, _w in (("ident", P), ("anti", P), ("tri", P), ("ones", P), ("ohk", P), ("ohv", 64), ("active", P), ("iota8", 8), ("step128", TILES),
               ("ebase", 8), ("neg_half", 1), ("eps12", 1), ("eps5", 1)):
    CONSTS[_n] = (_at, _w)
    _at += _w
NCONST = _at
ROWS = {}
_at = 0
for _n, _w in (("type", D), ("gamma", D), ("beta", D), ("gatew", D), ("gateb", 1), ("bproj", D), ("subln", D),
               ("moe0_b2", D), ("a2_b", 5 * D), ("lam", 4 * HS)):
    ROWS[_n] = (_at, _w)
    _at += _w
NROW = _at


def norm_statistics(v, w, sem, src):
    v.bn_stats(w["st"][:], src).then_inc(sem["dve"], 1)
    v.wait_ge(sem["dve"], 1)
    v.sem_inc(sem["dve"], -1)
    v.bn_aggr(w["mv"][:], w["st"][:]).then_inc(sem["var"], 1)


def norm_apply(v, w, sem, src, dst, done):
    v.wait_ge(sem["rstd"], 1)
    v.sem_inc(sem["rstd"], -1)
    return v.tensor_scalar(dst, src, w["mv"][:, 0:1], w["rstd"][:], ALU.subtract, ALU.mult).then_inc(done, 1)


def layer_norm(v, w, sem, src, dst, done):
    norm_statistics(v, w, sem, src)
    return norm_apply(v, w, sem, src, dst, done)


def inverse_root(g, w, sem, eps, half):
    g.wait_ge(sem["var"], 1)
    g.sem_inc(sem["var"], -1)
    g.tensor_tensor(w["ve"][:], w["mv"][:, 1:2], eps, ALU.add).then_inc(sem["pool"], 1)
    g.wait_ge(sem["pool"], 1)
    g.sem_inc(sem["pool"], -1)
    g.tensor_tensor(w["rstd"][:], w["ve"][:], half, ALU.pow).then_inc(sem["rstd"], 1)


class Tower:
    def __init__(self, nc, ins, out):
        self.nc, self.ins, self.out = nc, ins, out

    def sems(self, ctx, *names):
        return {n: ctx.enter_context(self.nc.semaphore(n)) for n in names}

    def build(self):
        nc, ins = self.nc, self.ins
        with ExitStack() as ctx:
            def sb(name, shape, dt=F32):
                return ctx.enter_context(nc.sbuf_tensor(name, shape, dt))
            self.ps = [ctx.enter_context(nc.psum_tensor(f"bank{i}", [P, 512], F32)) for i in range(8)]
            self.h = sb("h", [P, B * D])
            self.consts = sb("consts", [P, NCONST])
            self.rows = sb("rows", [P, NROW])
            self.w1 = sb("moe_w1", [DH + 1, E * 2 * F])
            self.slots = sb("slots", [P, 2 * B])
            self.yrows = sb("yrows", [P, 2 * B], I32)
            self.mixw = sb("mixw", [P, 2 * B])
            self.feats = sb("feats", [P, B * 11])
            self.vall = sb("vall", [P, B])
            self.slotbase = sb("slotbase", [P, E])
            self.mixrows = sb("mixrows", [11, D])
            self.mixscale = sb("mixscale", [11, D])
            self.ln = {"st": sb("ln_st", [P, 6]), "mv": sb("ln_mv", [P, 2]), "ve": sb("ln_ve", [P, 1]),
                       "rstd": sb("ln_rstd", [P, 1])}
            self.zslots = nc.dram_tensor("zslots", ((E + 1) * CAP, D), F32, kind="Internal").ap()
            self.yslots = nc.dram_tensor("yslots", (TILES * P, D), F32, kind="Internal").ap()
            self.S = self.sems(ctx, "dve", "act", "pool", "var", "rstd", "loaded", "w1_loaded", "l1_loaded")
            self.embed_and_attend()
            self.w_q = sb("w_q", [DH + 1, 2 * F])
            self.w_k = sb("w_k", [DH + 1, 2 * 2 * P])
            self.w_vo = sb("w_vo", [DH + 1, 2 * 2 * D])
            self.w_up = sb("w_up", [DH + 1, 2 * F])
            self.w_down = sb("w_down", [P, MT * D])
            self.experts()
            self.differential_attention()
            self.feed_forward()

    def c(self, name, rows=slice(0, P)):
        a, w = CONSTS[name]
        return self.consts[rows, a:a + w]

    def r(self, name):
        a, w = ROWS[name]
        return self.rows[:, a:a + w]

    def embed_and_attend(self):
        nc, ins, ps, h, T = self.nc, self.ins, self.ps, self.h, self.S
        with ExitStack() as ctx:
            def sb(name, shape, dt=F32):
                return ctx.enter_context(nc.sbuf_tensor(name, shape, dt))
            wqkv = sb("wqkv", [DH, 3 * 2 * F])
            wproj = sb("wproj", [P, MT * D])
            relk = sb("relk", [P, NG0 * P])
            relv = sb("relv", [P, NG0 * P])
            wroute = sb("wroute", [DH + 1, 2 * 9])
            g2b = sb("g2b", [WD + 1, D])
            postype = sb("postype", [P, D])
            negb = sb("negb", [P, 1])
            ids_in = sb("ids_in", [B, 2 * P], I32)
            ids_f = sb("ids_f", [B, 2 * P])
            ids = sb("ids", [P, 2 * B], I32)
            idw, idv = sb("idw", [P, 1], I32), sb("idv", [P, 1], I32)
            wrow, vrow = sb("wrow", [P, D]), sb("vrow", [P, WD + 1])
            emb, nrm, tok, h0, y, z, junk = (sb(n, [P, D]) for n in ("emb", "nrm", "tok", "h0", "y", "z", "junk"))
            vrowT = sb("vrowT", [WD + 1, P])
            zs = sb("zs", [P, 4])
            yT = sb("yT", [DH, 2 * P])
            zT = sb("zT", [DH + 1, 2 * P])
            qT = sb("qT", [P, PAIRS * QSTEP])
            qa, ka = sb("qa", [P, H0 * P]), sb("ka", [P, H0 * P])
            vv = sb("vv", [P, F])
            probs = sb("probs", [P, H0 * P])
            probsT = sb("probsT", [P, H0 * P])
            avT = sb("avT", [P, PAIRS * QSTEP])
            oT = sb("oT", [P, PAIRS * P])
            nmax, psum_, rinv = sb("nmax", [P, H0]), sb("psum_", [P, H0]), sb("rinv", [P, H0])
            lg = sb("lg", [P, 9])
            rt = sb("rt", [P, 4])
            prob8, top8, oh1, oh2, cmb, rank = (sb(n, [P, E]) for n in ("prob8", "top8", "oh1", "oh2", "cmb", "rank"))
            both = sb("both", [P, E])
            top8i = sb("top8i", [P, E], U32)
            top2f = sb("top2f", [P, 2])
            w2s = sb("w2s", [P, 2])
            s2f = sb("s2f", [P, 2])
            ids1, ids2 = sb("ids1", [P, 1], I32), sb("ids2", [P, 1], I32)

            S = self.sems(
                ctx, "ids_loaded", "ids_float", "ids_ps", "ids_ready", "word_in", "wvec_in", "word_free", "wvec_free",
                "vrowT_ps", "vrowT_in", "gate_z", "gate_e", "g_ps", "g_free", "y_ready", "y_free", "yT_ps", "yT_in",
                "qk_ps", "q_in", "k_ps", "k_in", "qr_ps", "qr_in", "s_ps", "nmax_ready", "exp_done", "probs_ready",
                "pT_ps", "pT_in", "v_ps", "v_in", "av_ps", "av_in", "o_ps", "o_in", "o2_ps", "o2_in", "proj_ps", "proj_free",
                "z_ready", "z_free", "zT_ps", "zT_in", "lg_ps", "rank_free", "rt_max", "values_done", "rt_exp", "chosen", "rank_ps",
                "slot_ready", "z_scattered", "idx_free")
            block = ctx.enter_context(nc.Block())
            NW = 11

            def heads(t):
                return t[:].rearrange("p (h t) -> p h t", t=P)

            def by_parity(t, e):
                return t[:].rearrange("p (h e t) -> p e h t", e=2, t=P)[:, e]

            ranges = ((0, CUT), (CUT, P))

            def groups(bank):
                def run(a, n):
                    return lambda x, lo: x[:, :, a - lo:a - lo + n]

                def grid(a, rows, cols):
                    return lambda x, lo: x[:, :, a - lo:a - lo + SIDE * rows].rearrange(
                        "p h (i c) -> p h i c", c=SIDE)[:, :, :, 0:cols]
                out = []
                for g in range(NGV):
                    a = 1 + VC * SIDE * g
                    if (a >= CUT) == bool(bank):
                        out.append((g, run(a, min(VC * SIDE, P - a))))
                for g in range(NGH):
                    a, cols = (CUT if bank else 1) + HC * g, min(HC, SIDE - HC * g)
                    rows = NV // 2
                    if a + SIDE * (rows - 1) + cols > P:
                        rows -= 1
                    out.append((NGV + g, grid(a, rows, cols)))
                if not bank:
                    out += [(NGV + NGH, run(0, 1)), (NGV + NGH + 1, run(0, 1))]
                return out

            def window(tile, rows):
                return tile[rows, 0:PAIRS * PSTEP].rearrange("p (h t) -> p h t", t=PSTEP)

            def banked(tile, bank, rows):
                return window(tile, rows)[:, :, 0:ranges[bank][1] - ranges[bank][0]]

            def active(bank, rows):
                lo, hi = ranges[bank]
                return self.c("active", rows)[:, lo:hi].unsqueeze(1).to_broadcast([rows.stop - rows.start, PAIRS, hi - lo])

            @block.sync
            def _(sp):
                sp.dma_start(ids_in[:, 0:P], ins["x"]).then_inc(S["ids_loaded"], 16)
                sp.dma_start(ids_in[:, P:2 * P], ins["itok"]).then_inc(S["ids_loaded"], 16)
                sp.dma_start(self.consts[:], ins["consts"]).then_inc(T["loaded"], 16)
                sp.dma_start(self.rows[:], ins["rows"].partition_broadcast(P)).then_inc(T["loaded"], 16)
                sp.dma_start(postype[:], ins["pos"]).then_inc(T["loaded"], 16)
                sp.dma_start(g2b[:], ins["g2b"]).then_inc(T["loaded"], 16)
                sp.dma_start(wqkv[:], ins["wqkv"]).then_inc(T["loaded"], 16)
                sp.dma_start(relk[:], ins["relk"]).then_inc(T["loaded"], 16)
                sp.dma_start(relv[:], ins["relv"]).then_inc(T["loaded"], 16)
                sp.dma_start(wproj[:], ins["wproj"]).then_inc(T["loaded"], 16)
                sp.dma_start(wroute[:], ins["wroute"]).then_inc(T["loaded"], 16)
                sp.dma_start(self.mixrows[:], ins["mixrows"]).then_inc(T["loaded"], 16)
                sp.dma_start(self.mixscale[:], ins["mixscale"]).then_inc(T["loaded"], 16)
                sp.dma_start(self.w1[:], ins["moe_w1"]).then_inc(T["w1_loaded"], 16)

            @block.gpsimd
            def _(g):
                neg_half = self.c("neg_half")

                def gather_words(b, first=False):
                    if not first:
                        g.wait_ge(S["word_free"], 1)
                        g.sem_inc(S["word_free"], -1)
                    g.tensor_copy(idw[:], ids[:, bass.ds(b, 1)]).then_inc(T["pool"], 1)
                    g.wait_ge(T["pool"], 1)
                    g.sem_inc(T["pool"], -1)
                    g.indirect_dma_start(out=wrow[:], out_offset=None, in_=ins["word_emb"],
                                         in_offset=bass.IndirectOffsetOnAxis(ap=idw[:, 0:1], axis=0)
                                         ).then_inc(S["word_in"], 16)

                def gather_vectors(b, first=False):
                    if not first:
                        g.wait_ge(S["wvec_free"], 1)
                        g.sem_inc(S["wvec_free"], -1)
                    g.tensor_copy(idv[:], ids[:, bass.ds(b + B, 1)]).then_inc(T["pool"], 1)
                    g.wait_ge(T["pool"], 1)
                    g.sem_inc(T["pool"], -1)
                    g.indirect_dma_start(out=vrow[:, 0:WD], out_offset=None, in_=ins["wvec"],
                                         in_offset=bass.IndirectOffsetOnAxis(ap=idv[:, 0:1], axis=0)
                                         ).then_inc(S["wvec_in"], 16)

                def gather(b, first=False):
                    gather_words(b, first)
                    gather_vectors(b, first)

                def word_norm():
                    inverse_root(g, self.ln, T, self.c("eps12"), neg_half)

                def y_norm():
                    inverse_root(g, self.ln, T, self.c("eps5"), neg_half)

                def tail_norm():
                    inverse_root(g, self.ln, T, self.c("eps5"), neg_half)

                def scatter():
                    g.wait_ge(S["slot_ready"], 1)
                    g.sem_inc(S["slot_ready"], -1)
                    for ix in (ids1, ids2):
                        g.indirect_dma_start(out=self.zslots, out_offset=bass.IndirectOffsetOnAxis(ap=ix[:, 0:1], axis=0),
                                             in_=z[:], in_offset=None).then_inc(S["z_scattered"], 16)

                g.wait_ge(S["ids_ready"], 1)
                g.sem_inc(S["ids_ready"], -1)
                g.wait_ge(T["loaded"], 16 * NW)
                gather(0, first=True)
                word_norm()
                gather(1)
                y_norm()
                word_norm()
                gather(2)
                y_norm()

                def step(b, routed, fetch, embed):
                    if routed:
                        tail_norm()
                    if embed:
                        word_norm()
                    if fetch:
                        gather(b + 3)
                    if embed:
                        y_norm()
                    if routed:
                        scatter()
                step(0, False, True, True)
                with g.Fori(1, B - 3) as b:
                    step(b, True, True, True)
                step(B - 3, True, False, True)
                step(B - 2, True, False, False)
                step(B - 1, True, False, False)
                tail_norm()
                scatter()

            @block.scalar
            def _(act):
                act.wait_ge(T["loaded"], 16 * NW)
                act.activation(negb[:], self.r("gateb"), ACT.Copy, scale=-1.0).then_inc(T["act"], 1)
                act.wait_ge(T["act"], 1)
                act.sem_inc(T["act"], -1)

                def vrowT_evac():
                    act.wait_ge(S["vrowT_ps"], 1)
                    act.sem_inc(S["vrowT_ps"], -1)
                    act.activation(vrowT[:], ps[7][0:WD + 1, 0:P], ACT.Copy).then_inc(S["vrowT_in"], 1)

                def gate_exp():
                    act.wait_ge(S["gate_z"], 1)
                    act.sem_inc(S["gate_z"], -1)
                    act.activation(zs[:, 1:2], zs[:, 0:1], ACT.Exp, bias=negb[:], scale=-1.0).then_inc(S["gate_e"], 1)

                def yT_evac():
                    act.wait_ge(S["yT_ps"], 1)
                    act.sem_inc(S["yT_ps"], -1)
                    act.activation(yT[:], ps[7][0:DH, 0:2 * P], ACT.Copy).then_inc(S["yT_in"], 1)

                def q_evac():
                    act.wait_ge(S["qk_ps"], 2)
                    act.sem_inc(S["qk_ps"], -2)
                    for bank, n in ((3, 4), (4, 2)):
                        a = 0 if bank == 3 else 4
                        act.activation(qT[:].rearrange("p (h t) -> p h t", t=QSTEP)[:, a:a + n, 0:P],
                                       ps[bank][:, 0:n * P].rearrange("p (h t) -> p h t", t=P), ACT.Copy, scale=HD0 ** -0.5)
                    for bank, n in ((3, 4), (4, 2)):
                        a = 0 if bank == 3 else 4
                        for e in range(2):
                            last = act.activation(by_parity(qa, e)[0:64, a:a + n, :],
                                                  ps[bank][64 * e:64 * e + 64, 0:n * P].rearrange("p (h t) -> p h t", t=P),
                                                  ACT.Copy, scale=HD0 ** -0.5)
                    last.then_inc(S["q_in"], 1)

                def v_evac(first=False):
                    if not first:
                        act.wait_ge(S["values_done"], 1)
                        act.sem_inc(S["values_done"], -1)
                    for i in range(2):
                        act.wait_ge(S["v_ps"], 1)
                        act.sem_inc(S["v_ps"], -1)
                        act.activation(vv[:, 384 * i:384 * i + 384], ps[i][:, 0:384], ACT.Copy).then_inc(S["v_in"], 1)

                def softmax():
                    for g in range(3):
                        act.wait_ge(S["nmax_ready"], 1)
                        act.sem_inc(S["nmax_ready"], -1)
                        for k in range(4):
                            n = 4 * g + k
                            last = act.activation(probs[:, P * n:P * n + P], ps[g][:, P * k:P * k + P], ACT.Exp,
                                                  bias=nmax[:, n:n + 1], accum_out=psum_[:, n:n + 1])
                        last.then_inc(S["exp_done"], 1)

                def pT_evac():
                    for g in range(3):
                        act.wait_ge(S["pT_ps"], 1)
                        act.sem_inc(S["pT_ps"], -1)
                        act.activation(probsT[:, 512 * g:512 * g + 512], ps[g][:], ACT.Copy).then_inc(S["pT_in"], 1)

                def o_evac():
                    act.wait_ge(S["o2_ps"], 1)
                    act.sem_inc(S["o2_ps"], -1)
                    lo, hi = ranges[1]
                    act.activation(heads(oT)[:, :, lo:hi], banked(ps[4], 1, slice(0, P)), ACT.Copy).then_inc(S["o2_in"], 1)

                def zT_evac():
                    act.wait_ge(S["zT_ps"], 1)
                    act.sem_inc(S["zT_ps"], -1)
                    act.activation(zT[0:DH, :], ps[7][0:DH, 2 * P:4 * P], ACT.Copy).then_inc(S["zT_in"], 1)

                def route_exp():
                    act.wait_ge(S["rt_max"], 1)
                    act.sem_inc(S["rt_max"], -1)
                    act.activation(prob8[:], lg[:, 0:8], ACT.Exp, bias=rt[:, 0:1], accum_out=rt[:, 1:2]).then_inc(S["rt_exp"], 1)

                vrowT_evac()
                gate_exp()
                yT_evac()
                q_evac()
                v_evac(first=True)
                vrowT_evac()
                gate_exp()
                yT_evac()

                def step(route, one, two):
                    softmax()
                    if one:
                        q_evac()
                    pT_evac()
                    if two:
                        vrowT_evac()
                    if route:
                        zT_evac()
                    if two:
                        gate_exp()
                    if route:
                        route_exp()
                    if one:
                        v_evac()
                    else:
                        act.wait_ge(S["values_done"], 1)
                        act.sem_inc(S["values_done"], -1)
                    o_evac()
                    if two:
                        yT_evac()
                step(False, True, True)
                with act.Fori(1, B - 2) as b:
                    step(True, True, True)
                step(True, True, False)
                step(True, False, False)
                zT_evac()
                route_exp()

            @block.vector
            def _(v):
                def own(ins_):
                    ins_.then_inc(T["dve"], 1)
                    v.wait_ge(T["dve"], 1)
                    v.sem_inc(T["dve"], -1)

                v.wait_ge(T["loaded"], 16 * NW)
                v.memset(zT[DH:DH + 1, :], 1.0)
                v.memset(vrow[:, WD:WD + 1], 1.0)
                v.memset(self.feats[:], 1.0)
                v.tensor_copy(ka[64:P, :].rearrange("p (h t) -> p h t", t=P),
                              self.c("ohk", slice(64, P)).unsqueeze(1).to_broadcast([64, H0, P]))
                v.wait_ge(S["ids_loaded"], 32)
                v.tensor_copy(ids_f[:], ids_in[:]).then_inc(S["ids_float"], 1)
                v.tensor_copy(self.slotbase[:], self.c("ebase"))
                own(v.tensor_tensor(postype[:], postype[:], self.r("type"), ALU.add))
                v.wait_ge(S["ids_ps"], 1)
                v.sem_inc(S["ids_ps"], -1)
                v.tensor_copy(ids[:], ps[7][:, 0:2 * B]).then_inc(S["ids_ready"], 1)

                def embed(b):
                    v.wait_ge(S["word_in"], 16 * (b + 1))
                    own(v.tensor_tensor(emb[:], wrow[:], postype[:], ALU.add))
                    v.sem_inc(S["word_free"], 1)
                    layer_norm(v, self.ln, T, emb[:], nrm[:], T["dve"])
                    v.wait_ge(T["dve"], 1)
                    v.sem_inc(T["dve"], -1)
                    own(v.tensor_tensor(nrm[:], nrm[:], self.r("gamma"), ALU.mult))
                    own(v.tensor_tensor(tok[:], nrm[:], self.r("beta"), ALU.add))
                    v.tensor_tensor_reduce(out=junk[:], in0=tok[:], in1=self.r("gatew"), scale=1.0, scalar=0.0,
                                           op0=ALU.mult, op1=ALU.add, accum_out=zs[:, 0:1]).then_inc(S["gate_z"], 1)

                def gate():
                    v.wait_ge(S["gate_e"], 1)
                    v.sem_inc(S["gate_e"], -1)
                    own(v.tensor_scalar(zs[:, 2:3], zs[:, 1:2], 1.0, None, ALU.add))
                    own(v.reciprocal(zs[:, 3:4], zs[:, 2:3]))
                    v.wait_ge(S["g_ps"], 1)
                    v.sem_inc(S["g_ps"], -1)
                    own(v.tensor_tensor(nrm[:], ps[7][:, P:P + D], tok[:], ALU.subtract))
                    own(v.scalar_tensor_tensor(out=h0[:], in0=nrm[:], scalar=zs[:, 3:4], in1=tok[:],
                                               op0=ALU.mult, op1=ALU.add))

                def make_y(b, first=False):
                    v.tensor_tensor(h[:, bass.ds(b * D, D)], h0[:], self.r("bproj"), ALU.add)
                    if not first:
                        v.wait_ge(S["y_free"], 1)
                        v.sem_inc(S["y_free"], -1)
                    layer_norm(v, self.ln, T, h0[:], y[:], S["y_ready"])

                def k_evac():
                    v.wait_ge(S["k_ps"], 1)
                    v.sem_inc(S["k_ps"], -1)
                    for bank, a, n in ((5, 0, 4), (6, 4, 2)):
                        for e in range(2):
                            last = v.tensor_copy(by_parity(ka, e)[0:64, a:a + n, :],
                                                 ps[bank][64 * e:64 * e + 64, 0:n * P].rearrange("p (h t) -> p h t", t=P))
                    last.then_inc(S["k_in"], 1)

                def qr_evac():
                    v.wait_ge(S["qr_ps"], 1)
                    v.sem_inc(S["qr_ps"], -1)
                    for bank in range(2):
                        lo, hi = ranges[bank]
                        for e in range(2):
                            half = slice(64 * e, 64 * e + 64)
                            last = v.tensor_tensor(by_parity(qa, e)[64:P, :, lo:hi], banked(ps[3 + bank], bank, half),
                                                   active(bank, half), ALU.mult)
                    last.then_inc(S["qr_in"], 1)

                def av_evac():
                    v.wait_ge(S["av_ps"], 1)
                    v.sem_inc(S["av_ps"], -1)
                    for bank in range(2):
                        lo, hi = ranges[bank]
                        last = v.tensor_tensor(avT[:].rearrange("p (h t) -> p h t", t=QSTEP)[:, :, lo:hi],
                                               banked(ps[5 + bank], bank, slice(0, P)), active(bank, slice(0, P)), ALU.mult)
                    last.then_inc(S["av_in"], 1)

                def o_evac():
                    v.wait_ge(S["o_ps"], 1)
                    v.sem_inc(S["o_ps"], -1)
                    lo, hi = ranges[0]
                    v.tensor_copy(heads(oT)[:, :, lo:hi], banked(ps[3], 0, slice(0, P))).then_inc(S["o_in"], 1)

                def maxima():
                    for g in range(3):
                        v.wait_ge(S["s_ps"], 1)
                        v.sem_inc(S["s_ps"], -1)
                        v.tensor_reduce(out=nmax[:, 4 * g:4 * g + 4], in_=ps[g][:].rearrange("p (h t) -> p h t", t=P),
                                        op=ALU.max, axis=AX, negate=True).then_inc(S["nmax_ready"], 1)

                def normalise():
                    for g in range(3):
                        v.wait_ge(S["exp_done"], 1)
                        v.sem_inc(S["exp_done"], -1)
                        own(v.reciprocal(rinv[:, 4 * g:4 * g + 4], psum_[:, 4 * g:4 * g + 4]))
                        e4 = probs[:, 512 * g:512 * g + 512].rearrange("p (h t) -> p h t", t=P)
                        v.tensor_tensor(e4, e4, rinv[:, 4 * g:4 * g + 4].unsqueeze(2).to_broadcast([P, 4, P]),
                                        ALU.mult).then_inc(S["probs_ready"], 1)

                def add_proj(b):
                    v.wait_ge(S["proj_ps"], 1)
                    v.sem_inc(S["proj_ps"], -1)
                    own(v.tensor_tensor(h[:, bass.ds(b * D, D)], h[:, bass.ds(b * D, D)], ps[5][:, 0:D], ALU.add))
                    v.sem_inc(S["proj_free"], 1)

                def tail_norm(b, first=False):
                    if not first:
                        v.wait_ge(S["z_scattered"], 32 * b)
                        v.wait_ge(S["z_free"], 1)
                        v.sem_inc(S["z_free"], -1)
                    norm_apply(v, self.ln, T, h[:, bass.ds(b * D, D)], z[:], S["z_ready"])

                def choose(b):
                    v.wait_ge(S["lg_ps"], 1)
                    v.sem_inc(S["lg_ps"], -1)
                    own(v.tensor_copy(lg[:], ps[2][:, 0:9]))
                    v.tensor_copy(self.vall[:, bass.ds(b, 1)], lg[:, 8:9])
                    v.tensor_reduce(out=rt[:, 0:1], in_=lg[:, 0:8], op=ALU.max, axis=AX, negate=True).then_inc(S["rt_max"], 1)
                    v.wait_ge(S["rt_exp"], 1)
                    v.sem_inc(S["rt_exp"], -1)
                    own(v.reciprocal(rt[:, 2:3], rt[:, 1:2]))
                    own(v.tensor_scalar(prob8[:], prob8[:], rt[:, 2:3], None, ALU.mult))
                    own(v.max(out=top8[:], in_=prob8[:]))
                    own(v.max_index(out=top8i[:], in_max=top8[:], in_values=prob8[:]))
                    own(v.tensor_copy(top2f[:], top8i[:, 0:2]))
                    v.tensor_scalar(oh1[:], self.c("iota8"), top2f[:, 0:1], None, ALU.is_equal)
                    own(v.tensor_scalar(oh2[:], self.c("iota8"), top2f[:, 1:2], None, ALU.is_equal))
                    v.tensor_tensor(both[:], oh1[:], oh2[:], ALU.add).then_inc(S["chosen"], 1)
                    own(v.tensor_tensor(rt[:, 3:4], top8[:, 0:1], top8[:, 1:2], ALU.add))
                    own(v.reciprocal(rt[:, 2:3], rt[:, 3:4]))
                    own(v.tensor_scalar(w2s[:], top8[:, 0:2], rt[:, 2:3], None, ALU.mult))
                    v.tensor_copy(self.mixw[:, bass.ds(2 * b, 2)], w2s[:])
                    own(v.tensor_scalar(cmb[:], oh1[:], w2s[:, 0:1], None, ALU.mult))
                    v.scalar_tensor_tensor(out=self.feats[:, bass.ds(11 * b, 8)], in0=oh2[:], scalar=w2s[:, 1:2], in1=cmb[:],
                                           op0=ALU.mult, op1=ALU.add)

                def place(b):
                    v.wait_ge(S["rank_ps"], 1)
                    v.sem_inc(S["rank_ps"], -1)
                    own(v.tensor_tensor(rank[:], ps[6][:, 0:8], self.slotbase[:], ALU.add))
                    own(v.tensor_tensor(self.slotbase[:], self.slotbase[:], ps[6][:, 8:16], ALU.add))
                    v.sem_inc(S["rank_free"], 1)
                    v.tensor_tensor_reduce(out=cmb[:], in0=oh1[:], in1=rank[:], scale=1.0, scalar=0.0, op0=ALU.mult,
                                           op1=ALU.add, accum_out=s2f[:, 0:1])
                    own(v.tensor_tensor_reduce(out=top8[:], in0=oh2[:], in1=rank[:], scale=1.0, scalar=0.0, op0=ALU.mult,
                                               op1=ALU.add, accum_out=s2f[:, 1:2]))
                    v.tensor_copy(self.slots[:, bass.ds(2 * b, 2)], s2f[:])
                    v.tensor_copy(ids1[:], s2f[:, 0:1])
                    v.tensor_copy(ids2[:], s2f[:, 1:2]).then_inc(S["slot_ready"], 1)

                embed(0)
                gate()
                make_y(0, first=True)
                k_evac()
                qr_evac()
                embed(1)
                gate()
                make_y(1)

                def step(b, routed, one, two, first_tail=False):
                    maxima()
                    if routed:
                        add_proj(b - 1)
                        norm_statistics(v, self.ln, T, h[:, bass.ds((b - 1) * D, D)])
                    normalise()
                    if one:
                        k_evac()
                    if routed:
                        tail_norm(b - 1, first=first_tail)
                    if two:
                        embed(b + 2)
                    if one:
                        qr_evac()
                    av_evac()
                    if routed:
                        choose(b - 1)
                    if two:
                        gate()
                    o_evac()
                    if two:
                        make_y(b + 2)
                    if routed:
                        place(b - 1)
                step(0, False, True, True)
                step(1, True, True, True, first_tail=True)
                with v.Fori(2, B - 2) as b:
                    step(b, True, True, True)
                step(B - 2, True, True, False)
                step(B - 1, True, False, False)
                add_proj(B - 1)
                norm_statistics(v, self.ln, T, h[:, (B - 1) * D:B * D])
                tail_norm(B - 1)
                choose(B - 1)
                place(B - 1)
                v.wait_ge(S["z_scattered"], 32 * B)

            @block.tensor
            def _(pe):
                ident = self.c("ident")
                pe.wait_ge(T["loaded"], 16 * NW)
                pe.wait_ge(S["ids_float"], 1)
                pe.sem_inc(S["ids_float"], -1)
                pe.transpose(ps[7][:, 0:B], ids_f[:, 0:P], ident[0:B, 0:B])
                pe.transpose(ps[7][:, B:2 * B], ids_f[:, P:2 * P], ident[0:B, 0:B]).then_inc(S["ids_ps"], 1)

                def vrow_T(b):
                    pe.wait_ge(S["wvec_in"], 16 * (b + 1))
                    pe.transpose(ps[7][0:WD + 1, 0:P], vrow[:], ident).then_inc(S["vrowT_ps"], 1)

                def word_proj():
                    pe.wait_ge(S["vrowT_in"], 1)
                    pe.sem_inc(S["vrowT_in"], -1)
                    pe.sem_inc(S["wvec_free"], 1)
                    pe.matmul(ps[7][:, P:P + D], vrowT[:], g2b[:], start=True, stop=True).then_inc(S["g_ps"], 1)

                def y_T():
                    pe.wait_ge(S["y_ready"], 1)
                    pe.sem_inc(S["y_ready"], -1)
                    for c in range(2):
                        last = pe.transpose(ps[7][0:DH, P * c:P * c + P], y[:, DH * c:DH * c + DH], ident)
                    last.then_inc(S["yT_ps"], 1)

                def qk_proj(before_k=None):
                    pe.wait_ge(S["yT_in"], 1)
                    pe.sem_inc(S["yT_in"], -1)
                    pe.sem_inc(S["y_free"], 1)
                    for t in range(12):
                        which, m = t // 6, t % 6
                        if t == 6 and before_k:
                            before_k()
                        for c in range(2):
                            a = which * 2 * F + c * F + m * P
                            last = pe.matmul(ps[3 + 2 * which + m // 4][:, (m % 4) * P:(m % 4) * P + P], wqkv[:, a:a + P],
                                             yT[:, P * c:P * c + P], start=(c == 0), stop=(c == 1))
                        if t == 3 or t == 5:
                            last.then_inc(S["qk_ps"], 1)
                        if t == 11:
                            last.then_inc(S["k_ps"], 1)

                def query_relations():
                    pe.wait_ge(S["q_in"], 1)
                    pe.sem_inc(S["q_in"], -1)
                    q3 = qT[:].rearrange("p (h t) -> p h t", t=QSTEP)
                    for bank in range(2):
                        o, gs = window(ps[3 + bank], slice(0, P)), groups(bank)
                        for n, (g, view) in enumerate(gs):
                            last = pe.matmul(view(o, ranges[bank][0]), relk[:, P * g:P * g + P], view(q3, 0),
                                             start=(n == 0), stop=(n == len(gs) - 1), skip_group_check=True)
                    last.then_inc(S["qr_ps"], 1)

                def v_proj():
                    for i in range(2):
                        for c in range(2):
                            a = 4 * F + c * F + 384 * i
                            last = pe.matmul(ps[i][:, 0:384], yT[:, P * c:P * c + P], wqkv[:, a:a + 384],
                                             start=(c == 0), stop=(c == 1))
                        last.then_inc(S["v_ps"], 1)

                def scores():
                    for n in range(H0):
                        last = pe.matmul(ps[n // 4][:, (n % 4) * P:(n % 4) * P + P], qa[:, P * n:P * n + P],
                                         ka[:, P * n:P * n + P], start=True, stop=True)
                        if n % 4 == 3:
                            last.then_inc(S["s_ps"], 1)

                def probs_T():
                    for g in range(3):
                        pe.wait_ge(S["probs_ready"], 1)
                        pe.sem_inc(S["probs_ready"], -1)
                        for k in range(4):
                            n = 4 * g + k
                            last = pe.transpose(ps[g][:, P * k:P * k + P], probs[:, P * n:P * n + P], ident)
                        last.then_inc(S["pT_ps"], 1)

                def probs_by_place():
                    pe.wait_ge(S["pT_in"], 3)
                    pe.sem_inc(S["pT_in"], -3)
                    pT = probsT[:].rearrange("p (h e t) -> p h e t", e=2, t=P)
                    for bank in range(2):
                        lo, hi = ranges[bank]
                        for e in range(2):
                            last = pe.matmul(banked(ps[5 + bank], bank, slice(64 * e, 64 * e + 64)), self.c("ohv"),
                                             pT[:, :, e, lo:hi], start=True, stop=True)
                    last.then_inc(S["av_ps"], 1)

                def values():
                    for bank in range(2):
                        lo, hi = ranges[bank]
                        for e in range(2):
                            for p_ in range(PAIRS):
                                n = 2 * p_ + e
                                last = pe.matmul(banked(ps[3 + bank], bank, slice(64 * e, 64 * e + 64))[:, p_, :],
                                          vv[:, 64 * n:64 * n + 64], probsT[:, P * n + lo:P * n + hi],
                                          start=(p_ == 0), stop=False, skip_group_check=True)
                    last.then_inc(S["values_done"], 1)

                def value_relations(between=None):
                    pe.wait_ge(S["av_in"], 1)
                    pe.sem_inc(S["av_in"], -1)
                    a3 = avT[:].rearrange("p (h t) -> p h t", t=QSTEP)
                    for bank in range(2):
                        if bank and between:
                            between()
                        o, gs = window(ps[3 + bank], slice(0, P)), groups(bank)
                        for n, (g, view) in enumerate(gs):
                            last = pe.matmul(view(o, ranges[bank][0]), relv[:, P * g:P * g + P], view(a3, 0),
                                             start=False, stop=(n == len(gs) - 1), skip_group_check=True)
                        last.then_inc(S["o2_ps" if bank else "o_ps"], 1)

                def out_proj():
                    pe.wait_ge(S["o_in"], 1)
                    pe.sem_inc(S["o_in"], -1)
                    pe.wait_ge(S["o2_in"], 1)
                    pe.sem_inc(S["o2_in"], -1)
                    for m in range(MT):
                        last = pe.matmul(ps[5][:, 0:D], oT[:, P * m:P * m + P], wproj[:, D * m:D * m + D],
                                         start=(m == 0), stop=(m == MT - 1))
                    last.then_inc(S["proj_ps"], 1)

                def z_T():
                    pe.wait_ge(S["z_ready"], 1)
                    pe.sem_inc(S["z_ready"], -1)
                    for c in range(2):
                        last = pe.transpose(ps[7][0:DH, P * (2 + c):P * (3 + c)], z[:, DH * c:DH * c + DH], ident)
                    last.then_inc(S["zT_ps"], 1)

                def zT_arrived():
                    pe.wait_ge(S["zT_in"], 1)
                    pe.sem_inc(S["zT_in"], -1)
                    pe.sem_inc(S["z_free"], 1)

                def route_logits():
                    for c in range(2):
                        k = DH + c
                        last = pe.matmul(ps[2][:, 0:9], zT[0:k, P * c:P * c + P], wroute[0:k, 9 * c:9 * c + 9],
                                         start=(c == 0), stop=(c == 1))
                    last.then_inc(S["lg_ps"], 1)

                def ranks():
                    pe.wait_ge(S["chosen"], 1)
                    pe.sem_inc(S["chosen"], -1)
                    pe.matmul(ps[6][:, 0:8], self.c("tri"), both[:], start=True, stop=True)
                    pe.matmul(ps[6][:, 8:16], self.c("ones"), both[:], start=True, stop=True).then_inc(S["rank_ps"], 1)

                vrow_T(0)
                word_proj()
                y_T()
                qk_proj()
                query_relations()
                pe.wait_ge(S["k_in"], 1)
                pe.sem_inc(S["k_in"], -1)
                v_proj()
                pe.wait_ge(S["qr_in"], 1)
                pe.sem_inc(S["qr_in"], -1)
                vrow_T(1)
                word_proj()
                y_T()

                def step(b, route, one, two, first=False, first_route=False):
                    pe.wait_ge(S["v_in"], 2)
                    pe.sem_inc(S["v_in"], -2)
                    scores()

                    def banks_free():
                        if not first:
                            pe.wait_ge(S["proj_free"], 1)
                            pe.sem_inc(S["proj_free"], -1)
                        if route and not first_route:
                            pe.wait_ge(S["rank_free"], 1)
                            pe.sem_inc(S["rank_free"], -1)
                    if one:
                        qk_proj(before_k=banks_free)
                    else:
                        banks_free()
                    probs_T()
                    if one:
                        query_relations()
                    if route:
                        z_T()
                    if two:
                        vrow_T(b + 2)
                    if one:
                        pe.wait_ge(S["k_in"], 1)
                        pe.sem_inc(S["k_in"], -1)
                    probs_by_place()
                    if route:
                        zT_arrived()
                    if two:
                        word_proj()
                    if route:
                        route_logits()
                    if one:
                        v_proj()
                        pe.wait_ge(S["qr_in"], 1)
                        pe.sem_inc(S["qr_in"], -1)
                    values()
                    value_relations(between=ranks if route else None)
                    out_proj()
                    if two:
                        y_T()
                step(0, False, True, True, first=True)
                step(1, True, True, True, first_route=True)
                with pe.Fori(2, B - 2) as b:
                    step(b, True, True, True)
                step(B - 2, True, True, False)
                step(B - 1, True, False, False)
                pe.wait_ge(S["proj_free"], 1)
                pe.sem_inc(S["proj_free"], -1)
                pe.wait_ge(S["rank_free"], 1)
                pe.sem_inc(S["rank_free"], -1)
                z_T()
                zT_arrived()
                route_logits()
                ranks()

    def experts(self):
        nc, ins, ps, T = self.nc, self.ins, self.ps, self.S
        with ExitStack() as ctx:
            def sb(name, shape, dt=F32):
                return ctx.enter_context(nc.sbuf_tensor(name, shape, dt))
            w2 = sb("moe_w2", [P, E * MT * D])
            coef = sb("coef", [P, TILES * 4])
            state = sb("state", [P, TILES * 4])

            def places(t, even, odd, n):
                v8 = t[:].rearrange("p (u c) -> p u c", c=8)
                return v8[:, 0:n // 2, even:odd + 5:odd + 4 - even]
            tile_row, tile_expert = sb("tile_row", [1, TILES], I32), sb("tile_expert", [1, TILES], I32)
            region_end = sb("region_end", [1, E], I32)
            zeros = sb("zeros", [P, D])
            vclip = sb("vclip", [P, B])
            zt = [sb(f"zt{p}", [P, D]) for p in range(2)]
            zT = [sb(f"zT{p}", [DH + 1, 2 * P]) for p in range(2)]
            hid2, hT2 = sb("hid", [P, 2 * F]), sb("hT", [P, 2 * F])
            hid = [hid2[:, F * p:F * p + F] for p in range(2)]
            hT = [hT2[:, F * p:F * p + F] for p in range(2)]
            yt = [sb(f"yt{p}", [P, D]) for p in range(2)]
            sq, nrm2, inv = sb("sq", [P, 2]), sb("nrm2", [P, 1]), sb("inv", [P, 1])
            big, big2 = hid2[0:1, 0:TILES * E], hT2[0:1, 0:TILES * E]
            t8 = sb("t8", [P, 6 * E])
            moved = sb("moved", [P, 2 * B])
            tt = sb("tt", [1, 4 * TILES])
            S = self.sems(ctx, "planned", "vclipped", "v_turned", "filled", "w2_loaded", "gelu_warm",
                          *(f"{n}{p}" for n in ("zt_in", "zt_free", "zT_ps", "zT_in", "h_ps", "h_in", "hT_ps", "hT_in", "y_ps", "y_in", "y_out")
                            for p in range(2)))
            S2 = self.sems(ctx, "state_split", "state_T", "state_in", "e_ps")
            dcomp = [hid2[:, 0:P], hid2[:, P:2 * P]]
            xs = [sb(f"xs{i}", [P, P]) for i in range(2)]
            fin = [sb(f"fin{i}", [P, B]) for i in range(4)]

            with nc.Block() as block:
                @block.sync
                def _(sp):
                    sp.dma_start(w2[:], ins["moe_w2"]).then_inc(S["w2_loaded"], 16)
                    for t, n, name in ((self.w_q, 1, "wq1"), (self.w_k, 1, "wk1"), (self.w_vo, 2, "wvo1"), (self.w_up, 1, "moe0_w1"), (self.w_down, 1, "moe0_w2")):
                        sp.dma_start(t[:], ins[name]).then_inc(T["l1_loaded"], 16)
                    sp.wait_ge(S["planned"], 1)
                    sp.sem_inc(S["planned"], -1)
                    for e in range(E):
                        r = sp.value_load(region_end[0:1, e:e + 1], min_val=0, max_val=E * CAP)
                        sp.dma_start(self.zslots[bass.ds(r, P), :], zeros[:]).then_inc(S["filled"], 16)
                        sp.dma_start(self.zslots[DUMP + P * e:DUMP + P * e + P, :], zeros[:]).then_inc(S["filled"], 16)
                    sp.wait_ge(S["filled"], 32 * E)
                    sp.wait_ge(T["w1_loaded"], 16)
                    sp.wait_ge(S["w2_loaded"], 16)
                    sp.wait_ge(T["l1_loaded"], 80)

                @block.vector
                def _(v):
                    def own(i):
                        i.then_inc(T["dve"], 1)
                        v.wait_ge(T["dve"], 1)
                        v.sem_inc(T["dve"], -1)
                    v.memset(zeros[:], 0.0)
                    for p in range(2):
                        v.memset(zT[p][DH:DH + 1, :], 1.0)
                    v.tensor_scalar(vclip[:], self.vall[:], -V_MAX, V_MAX, ALU.max, ALU.min).then_inc(S["vclipped"], 1)
                    total, tiles, incl, excl, shift, step = (t8[:, E * i:E * i + E] for i in range(6))
                    own(v.tensor_tensor(total, self.slotbase[:], self.c("ebase"), ALU.subtract))
                    m = hid2[:, 0:E * B].rearrange("p (e k) -> p e k", k=B)
                    own(v.tensor_tensor(m, total.unsqueeze(2).to_broadcast([P, E, B]),
                                        self.c("step128")[:, 0:B].unsqueeze(1).to_broadcast([P, E, B]), ALU.is_gt))
                    own(v.tensor_reduce(out=tiles, in_=m, op=ALU.add, axis=AX))
                    own(v.tensor_tensor_scan(incl, self.c("ones")[:, 0:E], tiles, 0.0, ALU.mult, ALU.add))
                    own(v.tensor_tensor(excl, incl, tiles, ALU.subtract))
                    own(v.tensor_scalar(shift, excl, -float(P), None, ALU.mult))
                    own(v.tensor_tensor(shift, shift, self.c("ebase"), ALU.add))
                    own(v.tensor_tensor(step[:, 1:E], shift[:, 0:E - 1], shift[:, 1:E], ALU.subtract))
                    own(v.tensor_copy(moved[:], self.slots[:]))
                    for e in range(1, E):
                        past = hT2[:, 0:2 * B]
                        own(v.tensor_scalar(past, self.slots[:], float(e * CAP), step[:, e:e + 1], ALU.is_ge, ALU.mult))
                        own(v.tensor_tensor(moved[:], moved[:], past, ALU.add))
                    v.tensor_copy(self.yrows[:], moved[:])
                    own(v.tensor_scalar(total, excl, float(P), None, ALU.mult))
                    own(v.tensor_scalar(incl, incl, float(P), None, ALU.mult))
                    total, incl, shift = total[0:1], incl[0:1], shift[0:1]
                    t128 = self.c("step128", slice(0, 1))
                    m1, m2 = (b_.rearrange("p (t e) -> p t e", e=E) for b_ in (big, big2))
                    tb = t128.unsqueeze(2).to_broadcast([1, TILES, E])

                    def eb(a):
                        return a.unsqueeze(1).to_broadcast([1, TILES, E])
                    v.tensor_tensor(m1, tb, eb(total), ALU.is_ge)
                    own(v.tensor_tensor(m2, tb, eb(incl), ALU.is_ge))
                    own(v.tensor_tensor(m1, m1, m2, ALU.subtract))
                    used, start, name, row = (tt[:, TILES * i:TILES * i + TILES] for i in range(4))
                    own(v.tensor_reduce(out=used, in_=m1, op=ALU.add, axis=AX))
                    own(v.tensor_tensor(m2, m1, eb(shift), ALU.mult))
                    own(v.tensor_reduce(out=start, in_=m2, op=ALU.add, axis=AX))
                    own(v.tensor_tensor(m2, m1, eb(self.c("iota8", slice(0, 1))), ALU.mult))
                    own(v.tensor_reduce(out=name, in_=m2, op=ALU.add, axis=AX))
                    own(v.tensor_scalar(used, used, -float(DUMP - 2 * B * P), float(DUMP - 2 * B * P), ALU.mult, ALU.add))
                    own(v.tensor_tensor(row, start, t128, ALU.add))
                    own(v.tensor_tensor(row, row, used, ALU.add))
                    v.tensor_copy(tile_row[:], row)
                    v.tensor_copy(tile_expert[:], name)
                    v.tensor_copy(region_end[:], self.slotbase[0:1, :]).then_inc(S["planned"], 1)
                    own(v.memset(coef[:], -1.0))
                    u0 = P // 2
                    c8 = coef[:].rearrange("p (u c) -> p u c", c=8)
                    for at, value in ((0, -2.0), (6, -2.0), (2, 2.0), (4, 2.0)):
                        v.memset(c8[:, u0:TILES // 2, at:at + 1], value)
                    v.wait_ge(S["v_turned"], 1)
                    v.sem_inc(S["v_turned"], -1)
                    turned = ps[0][:, 0:P].rearrange("p (u c) -> p u c", c=2)
                    v.tensor_scalar(places(coef, 0, 2, P), turned, -2.0, None, ALU.add)
                    own(v.tensor_scalar(c8[:, 0:u0, 2:5:2], turned, -1.0, 2.0, ALU.mult, ALU.add))
                    own(v.tensor_copy(state[:, 0:4], coef[:, 0:4]))

                @block.tensor
                def _(pe):
                    pe.wait_ge(S["vclipped"], 1)
                    pe.sem_inc(S["vclipped"], -1)
                    pe.matmul(ps[0][0:B, 0:P], vclip[:], self.c("ident"), start=True, stop=True)
                    pe.matmul(ps[0][B:2 * B, 0:P], vclip[:], self.c("anti"), start=True, stop=True).then_inc(S["v_turned"], 1)

                @block.scalar
                def _(act):
                    act.activation(self.ln["ve"][:], self.c("ones")[:, 0:1], ACT.Gelu_apprx_tanh).then_inc(S["gelu_warm"], 1)
                    act.wait_ge(S["gelu_warm"], 1)

            with nc.Block() as block:
                @block.sync
                def _(sp):
                    def row_of(t):
                        return sp.value_load(tile_row[0:1, bass.ds(t, 1)], min_val=0, max_val=(E + 1) * CAP - P)

                    def load(t, p, first=False):
                        if not first:
                            sp.wait_ge(S[f"zt_free{p}"], 1)
                            sp.sem_inc(S[f"zt_free{p}"], -1)
                        sp.dma_start(zt[p][:], self.zslots[bass.ds(row_of(t), P), :]).then_inc(S[f"zt_in{p}"], 16)

                    def store(t, p):
                        sp.wait_ge(S[f"y_in{p}"], 1)
                        sp.sem_inc(S[f"y_in{p}"], -1)
                        sp.dma_start(self.yslots[bass.ds(P * t, P), :], yt[p][:]).then_inc(S[f"y_out{p}"], 16)
                    load(0, 0, True)
                    load(1, 1, True)
                    load(2, 0)
                    with sp.Fori(0, TILES // 2 - 2) as u:
                        for p in range(2):
                            load(2 * u + p + 3, 1 - p)
                            store(2 * u + p, p)
                    load(TILES - 1, 1)
                    for t in range(TILES - 4, TILES):
                        store(t, t % 2)
                    for p in range(2):
                        sp.wait_ge(S[f"y_out{p}"], 16)
                        sp.sem_inc(S[f"y_out{p}"], -16)

                @block.scalar
                def _(act):
                    def gelu(p):
                        for i in range(2):
                            act.wait_ge(S[f"h_ps{p}"], 1)
                            act.sem_inc(S[f"h_ps{p}"], -1)
                            act.activation(hid[p][:, HF * i:HF * i + HF], ps[2 * p + i][:, 0:HF],
                                           ACT.Gelu_apprx_tanh).then_inc(S[f"h_in{p}"], 1)
                    with act.Fori(0, TILES // 2) as _u:
                        gelu(0)
                        gelu(1)

                @block.vector
                def _(v):
                    def own(i):
                        i.then_inc(T["dve"], 1)
                        v.wait_ge(T["dve"], 1)
                        v.sem_inc(T["dve"], -1)

                    def zT_evac(p):
                        v.wait_ge(S[f"zT_ps{p}"], 1)
                        v.sem_inc(S[f"zT_ps{p}"], -1)
                        v.tensor_copy(zT[p][0:DH, :], ps[6 + p][0:DH, 0:2 * P]).then_inc(S[f"zT_in{p}"], 1)

                    def hT_evac(p):
                        for i in range(2):
                            v.wait_ge(S[f"hT_ps{p}"], 1)
                            v.sem_inc(S[f"hT_ps{p}"], -1)
                            v.tensor_copy(hT[p][:, HF * i:HF * i + HF], ps[2 * p + i][:, 0:HF]).then_inc(S[f"hT_in{p}"], 1)

                    def y_evac(p, first=False):
                        v.wait_ge(S[f"y_ps{p}"], 1)
                        v.sem_inc(S[f"y_ps{p}"], -1)
                        if not first:
                            v.wait_ge(S[f"y_out{p}"], 16)
                            v.sem_inc(S[f"y_out{p}"], -16)
                        v.tensor_copy(yt[p][:], ps[4 + p][:, 0:D]).then_inc(S[f"y_in{p}"], 1)

                    def recur(s):
                        own(v.tensor_tensor(sq[:], state[:, bass.ds(4 * s - 4, 2)], state[:, bass.ds(4 * s - 4, 2)], ALU.mult))
                        own(v.tensor_tensor(nrm2[:], sq[:, 0:1], sq[:, 1:2], ALU.add))
                        own(v.reciprocal(inv[:], nrm2[:]))
                        own(v.scalar_tensor_tensor(out=state[:, bass.ds(4 * s, 4)], in0=state[:, bass.ds(4 * s - 4, 4)],
                                                   scalar=inv[:], in1=coef[:, bass.ds(4 * s, 4)], op0=ALU.mult, op1=ALU.add))
                    zT_evac(0)
                    zT_evac(1)
                    for p in range(2):
                        zT_evac(p)
                        hT_evac(p)
                        y_evac(p, True)
                        recur(p + 1)
                    with v.Fori(1, TILES // 2 - 1) as u:
                        for p in range(2):
                            zT_evac(p)
                            hT_evac(p)
                            y_evac(p)
                            recur(2 * u + p + 1)
                    for p in range(2):
                        hT_evac(p)
                        y_evac(p)

                @block.tensor
                def _(pe):
                    def turn(p):
                        pe.wait_ge(S[f"zt_in{p}"], 16)
                        pe.sem_inc(S[f"zt_in{p}"], -16)
                        for c in range(2):
                            last = pe.transpose(ps[6 + p][0:DH, P * c:P * c + P], zt[p][:, DH * c:DH * c + DH], self.c("ident"))
                        last.then_inc(S[f"zT_ps{p}"], 1)

                    def expert_of(t):
                        return pe.value_load(tile_expert[0:1, bass.ds(t, 1)], min_val=0, max_val=E - 1)

                    def up(t, p, free=True):
                        e = expert_of(t)
                        pe.wait_ge(S[f"zT_in{p}"], 1)
                        pe.sem_inc(S[f"zT_in{p}"], -1)
                        if free:
                            pe.sem_inc(S[f"zt_free{p}"], 1)
                        for i in range(2):
                            for c in range(2):
                                k = DH + c
                                last = pe.matmul(ps[2 * p + i][:, 0:HF], zT[p][0:k, P * c:P * c + P],
                                                 self.w1[0:k, bass.ds(e * (2 * F) + (c * F + i * HF), HF)],
                                                 start=(c == 0), stop=(c == 1))
                            last.then_inc(S[f"h_ps{p}"], 1)

                    def hidden_T(p):
                        for i in range(2):
                            pe.wait_ge(S[f"h_in{p}"], 1)
                            pe.sem_inc(S[f"h_in{p}"], -1)
                            for m in range(3):
                                n = 3 * i + m
                                last = pe.transpose(ps[2 * p + i][:, P * m:P * m + P], hid[p][:, P * n:P * n + P], self.c("ident"))
                            last.then_inc(S[f"hT_ps{p}"], 1)

                    def down(t, p):
                        e = expert_of(t)
                        pe.wait_ge(S[f"hT_in{p}"], 2)
                        pe.sem_inc(S[f"hT_in{p}"], -2)
                        for m in range(MT):
                            last = pe.matmul(ps[4 + p][:, 0:D], hT[p][:, P * m:P * m + P],
                                             w2[:, bass.ds(e * (MT * D) + m * D, D)], start=(m == 0), stop=(m == MT - 1))
                        last.then_inc(S[f"y_ps{p}"], 1)
                    turn(0)
                    turn(1)
                    up(0, 0)
                    with pe.Fori(0, TILES // 2 - 1) as u:
                        for p in range(2):
                            turn(p)
                            hidden_T(p)
                            up(2 * u + p + 1, 1 - p)
                            down(2 * u + p, p)
                    hidden_T(0)
                    up(TILES - 1, 1, free=False)
                    down(TILES - 2, 0)
                    hidden_T(1)
                    down(TILES - 1, 1)

            with nc.Block() as block:
                @block.tensor
                def _(pe):
                    pe.wait_ge(S2["state_split"], 1)
                    pe.sem_inc(S2["state_split"], -1)
                    for i in range(2):
                        pe.transpose(ps[i][:, 0:P], dcomp[i][:], self.c("ident")).then_inc(S2["state_T"], 1)
                    for i in range(2):
                        pe.wait_ge(S2["state_in"], 1)
                        pe.sem_inc(S2["state_in"], -1)
                        pe.matmul(ps[2 + i][:, 0:B], self.c("anti"), xs[i][:, B:2 * B], start=True, stop=True).then_inc(S2["e_ps"], 1)

                @block.vector
                def _(v):
                    def own(i):
                        i.then_inc(T["dve"], 1)
                        v.wait_ge(T["dve"], 1)
                        v.sem_inc(T["dve"], -1)
                    v.tensor_copy(dcomp[0][:].rearrange("p (u c) -> p u c", c=2), places(state, 0, 2, P))
                    v.tensor_copy(dcomp[1][:].rearrange("p (u c) -> p u c", c=2),
                                  state[:, 0:4 * P].rearrange("p (u c) -> p u c", c=8)[:, :, 1:6:4]).then_inc(S2["state_split"], 1)
                    for i in range(2):
                        v.wait_ge(S2["state_T"], 1)
                        v.sem_inc(S2["state_T"], -1)
                        v.tensor_copy(xs[i][:], ps[i][:, 0:P]).then_inc(S2["state_in"], 1)
                    re, im, n, t = (f[:] for f in fin)
                    v.wait_ge(S2["e_ps"], 1)
                    v.sem_inc(S2["e_ps"], -1)
                    own(v.tensor_tensor(re, ps[2][:, 0:B], xs[0][:, 0:B], ALU.add))
                    own(v.tensor_tensor(re, re, vclip[:], ALU.subtract))
                    own(v.tensor_scalar(re, re, 2.0, None, ALU.add))
                    v.wait_ge(S2["e_ps"], 1)
                    v.sem_inc(S2["e_ps"], -1)
                    own(v.tensor_tensor(im, ps[3][:, 0:B], xs[1][:, 0:B], ALU.add))
                    own(v.tensor_scalar(im, im, 1.0, None, ALU.add))
                    own(v.tensor_tensor(n, re, re, ALU.mult))
                    own(v.tensor_tensor(t, im, im, ALU.mult))
                    own(v.tensor_tensor(n, n, t, ALU.add))
                    own(v.reciprocal(t, n))
                    own(v.tensor_tensor(re, re, t, ALU.mult))
                    own(v.tensor_scalar(im, im, -1.0, None, ALU.mult))
                    own(v.tensor_tensor(im, im, t, ALU.mult))
                    f3 = self.feats[:].rearrange("p (b c) -> p b c", c=11)
                    v.tensor_scalar(f3[:, :, 8], re, -FEAT_CLAMP, FEAT_CLAMP, ALU.max, ALU.min)
                    own(v.tensor_scalar(f3[:, :, 9], im, -FEAT_CLAMP, FEAT_CLAMP, ALU.max, ALU.min))
                    own(v.tensor_tensor(self.mixrows[:], self.mixrows[:], self.mixscale[:], ALU.mult))

    def differential_attention(self):
        nc, ins, ps, h, T = self.nc, self.ins, self.ps, self.h, self.S
        with ExitStack() as ctx:
            def sb(name, shape, dt=F32):
                return ctx.enter_context(nc.sbuf_tensor(name, shape, dt))
            idx = [sb(f"idx{i}", [P, 1], I32) for i in range(2)]
            yrow = [sb(f"yrow{i}", [P, D]) for i in range(2)]
            w2s = sb("c_w2s", [P, 2])
            fcur = sb("fcur", [P, 11])
            fT = sb("fT", [11, P])
            y = sb("c_y", [P, D])
            yT = sb("c_yT", [DH + 1, 2 * P])
            qT, kT = sb("c_qT", [P, F]), sb("c_kT", [P, 2 * P])
            vv = sb("c_v", [P, D])
            sc = sb("sc", [P, NSUB * P])
            nmax, sums, rs = sb("c_nmax", [P, NSUB]), sb("c_sums", [P, NSUB]), sb("c_rs", [P, NSUB])
            diff = sb("diff", [P, H1 * P])
            diffT = sb("diffT", [P, H1 * P])
            cx, cx2 = sb("cx", [P, D]), sb("cx2", [P, D])
            cxT = sb("cxT", [DH + 1, 2 * P])
            ms, rr = sb("ms", [P, H1]), sb("rr", [P, H1])
            lam = sb("lam", [P, 8])
            ljunk = sb("ljunk", [P, HS])
            S = self.sems(ctx, "lam_in", "lam_e", "y_in", "mixed", "f_free", "f_ready", "fT_ps", "fT_in", "f_ps",
                          "y_ready", "y_free", "yT_ps", "yT_in", "q_ps", "q_in", "k_ps", "k_in", "v_ps", "v_in",
                          "s_ps", "clamped", "nmax", "exp_done", "odd_ready", "odd_scaled", "diff_ready", "yT_read", "dT_ps", "dT_in",
                          "ctx_ps", "ms_ready", "rr_ready", "cx_ready", "cxT_ps", "cxT_in", "o_ps", "o_free", "fcur_free")
            block = ctx.enter_context(nc.Block())

            @block.gpsimd
            def _(g):
                def gather(b):
                    for i in range(2):
                        g.tensor_copy(idx[i][:], self.yrows[:, bass.ds(2 * b + i, 1)]).then_inc(T["pool"], 1)
                        g.wait_ge(T["pool"], 1)
                        g.sem_inc(T["pool"], -1)
                        g.indirect_dma_start(out=yrow[i][:], out_offset=None, in_=self.yslots,
                                             in_offset=bass.IndirectOffsetOnAxis(ap=idx[i][:, 0:1], axis=0)).then_inc(S["y_in"], 16)

                def mix(b):
                    hb = h[:, bass.ds(b * D, D)]
                    g.wait_ge(S["y_in"], 32 * (b + 1))
                    g.tensor_copy(w2s[:], self.mixw[:, bass.ds(2 * b, 2)]).then_inc(T["pool"], 1)
                    g.wait_ge(T["pool"], 1)
                    g.sem_inc(T["pool"], -1)
                    for i in range(2):
                        g.tensor_scalar(yrow[i][:], yrow[i][:], w2s[:, i:i + 1], None, ALU.mult).then_inc(T["pool"], 1)
                        g.wait_ge(T["pool"], 1)
                        g.sem_inc(T["pool"], -1)
                        g.tensor_tensor(hb, hb, yrow[i][:], ALU.add).then_inc(T["pool"], 1)
                        g.wait_ge(T["pool"], 1)
                        g.sem_inc(T["pool"], -1)
                    g.sem_inc(S["mixed"], 1)

                def norm():
                    inverse_root(g, self.ln, T, self.c("eps5"), self.c("neg_half"))

                def scale_odd(r):
                    g.wait_ge(S["odd_ready"], 1)
                    g.sem_inc(S["odd_ready"], -1)
                    n0, n1 = ROUNDS[r]
                    o = sc[:].rearrange("p (h e t) -> p e h t", e=2, t=P)[:, 1, n0:n1, :]
                    c_ = rs[:].rearrange("p (h e) -> p e h", e=2)[:, 1, n0:n1]
                    g.tensor_tensor(o, o, c_.unsqueeze(2).to_broadcast([P, n1 - n0, P]), ALU.mult).then_inc(S["odd_scaled"], 1)

                def rms():
                    g.wait_ge(S["ms_ready"], 1)
                    g.sem_inc(S["ms_ready"], -1)
                    g.tensor_tensor(rr[:], ms[:], self.c("neg_half").to_broadcast([P, H1]), ALU.pow).then_inc(S["rr_ready"], 1)

                gather(0)
                mix(0)
                gather(1)
                mix(1)
                norm()
                gather(2)

                def step(b, prev, cur, one, two, three):
                    if one:
                        norm()
                    if two:
                        mix(b + 2)
                    if cur:
                        scale_odd(0)
                    if prev:
                        rms()
                    if cur:
                        scale_odd(1)
                    if three:
                        gather(b + 3)
                step(0, False, True, True, True, True)
                with g.Fori(1, B - 3) as b:
                    step(b, True, True, True, True, True)
                step(B - 3, True, True, True, True, False)
                step(B - 2, True, True, True, False, False)
                step(B - 1, True, True, False, False, False)
                step(B, True, False, False, False, False)

            @block.scalar
            def _(act):
                act.wait_ge(S["lam_in"], 1)
                act.sem_inc(S["lam_in"], -1)
                act.activation(lam[:, 2:4], lam[:, 0:2], ACT.Exp).then_inc(S["lam_e"], 1)

                def fT_evac():
                    act.wait_ge(S["fT_ps"], 1)
                    act.sem_inc(S["fT_ps"], -1)
                    act.activation(fT[:], ps[2][0:11, 0:P], ACT.Copy).then_inc(S["fT_in"], 1)

                def yT_evac():
                    act.wait_ge(S["yT_ps"], 1)
                    act.sem_inc(S["yT_ps"], -1)
                    act.activation(yT[0:DH, :], ps[7][0:DH, 0:2 * P], ACT.Copy).then_inc(S["yT_in"], 1)

                def kq_evac():
                    act.wait_ge(S["k_ps"], 1)
                    act.sem_inc(S["k_ps"], -1)
                    act.activation(kT[:], ps[6][:, 0:2 * P], ACT.Copy).then_inc(S["k_in"], 1)
                    act.wait_ge(S["q_ps"], 1)
                    act.sem_inc(S["q_ps"], -1)
                    act.activation(qT[:, 0:4 * P], ps[4][:], ACT.Copy, scale=HS ** -0.5)
                    act.activation(qT[:, 4 * P:6 * P], ps[5][:, 0:2 * P], ACT.Copy, scale=HS ** -0.5).then_inc(S["q_in"], 1)

                def exps(part):
                    act.wait_ge(S["nmax"], 1)
                    act.sem_inc(S["nmax"], -1)
                    for s in range(8 * part, 8 * part + 8):
                        last = act.activation(sc[:, P * s:P * s + P], sc[:, P * s:P * s + P], ACT.Exp,
                                              bias=nmax[:, s:s + 1], accum_out=sums[:, s:s + 1])
                    if part:
                        last.then_inc(S["exp_done"], 1)

                def dT_evac(r):
                    act.wait_ge(S["dT_ps"], 1)
                    act.sem_inc(S["dT_ps"], -1)
                    for bank in (4, 5) if r == 0 else (6,):
                        a = 4 * (bank - 4)
                        last = act.activation(diffT[:, P * a:P * (a + 4)], ps[bank][:], ACT.Copy)
                    last.then_inc(S["dT_in"], 1)

                def cxT_evac():
                    act.wait_ge(S["cxT_ps"], 1)
                    act.sem_inc(S["cxT_ps"], -1)
                    act.activation(cxT[0:DH, :], ps[3][0:DH, 0:2 * P], ACT.Copy).then_inc(S["cxT_in"], 1)

                fT_evac()
                yT_evac()
                kq_evac()
                fT_evac()

                def step(prev, cur, one, two):
                    if cur:
                        exps(0)
                    if prev:
                        dT_evac(0)
                    if one:
                        yT_evac()
                    if prev:
                        dT_evac(1)
                    if cur:
                        exps(1)
                        exps(2)
                    if one:
                        kq_evac()
                    if two:
                        fT_evac()
                    if prev:
                        cxT_evac()
                step(False, True, True, True)
                with act.Fori(1, B - 2) as _b:
                    step(True, True, True, True)
                step(True, True, True, False)
                step(True, True, False, False)
                step(True, False, False, False)

            @block.vector
            def _(v):
                def own(i):
                    i.then_inc(T["dve"], 1)
                    v.wait_ge(T["dve"], 1)
                    v.sem_inc(T["dve"], -1)

                v.memset(yT[DH:DH + 1, :], 1.0)
                v.memset(cxT[DH:DH + 1, :], 1.0)
                lr = self.r("lam")
                for i in range(2):
                    own(v.tensor_tensor_reduce(out=ljunk[:], in0=lr[:, 16 * i:16 * i + 8], in1=lr[:, 16 * i + 8:16 * i + 16], scale=1.0,
                                               scalar=0.0, op0=ALU.mult, op1=ALU.add, accum_out=lam[:, i:i + 1]))
                v.sem_inc(S["lam_in"], 1)
                own(v.tensor_scalar(self.r("subln"), self.r("subln"), 1.0 - LAMBDA_INIT, None, ALU.mult))
                v.wait_ge(S["lam_e"], 1)
                v.sem_inc(S["lam_e"], -1)
                own(v.tensor_tensor(lam[:, 4:5], lam[:, 3:4], lam[:, 2:3], ALU.subtract))
                own(v.tensor_scalar(lam[:, 5:6], lam[:, 4:5], -LAMBDA_INIT, None, ALU.add))

                def features(b, first=False):
                    if not first:
                        v.wait_ge(S["fcur_free"], 1)
                        v.sem_inc(S["fcur_free"], -1)
                    v.tensor_copy(fcur[:], self.feats[:, bass.ds(11 * b, 11)]).then_inc(S["f_ready"], 1)

                def add_spectral(b):
                    hb = h[:, bass.ds(b * D, D)]
                    v.wait_ge(S["mixed"], 1)
                    v.sem_inc(S["mixed"], -1)
                    v.wait_ge(S["f_ps"], 1)
                    v.sem_inc(S["f_ps"], -1)
                    own(v.tensor_tensor(hb, hb, ps[2][:, 0:D], ALU.add))
                    v.sem_inc(S["f_free"], 1)
                    norm_statistics(v, self.ln, T, hb)

                def make_y(b, first=False):
                    if not first:
                        v.wait_ge(S["y_free"], 1)
                        v.sem_inc(S["y_free"], -1)
                    norm_apply(v, self.ln, T, h[:, bass.ds(b * D, D)], y[:], S["y_ready"])

                def v_evac():
                    v.wait_ge(S["v_ps"], 1)
                    v.sem_inc(S["v_ps"], -1)
                    v.tensor_copy(vv[:], ps[7][:, 2 * P:2 * P + D]).then_inc(S["v_in"], 1)

                def clamp(dst, q, n):
                    v.wait_ge(S["s_ps"], 1)
                    v.sem_inc(S["s_ps"], -1)
                    v.tensor_scalar(dst, ps[q][:, 0:n * P].rearrange("p (m t) -> p m t", t=P), -BIG, BIG,
                                    ALU.max, ALU.min).then_inc(S["clamped"], 1)

                def maxima(part):
                    own(v.tensor_copy(ljunk[:, 0:1], lam[:, 5:6]))
                    s = slice(8 * part, 8 * part + 8)
                    v.tensor_reduce(out=nmax[:, s], in_=sc[:].rearrange("p (s t) -> p s t", t=P)[:, s],
                                    op=ALU.max, axis=AX, negate=True).then_inc(S["nmax"], 1)

                def softmax_front(between):
                    s3 = sc[:].rearrange("p (s t) -> p s t", t=P)
                    for q in range(4):
                        clamp(s3[:, QUAD * q:QUAD * q + QUAD], q, QUAD)
                        if q % 2:
                            maxima(q // 2)
                            if q == 1:
                                between()
                    late = s3[:, 4 * QUAD:].rearrange("p (g m i) t -> p g i m t", g=2, i=2)
                    for q in range(4):
                        clamp(late[:, q % 2, q // 2], q, 2)
                    maxima(2)

                def odd_scales(r):
                    v.wait_ge(S["exp_done"], 1)
                    v.sem_inc(S["exp_done"], -1)
                    n0, n1 = ROUNDS[r]
                    own(v.reciprocal(rs[:, 2 * n0:2 * n1], sums[:, 2 * n0:2 * n1]))
                    odd = rs[:].rearrange("p (h e) -> p e h", e=2)[:, 1, n0:n1]
                    v.tensor_scalar(odd, odd, lam[:, 5:6], None, ALU.mult).then_inc(S["odd_ready"], 1)

                def differences(r):
                    v.wait_ge(S["odd_scaled"], 1)
                    v.sem_inc(S["odd_scaled"], -1)
                    for n in range(*ROUNDS[r]):
                        s = 2 * n
                        last = v.scalar_tensor_tensor(out=diff[:, P * n:P * n + P], in0=sc[:, P * s:P * s + P],
                                                      scalar=rs[:, s:s + 1], in1=sc[:, P * (s + 1):P * (s + 2)],
                                                      op0=ALU.mult, op1=ALU.add)
                    own(last)
                    v.sem_inc(S["diff_ready"], 1)

                def mean_squares(cur):
                    v.wait_ge(S["ctx_ps"], 1)
                    v.sem_inc(S["ctx_ps"], -1)
                    own(v.tensor_copy(cx[:], ps[0][:, 0:D]))
                    if cur:
                        v_evac()
                    own(v.tensor_tensor(cx2[:], cx[:], cx[:], ALU.mult))
                    own(v.tensor_reduce(out=ms[:], in_=cx2[:].rearrange("p (h d) -> p h d", d=HV), op=ALU.add, axis=AX))
                    v.tensor_scalar(ms[:], ms[:], 1.0 / HV, 1e-5, ALU.mult, ALU.add).then_inc(S["ms_ready"], 1)

                def scale_context():
                    v.wait_ge(S["rr_ready"], 1)
                    v.sem_inc(S["rr_ready"], -1)
                    c3 = cx[:].rearrange("p (h d) -> p h d", d=HV)
                    own(v.tensor_tensor(c3, c3, rr[:].unsqueeze(2).to_broadcast([P, H1, HV]), ALU.mult))
                    v.tensor_tensor(cx[:], cx[:], self.r("subln"), ALU.mult).then_inc(S["cx_ready"], 1)

                def add_out(b):
                    hb = h[:, bass.ds(b * D, D)]
                    v.wait_ge(S["o_ps"], 1)
                    v.sem_inc(S["o_ps"], -1)
                    own(v.tensor_tensor(hb, hb, ps[3][:, 0:D], ALU.add))
                    v.sem_inc(S["o_free"], 1)

                features(0, first=True)
                add_spectral(0)
                make_y(0, first=True)
                features(1)

                def step(b, prev, cur, one, two, second=False):
                    if one:
                        add_spectral(b + 1)
                    if prev and not second:
                        add_out(b - 2)

                    def y_done():
                        if one:
                            make_y(b + 1)
                    if cur:
                        softmax_front(y_done)
                        odd_scales(0)
                    if prev:
                        mean_squares(cur)
                    elif cur:
                        v.wait_ge(S["yT_read"], 1)
                        v.sem_inc(S["yT_read"], -1)
                        v_evac()
                    if two:
                        features(b + 2)
                    if cur:
                        differences(0)
                        odd_scales(1)
                    if prev:
                        scale_context()
                    if cur:
                        differences(1)
                step(0, False, True, True, True)
                step(1, True, True, True, True, second=True)
                with v.Fori(2, B - 2) as b:
                    step(b, True, True, True, True)
                step(B - 2, True, True, True, False)
                step(B - 1, True, True, False, False)
                step(B, True, False, False, False)
                add_out(B - 1)

            @block.tensor
            def _(pe):
                def features_T():
                    pe.wait_ge(S["f_ready"], 1)
                    pe.sem_inc(S["f_ready"], -1)
                    pe.transpose(ps[2][0:11, 0:P], fcur[:], self.c("ident")).then_inc(S["fT_ps"], 1)

                def features():
                    pe.wait_ge(S["fT_in"], 1)
                    pe.sem_inc(S["fT_in"], -1)
                    pe.sem_inc(S["fcur_free"], 1)
                    pe.matmul(ps[2][:, 0:D], fT[:], self.mixrows[:], start=True, stop=True).then_inc(S["f_ps"], 1)

                def y_T():
                    pe.wait_ge(S["y_ready"], 1)
                    pe.sem_inc(S["y_ready"], -1)
                    for c in range(2):
                        last = pe.transpose(ps[7][0:DH, P * c:P * c + P], y[:, DH * c:DH * c + DH], self.c("ident"))
                    last.then_inc(S["yT_ps"], 1)

                def kq_proj(tell=False):
                    pe.wait_ge(S["yT_in"], 1)
                    pe.sem_inc(S["yT_in"], -1)
                    pe.sem_inc(S["y_free"], 1)
                    if tell:
                        pe.sem_inc(S["yT_read"], 1)
                    for w, bank, tiles, ready in ((self.w_k, 6, 2, "k_ps"), (self.w_q, 4, MT, "q_ps")):
                        for m in range(tiles):
                            for c in range(2):
                                k = DH + c
                                a = (c * tiles + m) * P
                                last = pe.matmul(ps[bank + m // 4][:, P * (m % 4):P * (m % 4) + P], w[0:k, a:a + P],
                                                 yT[0:k, P * c:P * c + P], start=(c == 0), stop=(c == 1))
                        last.then_inc(S[ready], 1)

                def v_proj():
                    for c in range(2):
                        k = DH + c
                        last = pe.matmul(ps[7][:, 2 * P:2 * P + D], yT[0:k, P * c:P * c + P], self.w_vo[0:k, c * D:c * D + D],
                                         start=(c == 0), stop=(c == 1))
                    last.then_inc(S["v_ps"], 1)

                def scores(r, q):
                    rows = slice(32 * q, 32 * q + 32)
                    for m, t in enumerate(range(QUAD) if r == 0 else range(QUAD, MT)):
                        last = pe.matmul(ps[q][:, P * m:P * m + P], qT[rows, P * t:P * t + P],
                                         kT[rows, P * r:P * r + P], start=True, stop=True)
                    last.then_inc(S["s_ps"], 1)

                def diff_T(r):
                    pe.wait_ge(S["diff_ready"], 1)
                    pe.sem_inc(S["diff_ready"], -1)
                    for n in range(*ROUNDS[r]):
                        last = pe.transpose(ps[4 + n // 4][:, P * (n % 4):P * (n % 4) + P],
                                            diff[:, P * n:P * n + P], self.c("ident"))
                    last.then_inc(S["dT_ps"], 1)

                def contexts():
                    for r in range(2):
                        pe.wait_ge(S["dT_in"], 1)
                        pe.sem_inc(S["dT_in"], -1)
                        for n in range(*ROUNDS[r]):
                            last = pe.matmul(ps[0][:, HV * n:HV * n + HV], diffT[:, P * n:P * n + P], vv[:, HV * n:HV * n + HV],
                                             start=True, stop=True)
                    last.then_inc(S["ctx_ps"], 1)

                def context_T():
                    pe.wait_ge(S["cx_ready"], 1)
                    pe.sem_inc(S["cx_ready"], -1)
                    for c in range(2):
                        last = pe.transpose(ps[3][0:DH, P * c:P * c + P], cx[:, DH * c:DH * c + DH], self.c("ident"))
                    last.then_inc(S["cxT_ps"], 1)

                def out_proj():
                    pe.wait_ge(S["cxT_in"], 1)
                    pe.sem_inc(S["cxT_in"], -1)
                    for c in range(2):
                        k = DH + c
                        last = pe.matmul(ps[3][:, 0:D], cxT[0:k, P * c:P * c + P], self.w_vo[0:k, 2 * D + c * D:2 * D + c * D + D],
                                         start=(c == 0), stop=(c == 1))
                    last.then_inc(S["o_ps"], 1)

                features_T()
                features()
                y_T()
                kq_proj()
                pe.wait_ge(S["f_free"], 1)
                pe.sem_inc(S["f_free"], -1)
                features_T()
                features()

                def step(prev, cur, one, two, second=False, spectral=True):
                    if cur:
                        pe.wait_ge(S["k_in"], 1)
                        pe.sem_inc(S["k_in"], -1)
                        pe.wait_ge(S["q_in"], 1)
                        pe.sem_inc(S["q_in"], -1)
                        for q in range(4):
                            if q == 2 and spectral:
                                pe.wait_ge(S["f_free"], 1)
                                pe.sem_inc(S["f_free"], -1)
                            if q == 3 and prev and not second:
                                pe.wait_ge(S["o_free"], 1)
                                pe.sem_inc(S["o_free"], -1)
                            scores(0, q)
                        v_proj()
                    if prev:
                        diff_T(0)
                    if one:
                        y_T()
                    if prev:
                        diff_T(1)
                    if cur:
                        for q in range(4):
                            pe.wait_ge(S["clamped"], 1)
                            pe.sem_inc(S["clamped"], -1)
                            scores(1, q)
                        pe.wait_ge(S["clamped"], 1)
                        pe.sem_inc(S["clamped"], -1)
                    if prev:
                        contexts()
                    if one:
                        kq_proj(tell=not prev)
                    if cur:
                        pe.wait_ge(S["clamped"], 3)
                        pe.sem_inc(S["clamped"], -3)
                    if two:
                        features_T()
                    if prev:
                        if not cur:
                            pe.wait_ge(S["o_free"], 1)
                            pe.sem_inc(S["o_free"], -1)
                        context_T()
                    if two:
                        features()
                    if prev:
                        out_proj()
                    if cur:
                        pe.wait_ge(S["v_in"], 1)
                        pe.sem_inc(S["v_in"], -1)
                step(False, True, True, True)
                step(True, True, True, True, second=True)
                with pe.Fori(2, B - 2) as _b:
                    step(True, True, True, True)
                step(True, True, True, False)
                step(True, True, False, False, spectral=False)
                step(True, False, False, False)
                pe.wait_ge(S["o_free"], 1)
                pe.sem_inc(S["o_free"], -1)

    def feed_forward(self):
        nc, ins, ps, h, T = self.nc, self.ins, self.ps, self.h, self.S
        NG, W = B // GRP, GRP * P
        with ExitStack() as ctx:
            def sb(name, shape, dt=F32):
                return ctx.enter_context(nc.sbuf_tensor(name, shape, dt))
            a2 = sb("a2", [P, 5 * MT * D])
            gates_w = sb("gates_w", [DH, 2 * 2 * NCLS])
            z4 = sb("z4", [P, GRP * D])
            zT = sb("d_zT", [DH + 1, 2 * W])
            zc = sb("zc", [DH + 1, 2 * NCLS * B])
            hT = sb("d_hT", [P, MT * W])
            ob = sb("ob", [P, GRP * D])
            hc = sb("hc", [B, NCLS * D])
            hcT = [sb(f"hcT{i}", [P, MT * B]) for i in range(2)]
            gt = [sb(f"gt{i}", [B, 2 * NCLS]) for i in range(3)]
            g6 = [sb(f"g6_{i}", [B, NCLS]) for i in range(3)]
            eo = sb("eo", [B, D])
            S = self.sems(ctx, "cls_loaded", "gelu_warm", "z_ready", "z_free", "zT_ps", "zT_in", "zT_free", "h_ps", "h_in", "y_ps", "y_in",
                          "ob_ready", "ob_out", "hc_in", "gates_ps", "gates_m", "gates_e", "zc_ready", "u_ps", "u_in", "e_ps", "e_free", "cls_done")

            with nc.Block() as block:
                @block.sync
                def _(sp):
                    sp.dma_start(self.w1[:, 0:5 * 2 * F], ins["a1"]).then_inc(S["cls_loaded"], 16)
                    sp.dma_start(a2[:], ins["a2"]).then_inc(S["cls_loaded"], 16)
                    sp.dma_start(gates_w[:], ins["gates_w"]).then_inc(S["cls_loaded"], 16)
                    for i in range(NCLS):
                        sp.dma_start(hc[:, D * i:D * i + D], h[i:i + 1, :].rearrange("o (b d) -> o b d", d=D)).then_inc(S["hc_in"], 16)
                    o = ob[NCLS:P, :].rearrange("p (b d) -> p b d", d=D)
                    with sp.Fori(0, NG) as g:
                        sp.wait_ge(S["ob_ready"], 1)
                        sp.sem_inc(S["ob_ready"], -1)
                        sp.dma_start(self.out[bass.ds(GRP * g, GRP), NCLS:P, :].rearrange("b s d -> s b d"), o).then_inc(S["ob_out"], 16)
                    sp.wait_ge(S["cls_done"], 1)
                    sp.sem_inc(S["cls_done"], -1)
                    sp.wait_ge(S["ob_out"], 16)
                    sp.sem_inc(S["ob_out"], -16)
                    sp.dma_start(self.out[:, 0:NCLS, :], hc[:].rearrange("p (i d) -> p i d", d=D)).then_inc(S["ob_out"], 16)
                    sp.wait_ge(S["ob_out"], 16)
                    sp.sem_inc(S["ob_out"], -16)

                @block.gpsimd
                def _(g):
                    with g.Fori(0, B) as _b:
                        inverse_root(g, self.ln, T, self.c("eps5"), self.c("neg_half"))

                @block.scalar
                def _(act):
                    act.activation(gt[2][:, 0:1], self.c("ones", slice(0, B))[:, 0:1], ACT.Gelu).then_inc(S["gelu_warm"], 1)
                    act.wait_ge(S["gelu_warm"], 1)

                    def group():
                        act.wait_ge(S["zT_ps"], 1)
                        act.sem_inc(S["zT_ps"], -1)
                        for c in range(2):
                            last = act.activation(zT[0:DH, W * c:W * c + W], ps[c][0:DH, :], ACT.Copy)
                        last.then_inc(S["zT_in"], 1)

                    def gelus():
                        for m in range(MT):
                            act.wait_ge(S["h_ps"], 1)
                            act.sem_inc(S["h_ps"], -1)
                            act.activation(hT[:, W * m:W * m + W], ps[2 + (m + 2) % MT][:], ACT.Gelu).then_inc(S["h_in"], 1)
                    group()
                    with act.Fori(0, NG - 1) as _g:
                        gelus()
                        group()
                    gelus()
                    act.wait_ge(S["gates_m"], 1)
                    act.sem_inc(S["gates_m"], -1)
                    act.activation(gt[1][:], gt[0][:], ACT.Exp).then_inc(S["gates_e"], 1)
                    for n in range(2 * NCLS):
                        act.wait_ge(S["u_ps"], 1)
                        act.sem_inc(S["u_ps"], -1)
                        act.activation(hcT[n % 2][:], ps[4 + n % 2][:, 0:MT * B], ACT.Gelu).then_inc(S["u_in"], 1)

                @block.vector
                def _(v):
                    def own(i):
                        i.then_inc(T["dve"], 1)
                        v.wait_ge(T["dve"], 1)
                        v.sem_inc(T["dve"], -1)
                    for c in range(2):
                        v.memset(zT[DH:DH + 1, W * c:W * c + W], 1.0)
                    v.memset(zc[DH:DH + 1, :], 1.0)

                    def norms(g):
                        for j in range(GRP):
                            layer_norm(v, self.ln, T, h[:, bass.ds((GRP * g + j) * D, D)], z4[:, D * j:D * j + D], S["z_ready"])

                    def keep_class_tokens(g):
                        v.wait_ge(S["zT_free"], 1)
                        v.sem_inc(S["zT_free"], -1)
                        z3 = zT[0:DH, :].rearrange("p (c b t) -> p c b t", c=2, t=P)
                        zc3 = zc[0:DH, :].rearrange("p (b c i) -> p b c i", c=2, i=NCLS)
                        for c in range(2):
                            last = v.tensor_copy(zc3[:, bass.ds(GRP * g, GRP), c, :], z3[:, c, :, 0:NCLS])
                        last.then_inc(S["zc_ready"], 1)

                    def outputs(g, first=False):
                        for j in range(GRP):
                            if j % 2 == 0:
                                v.wait_ge(S["y_ps"], 1)
                                v.sem_inc(S["y_ps"], -1)
                            if j == 0 and not first:
                                v.wait_ge(S["ob_out"], 16)
                                v.sem_inc(S["ob_out"], -16)
                            o = ob[:, D * j:D * j + D]
                            own(v.tensor_tensor(o, ps[2 + j // 2][:, D * (j % 2):D * (j % 2) + D], self.r("moe0_b2"), ALU.add))
                            i = v.tensor_tensor(o, o, h[:, bass.ds((GRP * g + j) * D, D)], ALU.add)
                            if j % 2:
                                own(i)
                                v.sem_inc(S["y_in"], 1)
                        v.sem_inc(S["ob_ready"], 1)
                    norms(0)
                    keep_class_tokens(0)
                    v.wait_ge(S["z_free"], 1)
                    v.sem_inc(S["z_free"], -1)
                    norms(1)
                    keep_class_tokens(1)
                    outputs(0, first=True)
                    with v.Fori(1, NG - 1) as g:
                        v.wait_ge(S["z_free"], 1)
                        v.sem_inc(S["z_free"], -1)
                        norms(g + 1)
                        keep_class_tokens(g + 1)
                        outputs(g)
                    outputs(NG - 1)
                    l3, e3, m3 = (t[:].rearrange("p (i k) -> p i k", k=2) for t in gt)
                    mx, den, inv = (t[:] for t in g6)

                    def wide(a):
                        return a.unsqueeze(2).to_broadcast([B, NCLS, 2])
                    v.wait_ge(S["gates_ps"], 1)
                    v.sem_inc(S["gates_ps"], -1)
                    own(v.tensor_copy(gt[0][:], ps[0][0:B, 0:2 * NCLS]))
                    own(v.tensor_reduce(out=mx, in_=l3, op=ALU.max, axis=AX))
                    v.tensor_tensor(l3, l3, wide(mx), ALU.subtract).then_inc(S["gates_m"], 1)
                    v.wait_ge(S["gates_e"], 1)
                    v.sem_inc(S["gates_e"], -1)
                    own(v.tensor_reduce(out=den, in_=e3, op=ALU.add, axis=AX))
                    own(v.reciprocal(inv, den))
                    own(v.tensor_tensor(e3, e3, wide(inv), ALU.mult))
                    own(v.tensor_reduce(out=mx, in_=e3, op=ALU.min, axis=AX))
                    own(v.tensor_tensor(m3, e3, wide(mx), ALU.is_gt))
                    own(v.tensor_tensor(e3, e3, m3, ALU.mult))
                    own(v.tensor_reduce(out=den, in_=e3, op=ALU.add, axis=AX))
                    own(v.tensor_scalar(den, den, 1e-6, None, ALU.max))
                    own(v.reciprocal(inv, den))
                    own(v.tensor_tensor(e3, e3, wide(inv), ALU.mult))
                    v.wait_ge(S["hc_in"], 16 * NCLS)
                    for n in range(2 * NCLS):
                        i, k = n // 2, n % 2
                        c = CLS_PAIRS[i][k][1]
                        v.wait_ge(S["e_ps"], 1)
                        v.sem_inc(S["e_ps"], -1)
                        own(v.tensor_tensor(eo[:], ps[6 + n % 2][0:B, 0:D], self.r("a2_b")[0:B, D * c:D * c + D], ALU.add))
                        v.sem_inc(S["e_free"], 1)
                        hi = hc[:, D * i:D * i + D]
                        own(v.scalar_tensor_tensor(out=hi, in0=eo[:], scalar=gt[1][:, n:n + 1], in1=hi, op0=ALU.mult, op1=ALU.add))
                    v.sem_inc(S["cls_done"], 1)

                @block.tensor
                def _(pe):
                    ident = self.c("ident")

                    def turn():
                        pe.wait_ge(S["z_ready"], GRP)
                        pe.sem_inc(S["z_ready"], -GRP)
                        for c in range(2):
                            for j in range(GRP):
                                last = pe.transpose(ps[c][0:DH, P * j:P * j + P], z4[:, D * j + DH * c:D * j + DH * c + DH], ident)
                        last.then_inc(S["zT_ps"], 1)

                    def up(first=False):
                        for m in range(MT):
                            if not first and m == MT - 2:
                                pe.wait_ge(S["y_in"], 2)
                                pe.sem_inc(S["y_in"], -2)
                            for c in range(2):
                                k = DH + c
                                last = pe.matmul(ps[2 + (m + 2) % MT][:], self.w_up[0:k, c * F + m * P:c * F + m * P + P],
                                                 zT[0:k, W * c:W * c + W], start=(c == 0), stop=(c == 1))
                            last.then_inc(S["h_ps"], 1)

                    def turned():
                        pe.wait_ge(S["zT_in"], 1)
                        pe.sem_inc(S["zT_in"], -1)
                        pe.sem_inc(S["z_free"], 1)
                        pe.sem_inc(S["zT_free"], 1)

                    def down():
                        for j in range(GRP):
                            for m in range(MT):
                                last = pe.matmul(ps[2 + j // 2][:, D * (j % 2):D * (j % 2) + D], hT[:, W * m + P * j:W * m + P * j + P],
                                                 self.w_down[:, D * m:D * m + D], start=(m == 0), stop=(m == MT - 1))
                            if j % 2:
                                last.then_inc(S["y_ps"], 1)

                    turn()
                    turned()
                    up(first=True)

                    def step(more=True):
                        if more:
                            pe.wait_ge(S["zc_ready"], 1)
                            pe.sem_inc(S["zc_ready"], -1)
                            turn()
                        pe.wait_ge(S["h_in"], MT)
                        pe.sem_inc(S["h_in"], -MT)
                        down()
                        if more:
                            turned()
                            up()
                    with pe.Fori(0, NG - 1) as _g:
                        step()
                    step(more=False)
                    pe.wait_ge(S["cls_loaded"], 48)
                    pe.wait_ge(S["zc_ready"], 1)
                    pe.sem_inc(S["zc_ready"], -1)
                    zc3 = zc[:].rearrange("p (b c i) -> p c i b", c=2, i=NCLS)
                    for i in range(NCLS):
                        for c in range(2):
                            last = pe.matmul(ps[0][0:B, 2 * i:2 * i + 2], zc3[0:DH, c, i], gates_w[:, 2 * NCLS * c + 2 * i:2 * NCLS * c + 2 * i + 2],
                                             start=(c == 0), stop=(c == 1))
                    last.then_inc(S["gates_ps"], 1)

                    def cls_up(n):
                        a = CLS_PAIRS[n // 2][n % 2][0]
                        for m in range(MT):
                            for c in range(2):
                                k = DH + c
                                w = 2 * F * a + c * F + m * P
                                last = pe.matmul(ps[4 + n % 2][:, B * m:B * m + B], self.w1[0:k, w:w + P], zc3[0:k, c, n // 2],
                                                 start=(c == 0), stop=(c == 1))
                        last.then_inc(S["u_ps"], 1)

                    def cls_down(n):
                        c = CLS_PAIRS[n // 2][n % 2][1]
                        pe.wait_ge(S["u_in"], 1)
                        pe.sem_inc(S["u_in"], -1)
                        if n >= 2:
                            pe.wait_ge(S["e_free"], 1)
                            pe.sem_inc(S["e_free"], -1)
                        for m in range(MT):
                            last = pe.matmul(ps[6 + n % 2][0:B, 0:D], hcT[n % 2][:, B * m:B * m + B],
                                             a2[:, MT * D * c + D * m:MT * D * c + D * m + D], start=(m == 0), stop=(m == MT - 1))
                        last.then_inc(S["e_ps"], 1)
                    cls_up(0)
                    for n in range(2 * NCLS):
                        if n + 1 < 2 * NCLS:
                            cls_up(n + 1)
                        cls_down(n)



def _halves(w, bias=None):
    import numpy as np
    n = w.shape[1]
    o = np.zeros((DH + 1, 2, n), np.float32)
    o[:DH, 0], o[:DH, 1] = w[:DH], w[DH:]
    if bias is not None:
        o[DH, 1] = bias
    return o


def _relation_tables(tv, th):
    import numpy as np
    o = np.zeros((NG0, 64, tv.shape[1]), np.float32)
    for g in range(NGV):
        o[g, PLACE0] = tv[0]
        for c in range(VC):
            for r in range(NV):
                o[g, NV * c + r] = tv[r - (VC * g + c) + 15]
    for g in range(NGH):
        o[NGV + g, PLACE0] = th[0]
        for c in range(min(HC, SIDE - HC * g)):
            for r in range(SIDE):
                o[NGV + g, VC * NV + SIDE * c + r] = th[r - (HC * g + c) + 15]
    o[NGV + NGH, 0:NV] = o[NGV + NGH, PLACE0] = tv[0]
    o[NGV + NGH + 1, VC * NV:VC * NV + SIDE] = o[NGV + NGH + 1, PLACE0] = th[0]
    return o


def _constants():
    import numpy as np
    o = np.zeros((P, NCONST), np.float32)

    def put(name, a):
        at, w = CONSTS[name]
        o[:a.shape[0], at:at + w] = a
    put("ident", np.eye(P))
    put("anti", np.eye(P)[::-1])
    put("tri", np.triu(np.ones((P, P)), 1))
    put("ones", np.ones((P, P)))
    j = np.arange(1, P)
    row, col = (j - 1) // SIDE, (j - 1) % SIDE
    place, active = np.zeros((64, P)), np.zeros((64, P))
    for c in range(VC):
        place[NV * c + row, j] = 1
        active[NV * c:NV * c + NV, 1:] = row % VC == c
    for c in range(HC):
        at = VC * NV + SIDE * c
        place[at + col, j] = 1
        active[at:at + SIDE, 1:] = col % HC == c
    active[0:NV, 0] = active[VC * NV:VC * NV + SIDE, 0] = 1
    place[PLACE0, 0] = 1
    active[PLACE0] = 1
    put("ohk", np.concatenate([np.zeros((64, P)), place]))
    put("ohv", place.T)
    put("active", np.concatenate([active, active]))
    put("iota8", np.tile(np.arange(8.0), (P, 1)))
    put("ebase", np.tile(np.arange(8.0) * CAP, (P, 1)))
    put("step128", np.tile(P * np.arange(float(TILES)), (P, 1)))
    put("neg_half", np.full((P, 1), -0.5))
    put("eps12", np.full((P, 1), 1e-12))
    put("eps5", np.full((P, 1), 1e-5))
    return o


def _layout(x):
    import numpy as np
    x = {k: np.asarray(a) for k, a in x.items()}
    wqkv = np.stack([_halves(x["L0_attn_" + n])[:DH] for n in ("wq", "wk", "wv")], 1)
    rk = _relation_tables(x["L0_attn_rk_v"], x["L0_attn_rk_h"])
    rv = _relation_tables(x["L0_attn_rv_v"], x["L0_attn_rv_h"])
    relk = np.zeros((2, HD0, NG0, 2, 64), np.float32)
    relv = np.zeros((2, 64, NG0, 2, HD0), np.float32)
    for e in range(2):
        relk[e, :, :, e] = rk.transpose(2, 0, 1)
        relv[e, :, :, e] = rv.transpose(1, 0, 2)
    rows = np.zeros(NROW, np.float32)
    for name, a in (("type", x["L0_tok_type_emb"][0]), ("gamma", x["L0_tok_ln_gamma"]), ("beta", x["L0_tok_ln_beta"]),
                    ("gatew", x["L0_tok_gate_w"][0]), ("gateb", x["L0_tok_gate_b"]), ("bproj", x["L0_attn_bproj"]),
                    ("subln", np.tile(x["L1_attn_subln_w"], H1)),
                    ("moe0_b2", x["L1_ffn_moe0_b2"]), ("a2_b", x["L1_ffn_A2_b"].ravel()),
                    ("lam", np.concatenate([x["L1_attn_lambda_" + n] for n in ("q1", "k1", "q2", "k2")]))):
        at, w = ROWS[name]
        rows[at:at + w] = a
    wr = np.concatenate([x["L0_ffn_gate_w"], x["L0_ffn_v_w"][:, None]], 1)
    br = np.concatenate([x["L0_ffn_gate_b"], x["L0_ffn_v_b"].reshape(1)])
    def alone(w):
        n = w.shape[0]
        o, w = np.zeros((n, MT, 4, QUAD, HS), np.float32), w.reshape(n, 6, QUAD, HS)
        for j in range(QUAD):
            o[:, j, :, j] = w[:, 0:4, j]
            o[:, QUAD + j // 2, 2 * (j % 2):2 * (j % 2) + 2, j] = w[:, 4:6, j]
        return o.reshape(n, -1)

    def twice(w):
        return np.concatenate([w, w[:, P:]], 1)

    def proj1(n, cols=lambda w: w):
        return _halves(cols(x["L1_attn_W" + n]), cols(x["L1_attn_b" + n][None])[0])

    def down(w):
        return w.reshape(MT, P, D).transpose(1, 0, 2)

    ones = np.ones((8, D), np.float32)
    return {
        "mixrows": np.concatenate([x["L0_ffn_b2"], x["L0_ffn_out_w"], x["L0_ffn_out_b"][None]], 0),
        "mixscale": np.concatenate([ones] + [x["L0_ffn_bk_scale"][None]] * 3, 0),
        "moe_w2": np.stack([down(w) for w in x["L0_ffn_w2"]], 1).reshape(P, -1),
        "wq1": proj1("q", alone).reshape(DH + 1, -1), "wk1": proj1("k", twice).reshape(DH + 1, -1),
        "wvo1": np.stack([proj1("v"), proj1("o")], 1).reshape(DH + 1, -1),
        "moe0_w1": _halves(x["L1_ffn_moe0_W1"], x["L1_ffn_moe0_b1"]).reshape(DH + 1, -1),
        "moe0_w2": down(x["L1_ffn_moe0_W2"]).reshape(P, -1),
        "a1": np.stack([_halves(x["L1_ffn_A1_W"][e], x["L1_ffn_A1_b"][e]) for e in range(5)], 1).reshape(DH + 1, -1),
        "a2": np.stack([down(w) for w in x["L1_ffn_A2_W"]], 1).reshape(P, -1),
        "gates_w": _halves(x["L1_ffn_G_W"].transpose(1, 0, 2).reshape(D, -1))[:DH].reshape(DH, -1),
        "x": x["x"], "itok": x["itok_BS_2_399970"], "word_emb": x["L0_tok_word_emb"], "wvec": x["L0_tok_wvec"],
        "consts": _constants(), "rows": rows, "pos": x["L0_tok_pos_emb"],
        "g2b": np.concatenate([x["L0_tok_g2b_w"].T, x["L0_tok_g2b_b"][None]], 0),
        "wqkv": wqkv.reshape(DH, -1),
        "relk": relk.reshape(P, -1), "relv": relv.reshape(P, -1),
        "wproj": x["L0_attn_wproj"].reshape(MT, P, D).transpose(1, 0, 2).reshape(P, -1),
        "wroute": _halves(wr, br).reshape(DH + 1, -1),
        "moe_w1": np.stack([_halves(x["L0_ffn_w1"][e], x["L0_ffn_b1"][e]) for e in range(E)], 1).reshape(DH + 1, -1),
    }


def kernel(**inputs):
    import numpy as _np
    import concourse.bacc as _bacc
    from concourse import mybir as _mybir
    from concourse.bass_utils import run_bass_kernel_spmd as _run

    nc = _bacc.Bacc("TRN2", target_bir_lowering=False, num_devices=1)
    arrays, args = {}, {}
    for name, a in _layout(inputs).items():
        a = _np.ascontiguousarray(a)
        arrays[f"in_{name}"] = a
        args[name] = nc.dram_tensor(f"in_{name}", a.shape, _mybir.dt.from_np(a.dtype), kind="ExternalInput").ap()
    out = nc.dram_tensor("out_0", (B, P, D), F32, kind="ExternalOutput").ap()
    Tower(nc, args, out).build()
    r = _run(nc, [arrays], core_ids=[0])
    return r.results[0]["out_0"]
```
